# Optimizing a Trainium2 kernel written in Bass

```python
import numpy as np
import jax
import jax.numpy as jnp

def _softmax(x, axis=-1):
    return jax.nn.softmax(x, axis=axis)

def _gelu(x):
    return jax.nn.gelu(x, approximate=True)

def _silu(x):
    return jax.nn.silu(x)

def _sigmoid(x):
    return jax.nn.sigmoid(x)

def _layernorm(x, axis=-1, eps=1e-05):
    m = jnp.mean(x, axis=axis, keepdims=True)
    v = jnp.var(x, axis=axis, keepdims=True)
    return (x - m) / jnp.sqrt(v + eps)

def _scatter_add(tgt, idx, src, axis=0):
    return tgt.at[idx].add(src)

def _segment_sum(src, seg, n):
    return jax.ops.segment_sum(src, seg, n)
kernel_name = 'mk_vit_tower_d2_tok_img256_r4_53e82c'

def setup_inputs(seed: int=0):
    np.random.seed(seed)
    _w = jnp.asarray

    def _rec_inputs():
        import jax
        import jax.numpy as jnp
        _rk = jax.random.key(seed)
        x = -7.10856e-05 + 0.999911 * jax.random.normal(jax.random.fold_in(_rk, 1), (16, 64, 64, 64), jnp.float32)
        return x
    x = _rec_inputs()

    def _L0_tok_setup():
        import jax, jax.numpy as jnp
        import numpy as np
        GS = 8
        NH = 8
        DM = 64
        B, W, H = (4, 64, 64)
        key = jax.random.key(seed)
        ks = jax.random.split(key, 5)
        s = 0.02
        return {'x': jax.random.normal(ks[0], (B, DM, W, H), dtype=jnp.float32), 'Wq': jax.random.normal(ks[1], (DM, DM), dtype=jnp.float32) * s, 'bq': jnp.zeros((DM,), dtype=jnp.float32), 'Wk': jax.random.normal(ks[2], (DM, DM), dtype=jnp.float32) * s, 'bk': jnp.zeros((DM,), dtype=jnp.float32), 'Wv': jax.random.normal(ks[3], (DM, DM), dtype=jnp.float32) * s, 'bv': jnp.zeros((DM,), dtype=jnp.float32), 'Wo': jax.random.normal(ks[4], (DM, DM), dtype=jnp.float32) * s, 'bo': jnp.zeros((DM,), dtype=jnp.float32)}
    _L0_tok_all = _L0_tok_setup()
    _L0_tok_in = {k: v for k, v in _L0_tok_all.items() if k in ('Wq', 'bq', 'Wk', 'bk', 'Wv', 'bv', 'Wo', 'bo')}
    del _L0_tok_all

    def _L0_attn_setup():
        import jax, jax.numpy as jnp
        import numpy as np
        SEQ_LEN = 512
        EMBED_DIM = 64
        BATCH = 8
        LN_EPS = 1e-05

        def _layernorm(x, g, b):
            mu = jnp.mean(x, axis=-1, keepdims=True)
            var = jnp.mean(jnp.square(x - mu), axis=-1, keepdims=True)
            return (x - mu) * jax.lax.rsqrt(var + LN_EPS) * g + b
        key = jax.random.key(seed)
        ks = jax.random.split(key, 8)
        C = EMBED_DIM
        x = jax.random.normal(ks[0], (BATCH, SEQ_LEN, C), dtype=jnp.float32)
        qkv_w = jax.random.normal(ks[1], (C, 3 * C), dtype=jnp.float32) * 0.02
        qkv_b = jnp.zeros((3 * C,), dtype=jnp.float32)
        proj_w = jax.random.normal(ks[2], (C, C), dtype=jnp.float32) * 0.02
        proj_b = jnp.zeros((C,), dtype=jnp.float32)
        ln1_g = jnp.ones((C,), dtype=jnp.float32)
        ln1_b = jnp.zeros((C,), dtype=jnp.float32)
        ln2_g = jnp.ones((C,), dtype=jnp.float32)
        ln2_b = jnp.zeros((C,), dtype=jnp.float32)
        bias_table = jax.random.truncated_normal(ks[3], -2.0, 2.0, (2 * SEQ_LEN - 1,), dtype=jnp.float32) * 0.02
        scale = jnp.asarray(1.0 / np.sqrt(C), dtype=jnp.float32)
        return {'x': x, 'ln1_g': ln1_g, 'ln1_b': ln1_b, 'qkv_w': qkv_w, 'qkv_b': qkv_b, 'bias_table': bias_table, 'scale': scale, 'proj_w': proj_w, 'proj_b': proj_b, 'ln2_g': ln2_g, 'ln2_b': ln2_b}
    _L0_attn_all = _L0_attn_setup()
    _L0_attn_in = {k: v for k, v in _L0_attn_all.items() if k in ('ln1_g', 'ln1_b', 'qkv_w', 'qkv_b', 'bias_table', 'scale', 'proj_w', 'proj_b', 'ln2_g', 'ln2_b')}
    del _L0_attn_all

    def _L0_ffn_setup():
        import jax, jax.numpy as jnp
        import numpy as np
        DIM = 64
        HEADS = 8
        NUM_KEYS = 64
        NUM_KV = NUM_KEYS ** 2
        PK_TOPK = 16
        FINAL_TOPK = 16
        DIM_KEY = DIM // 2
        P = 2

        def _pk(x, Wq_pk, pk_keys):
            b, n, _ = x.shape
            q = (x @ Wq_pk).reshape(b, n, P, HEADS, DIM_KEY).transpose(2, 0, 1, 3, 4)
            sim = jnp.einsum('pbnhd,pkhd->pbnhk', q, pk_keys)
            scores, idx = jax.lax.top_k(sim, PK_TOPK)
            idx0 = idx[0]
            idx1 = idx[1] * NUM_KEYS
            index = (idx0[..., :, None] + idx1[..., None, :]).reshape(b, n, HEADS, PK_TOPK * PK_TOPK)
            score = (scores[0][..., :, None] + scores[1][..., None, :]).reshape(b, n, HEADS, PK_TOPK * PK_TOPK)
            final_scores, pk_idx = jax.lax.top_k(score, FINAL_TOPK)
            final_indices = jnp.take_along_axis(index, pk_idx, axis=-1)
            final_scores = jax.nn.softmax(final_scores, axis=-1)
            return (final_scores, final_indices)
        key = jax.random.key(seed)
        ks = jax.random.split(key, 7)
        b, n = (2, 256)
        std = 0.02
        x = jax.random.normal(ks[0], (b, n, DIM), dtype=jnp.float32)
        Wq_pk = jax.random.normal(ks[1], (DIM, P * HEADS * DIM_KEY), dtype=jnp.float32) * std
        pk_keys = jax.random.normal(ks[2], (P, NUM_KEYS, HEADS, DIM_KEY), dtype=jnp.float32) * std
        Wq = jax.random.normal(ks[3], (DIM, HEADS * DIM), dtype=jnp.float32) * std
        keys_table = jax.random.normal(ks[4], (NUM_KV * HEADS, DIM), dtype=jnp.float32) * std
        values_table = jax.random.normal(ks[5], (NUM_KV * HEADS, DIM), dtype=jnp.float32) * std
        Wo = jax.random.normal(ks[6], (DIM * HEADS, DIM), dtype=jnp.float32) * std
        return {'x': x, 'Wq_pk': Wq_pk, 'pk_keys': pk_keys, 'Wq': Wq, 'keys_table': keys_table, 'values_table': values_table, 'Wo': Wo}
    _L0_ffn_all = _L0_ffn_setup()
    _L0_ffn_in = {k: v for k, v in _L0_ffn_all.items() if k in ('Wq_pk', 'pk_keys', 'Wq', 'keys_table', 'values_table', 'Wo')}
    del _L0_ffn_all

    def _L1_attn_setup():
        import jax, jax.numpy as jnp
        import numpy as np
        import math
        H = 8
        DH = 16
        DEPTH = 1
        LAMBDA_INIT = 0.8 - 0.6 * math.exp(-0.3 * DEPTH)
        LN_EPS = 1e-05
        key = jax.random.key(seed)
        ks = jax.random.split(key, 12)
        dim = 64
        inner = 2 * H * DH
        b, n = (2, 512)
        s = lambda fan_in: 1.0 / math.sqrt(fan_in)
        return {'x': jax.random.normal(ks[0], (b, n, dim), jnp.float32), 'Wq': jax.random.normal(ks[1], (dim, inner), jnp.float32) * s(dim), 'Wkv': jax.random.normal(ks[2], (dim, 2 * inner), jnp.float32) * s(dim), 'Wout': jax.random.normal(ks[3], (inner, dim), jnp.float32) * s(inner), 'bout': jnp.zeros((dim,), jnp.float32), 'Wg': jax.random.normal(ks[4], (dim, inner), jnp.float32) * s(dim), 'bg': jnp.ones((inner,), jnp.float32), 'lq1': jax.random.normal(ks[5], (DH,), jnp.float32) * 0.1, 'lk1': jax.random.normal(ks[6], (DH,), jnp.float32) * 0.1, 'lq2': jax.random.normal(ks[7], (DH,), jnp.float32) * 0.1, 'lk2': jax.random.normal(ks[8], (DH,), jnp.float32) * 0.1, 'ln_gamma': jnp.ones((2 * DH,), jnp.float32), 'ln_beta': jnp.zeros((2 * DH,), jnp.float32)}
    _L1_attn_all = _L1_attn_setup()
    _L1_attn_in = {k: v for k, v in _L1_attn_all.items() if k in ('Wq', 'Wkv', 'Wout', 'bout', 'Wg', 'bg', 'lq1', 'lk1', 'lq2', 'lk2', 'ln_gamma', 'ln_beta')}
    del _L1_attn_all

    def _L1_ffn_setup():
        import jax, jax.numpy as jnp
        import numpy as np
        B, S, D = (8, 1024, 64)
        H = 4 * D
        CAPACITY = 0.5
        key = jax.random.key(seed)
        ks = jax.random.split(key, 6)
        x = jax.random.normal(ks[0], (B, S, D), dtype=jnp.float32)
        attention_mask = jnp.zeros((B, 1, 1, S), dtype=jnp.float32)
        wr = jax.random.normal(ks[1], (D, 1), dtype=jnp.float32) * 0.02
        br = jnp.zeros((1,), dtype=jnp.float32)
        w1 = jax.random.normal(ks[2], (D, H), dtype=jnp.float32) * 0.02
        b1 = jnp.zeros((H,), dtype=jnp.float32)
        w2 = jax.random.normal(ks[3], (H, D), dtype=jnp.float32) * 0.02
        b2 = jnp.zeros((D,), dtype=jnp.float32)
        return {'x': x, 'attention_mask': attention_mask, 'wr': wr, 'br': br, 'w1': w1, 'b1': b1, 'w2': w2, 'b2': b2}
    _L1_ffn_all = _L1_ffn_setup()
    _L1_ffn_in = {k: v for k, v in _L1_ffn_all.items() if k in ('attention_mask', 'wr', 'br', 'w1', 'b1', 'w2', 'b2')}
    del _L1_ffn_all
    return {'x': x, 'L0_tok_Wq': _L0_tok_in['Wq'], 'L0_tok_bq': _L0_tok_in['bq'], 'L0_tok_Wk': _L0_tok_in['Wk'], 'L0_tok_bk': _L0_tok_in['bk'], 'L0_tok_Wv': _L0_tok_in['Wv'], 'L0_tok_bv': _L0_tok_in['bv'], 'L0_tok_Wo': _L0_tok_in['Wo'], 'L0_tok_bo': _L0_tok_in['bo'], 'L0_attn_ln1_g': _L0_attn_in['ln1_g'], 'L0_attn_ln1_b': _L0_attn_in['ln1_b'], 'L0_attn_qkv_w': _L0_attn_in['qkv_w'], 'L0_attn_qkv_b': _L0_attn_in['qkv_b'], 'L0_attn_bias_table': _L0_attn_in['bias_table'], 'L0_attn_scale': _L0_attn_in['scale'], 'L0_attn_proj_w': _L0_attn_in['proj_w'], 'L0_attn_proj_b': _L0_attn_in['proj_b'], 'L0_attn_ln2_g': _L0_attn_in['ln2_g'], 'L0_attn_ln2_b': _L0_attn_in['ln2_b'], 'L0_ffn_Wq_pk': _L0_ffn_in['Wq_pk'], 'L0_ffn_pk_keys': _L0_ffn_in['pk_keys'], 'L0_ffn_Wq': _L0_ffn_in['Wq'], 'L0_ffn_keys_table': _L0_ffn_in['keys_table'], 'L0_ffn_values_table': _L0_ffn_in['values_table'], 'L0_ffn_Wo': _L0_ffn_in['Wo'], 'L1_attn_Wq': _L1_attn_in['Wq'], 'L1_attn_Wkv': _L1_attn_in['Wkv'], 'L1_attn_Wout': _L1_attn_in['Wout'], 'L1_attn_bout': _L1_attn_in['bout'], 'L1_attn_Wg': _L1_attn_in['Wg'], 'L1_attn_bg': _L1_attn_in['bg'], 'L1_attn_lq1': _L1_attn_in['lq1'], 'L1_attn_lk1': _L1_attn_in['lk1'], 'L1_attn_lq2': _L1_attn_in['lq2'], 'L1_attn_lk2': _L1_attn_in['lk2'], 'L1_attn_ln_gamma': _L1_attn_in['ln_gamma'], 'L1_attn_ln_beta': _L1_attn_in['ln_beta'], 'L1_ffn_attention_mask': _L1_ffn_in['attention_mask'], 'L1_ffn_wr': _L1_ffn_in['wr'], 'L1_ffn_br': _L1_ffn_in['br'], 'L1_ffn_w1': _L1_ffn_in['w1'], 'L1_ffn_b1': _L1_ffn_in['b1'], 'L1_ffn_w2': _L1_ffn_in['w2'], 'L1_ffn_b2': _L1_ffn_in['b2']}

def reference(x, L0_tok_Wq, L0_tok_bq, L0_tok_Wk, L0_tok_bk, L0_tok_Wv, L0_tok_bv, L0_tok_Wo, L0_tok_bo, L0_attn_ln1_g, L0_attn_ln1_b, L0_attn_qkv_w, L0_attn_qkv_b, L0_attn_bias_table, L0_attn_scale, L0_attn_proj_w, L0_attn_proj_b, L0_attn_ln2_g, L0_attn_ln2_b, L0_ffn_Wq_pk, L0_ffn_pk_keys, L0_ffn_Wq, L0_ffn_keys_table, L0_ffn_values_table, L0_ffn_Wo, L1_attn_Wq, L1_attn_Wkv, L1_attn_Wout, L1_attn_bout, L1_attn_Wg, L1_attn_bg, L1_attn_lq1, L1_attn_lk1, L1_attn_lq2, L1_attn_lk2, L1_attn_ln_gamma, L1_attn_ln_beta, L1_ffn_attention_mask, L1_ffn_wr, L1_ffn_br, L1_ffn_w1, L1_ffn_b1, L1_ffn_w2, L1_ffn_b2):
    import jax
    import jax.numpy as jnp

    def _L0_tok_ref(x, Wq, bq, Wk, bk, Wv, bv, Wo, bo):
        import jax, jax.numpy as jnp
        import numpy as np
        GS = 8
        NH = 8
        DM = 64
        B, W, H = (4, 64, 64)
        b, d, w, h = x.shape
        gw, gh = (w // GS, h // GS)
        n = gw * gh
        L = GS * GS
        dh = d // NH
        q = x.reshape(b, d, gw, GS, gh, GS).mean(axis=(3, 5))
        q = q.reshape(b, d, n).transpose(0, 2, 1).reshape(b * n, 1, d)
        kv = x.transpose(0, 2, 3, 1)
        kv = kv.reshape(b, gw, GS, gh, GS, d)
        kv = kv.transpose(0, 1, 3, 2, 4, 5).reshape(b * n, L, d)
        qp = (q @ Wq.T + bq).reshape(b * n, 1, NH, dh).transpose(0, 2, 1, 3)
        kp = (kv @ Wk.T + bk).reshape(b * n, L, NH, dh).transpose(0, 2, 1, 3)
        vp = (kv @ Wv.T + bv).reshape(b * n, L, NH, dh).transpose(0, 2, 1, 3)
        scores = jnp.einsum('bhqd,bhkd->bhqk', qp, kp) / jnp.sqrt(jnp.float32(dh))
        attn = jax.nn.softmax(scores, axis=-1)
        ctx = jnp.einsum('bhqk,bhkd->bhqd', attn, vp)
        ctx = ctx.transpose(0, 2, 1, 3).reshape(b * n, 1, d)
        attn_out = ctx @ Wo.T + bo
        out = q + attn_out
        return out.reshape(b, n, d)

    def _L0_attn_ref(x, ln1_g, ln1_b, qkv_w, qkv_b, bias_table, scale, proj_w, proj_b, ln2_g, ln2_b):
        import jax, jax.numpy as jnp
        import numpy as np
        SEQ_LEN = 512
        EMBED_DIM = 64
        BATCH = 8
        LN_EPS = 1e-05

        def _layernorm(x, g, b):
            mu = jnp.mean(x, axis=-1, keepdims=True)
            var = jnp.mean(jnp.square(x - mu), axis=-1, keepdims=True)
            return (x - mu) * jax.lax.rsqrt(var + LN_EPS) * g + b
        B, N, C = x.shape
        h = _layernorm(x, ln1_g, ln1_b)
        qkv = h @ qkv_w + qkv_b
        q, k, v = jnp.split(qkv, 3, axis=-1)
        coords = jnp.arange(N)
        rel_idx = coords[None, :] - coords[:, None] + (N - 1)
        rel_bias = bias_table[rel_idx]
        attn = jnp.einsum('bnc,bmc->bnm', q, k) + rel_bias
        attn = jax.nn.softmax(attn, axis=-1) * scale
        out = jnp.einsum('bnm,bmc->bnc', attn, v)
        out = out @ proj_w + proj_b
        out = _layernorm(out, ln2_g, ln2_b)
        return out

    def _L0_ffn_ref(x, Wq_pk, pk_keys, Wq, keys_table, values_table, Wo):
        import jax, jax.numpy as jnp
        import numpy as np
        DIM = 64
        HEADS = 8
        NUM_KEYS = 64
        NUM_KV = NUM_KEYS ** 2
        PK_TOPK = 16
        FINAL_TOPK = 16
        DIM_KEY = DIM // 2
        P = 2

        def _pk(x, Wq_pk, pk_keys):
            b, n, _ = x.shape
            q = (x @ Wq_pk).reshape(b, n, P, HEADS, DIM_KEY).transpose(2, 0, 1, 3, 4)
            sim = jnp.einsum('pbnhd,pkhd->pbnhk', q, pk_keys)
            scores, idx = jax.lax.top_k(sim, PK_TOPK)
            idx0 = idx[0]
            idx1 = idx[1] * NUM_KEYS
            index = (idx0[..., :, None] + idx1[..., None, :]).reshape(b, n, HEADS, PK_TOPK * PK_TOPK)
            score = (scores[0][..., :, None] + scores[1][..., None, :]).reshape(b, n, HEADS, PK_TOPK * PK_TOPK)
            final_scores, pk_idx = jax.lax.top_k(score, FINAL_TOPK)
            final_indices = jnp.take_along_axis(index, pk_idx, axis=-1)
            final_scores = jax.nn.softmax(final_scores, axis=-1)
            return (final_scores, final_indices)
        b, n, d = x.shape
        q = (x @ Wq).reshape(b, n, HEADS, DIM) * DIM ** (-0.5)
        kv_scores, indices = _pk(x, Wq_pk, pk_keys)
        offsets = jnp.arange(HEADS, dtype=indices.dtype) * NUM_KV
        ind = indices + offsets[None, None, :, None]
        k = jnp.einsum('bnhk,bnhkd->bnhd', kv_scores, keys_table[ind])
        v = jnp.einsum('bnhk,bnhkd->bnhd', kv_scores, values_table[ind])
        sim = jnp.einsum('bihd,bjhd->bhij', q, k)
        neg = -jnp.finfo(sim.dtype).max
        causal = jnp.tril(jnp.ones((n, n), dtype=bool))
        sim = jnp.where(causal, sim, neg)
        attn = jax.nn.softmax(sim, axis=-1)
        out = jnp.einsum('bhij,bjhd->bhid', attn, v)
        out = out.transpose(0, 2, 1, 3).reshape(b, n, HEADS * DIM)
        return out @ Wo

    def _L1_attn_ref(x, Wq, Wkv, Wout, bout, Wg, bg, lq1, lk1, lq2, lk2, ln_gamma, ln_beta):
        import jax, jax.numpy as jnp
        import numpy as np
        import math
        H = 8
        DH = 16
        DEPTH = 1
        LAMBDA_INIT = 0.8 - 0.6 * math.exp(-0.3 * DEPTH)
        LN_EPS = 1e-05
        b, n, dim = x.shape
        scale = DH ** (-0.5)
        q = x @ Wq
        kv = x @ Wkv
        k, v = jnp.split(kv, 2, axis=-1)
        q = q.reshape(b, n, 2 * H, DH).transpose(0, 2, 1, 3) * scale
        k = k.reshape(b, n, 2 * H, DH).transpose(0, 2, 1, 3)
        v = v.reshape(b, n, H, 2 * DH).transpose(0, 2, 1, 3)
        dots = jnp.einsum('bhid,bhjd->bhij', q, k)
        attn = jax.nn.softmax(dots, axis=-1)
        lam1 = jnp.exp(jnp.sum(lq1 * lk1))
        lam2 = jnp.exp(jnp.sum(lq2 * lk2))
        lam = lam1 - lam2 + LAMBDA_INIT
        attn = attn.reshape(b, H, 2, n, n)
        attn = attn[:, :, 0] - lam * attn[:, :, 1]
        out = jnp.einsum('bhij,bhjd->bhid', attn, v)
        mu = jnp.mean(out, axis=-1, keepdims=True)
        var = jnp.var(out, axis=-1, keepdims=True)
        out = (out - mu) * jax.lax.rsqrt(var + LN_EPS) * ln_gamma + ln_beta
        out = out * (1.0 - LAMBDA_INIT)
        out = out.transpose(0, 2, 1, 3).reshape(b, n, H * 2 * DH)
        gates = x @ Wg + bg
        out = out * jax.nn.sigmoid(gates)
        return out @ Wout + bout

    def _L1_ffn_ref(x, attention_mask, wr, br, w1, b1, w2, b2):
        import jax, jax.numpy as jnp
        import numpy as np
        B, S, D = (8, 1024, 64)
        H = 4 * D
        CAPACITY = 0.5
        b, s, d = x.shape
        weights = (jnp.einsum('bsd,do->bso', x, wr) + br)[..., 0]
        k = max(1, int(CAPACITY * s))
        kk = k - 1 if k > 1 else 1
        _, idx = jax.lax.top_k(weights, k)
        sel_idx = idx[:, :kk]
        sel = jnp.take_along_axis(x, sel_idx[:, :, None], axis=1)
        h = jax.nn.gelu(jnp.einsum('bkd,dh->bkh', sel, w1) + b1)
        y = jnp.einsum('bkh,hd->bkd', h, w2) + b2
        w_sel = jnp.take_along_axis(weights, sel_idx, axis=1)
        y = y * w_sel[..., None]
        batch_idx = jnp.arange(b)[:, None]
        processed = jnp.zeros_like(x).at[batch_idx, sel_idx].set(y)
        return processed + x
    h = _L0_tok_ref(x, L0_tok_Wq, L0_tok_bq, L0_tok_Wk, L0_tok_bk, L0_tok_Wv, L0_tok_bv, L0_tok_Wo, L0_tok_bo)
    h = h + _L0_attn_ref(_layernorm(h, axis=-1), L0_attn_ln1_g, L0_attn_ln1_b, L0_attn_qkv_w, L0_attn_qkv_b, L0_attn_bias_table, L0_attn_scale, L0_attn_proj_w, L0_attn_proj_b, L0_attn_ln2_g, L0_attn_ln2_b)
    h = h + _L0_ffn_ref(_layernorm(h, axis=-1), L0_ffn_Wq_pk, L0_ffn_pk_keys, L0_ffn_Wq, L0_ffn_keys_table, L0_ffn_values_table, L0_ffn_Wo)
    h = h + _L1_attn_ref(_layernorm(h, axis=-1), L1_attn_Wq, L1_attn_Wkv, L1_attn_Wout, L1_attn_bout, L1_attn_Wg, L1_attn_bg, L1_attn_lq1, L1_attn_lk1, L1_attn_lq2, L1_attn_lk2, L1_attn_ln_gamma, L1_attn_ln_beta)
    h = h + _L1_ffn_ref(_layernorm(h, axis=-1), L1_ffn_attention_mask, L1_ffn_wr, L1_ffn_br, L1_ffn_w1, L1_ffn_b1, L1_ffn_w2, L1_ffn_b2)
    return h

_drawn_inputs = setup_inputs


def setup_inputs(seed=0):
    import zlib

    import numpy as np

    out = dict(_drawn_inputs(seed))
    spreads = {'L0_tok_bq': (0.0, 0.8),
     'L0_tok_bk': (0.0, 2.0),
     'L0_tok_bv': (0.0, 0.532),
     'L0_tok_bo': (0.0, 0.1),
     'L0_attn_ln1_g': (1.0, 0.6),
     'L0_attn_ln1_b': (0.0, 0.8),
     'L0_attn_qkv_b': (0.0, 0.419),
     'L0_attn_proj_b': (0.0, 0.1),
     'L0_attn_ln2_g': (1.0, 0.2),
     'L0_attn_ln2_b': (0.0, 0.1),
     'L1_attn_bout': (0.0, 0.1),
     'L1_attn_bg': (1.0, 0.6),
     'L1_attn_ln_gamma': (1.0, 0.2),
     'L1_attn_ln_beta': (0.0, 0.1),
     'L1_ffn_b1': (0.0, 0.8),
     'L1_ffn_b2': (0.0, 0.634)}
    factors = {'L0_tok_Wq': 8.0,
     'L0_tok_Wk': 8.0,
     'L0_tok_Wv': 8.0,
     'L0_tok_Wo': 3.515,
     'L0_attn_bias_table': 64.0,
     'L0_ffn_Wq_pk': 8.0,
     'L0_ffn_pk_keys': 8.0,
     'L0_ffn_Wq': 64.0,
     'L0_ffn_keys_table': 64.0,
     'L0_ffn_values_table': 8.0,
     'L0_ffn_Wo': 8.0,
     'L1_attn_Wq': 8.0,
     'L1_attn_lq1': 8.0,
     'L1_attn_lk1': 8.0,
     'L1_attn_lq2': 8.0,
     'L1_attn_lk2': 8.0,
     'L1_ffn_wr': 5.443,
     'L1_ffn_w1': 8.0,
     'L1_ffn_w2': 8.0}
    for name, (base, spread) in spreads.items():
        noise = np.random.default_rng([zlib.crc32(name.encode()), seed]).standard_normal(out[name].shape)
        drawn = base * np.exp(spread * noise) if base else spread * noise
        out[name] = jnp.asarray(drawn.astype(out[name].dtype))
    for name, factor in factors.items():
        out[name] = (out[name] * factor).astype(out[name].dtype)
    return out
```

```python
from contextlib import ExitStack

import concourse.bass as bass
from concourse import mybir

F32 = mybir.dt.float32
U32 = mybir.dt.uint32
I32 = mybir.dt.int32
ALU = mybir.AluOpType
ACT = mybir.ActivationFunctionType
AX = mybir.AxisListType

P = 128
C = 64
N = 64
GS = 8
GW = 8
NH = 8
TOPK = 16
NKEY = 64
NKV = NKEY * NKEY
H3 = 16
D3 = 32
HID = 256
KEEP = N // 2 - 1
EPS = 1e-5
NEG = -1e30
LOWEST = -3.0e38
LAMBDA_INIT = 0.8 - 0.6 * 2.718281828459045 ** (-0.3)
GELU_C = 2.0 * 0.7978845608028654
RUNS = [(0, 1, 16), (1, 1, 8), (2, 1, 5), (3, 1, 4), (4, 1, 3), (5, 3, 2), (8, 8, 1)]
NC = sum(na * nb for _, na, nb in RUNS)
CHUNKS = 8
TC = P // CHUNKS


class Steps:

    def __init__(self, eng, sem, n, p):
        self.eng, self.sem, self.n, self.base, self.k = eng, sem, n, p * n, 0

    def __call__(self, ins, apart=False):
        self.k += 1
        ins.then_inc(self.sem, 1)
        self.eng.wait_ge(self.sem, self.base + self.k)
        if apart:
            self.eng.nop(nofuse=True)

    def end(self):
        assert self.k == self.n, (self.k, self.n)


def vit_tower_kernel(nc, a, out):
    pairs = a["x"].shape[0] // 2
    with ExitStack() as ctx:
        def sb(name, shape, dt=F32):
            return ctx.enter_context(nc.sbuf_tensor(name, shape, dt))

        def sem(name):
            return ctx.enter_context(nc.semaphore(name))

        table = nc.dram_tensor("table", [NH * NKV, 2 * C], F32, kind="Internal").ap()

        ident = sb("ident", [P, P])
        ident2 = sb("ident2", [P, C])
        anti = sb("anti", [N, P])
        m8 = sb("m8", [P, 16])
        m16 = sb("m16", [P, 8])
        same01 = sb("same01", [P, P])
        before01 = sb("before01", [P, P])
        same_neg = sb("same_neg", [P, P])
        causal_neg = sb("causal_neg", [P, P])
        rel_bias = sb("rel_bias", [P, P])
        rel_rows = sb("rel_rows", [N, N])
        mask_l = sb("mask_l", [P, 1024])
        mask_r = sb("mask_r", [P, P])
        pos50_i = sb("pos50_i", [P, NC], I32)
        pos50 = sb("pos50", [P, NC])
        head_off_i = sb("head_off_i", [P, NH * TOPK], I32)
        head_off = sb("head_off", [P, NH * TOPK])
        eps = sb("eps", [P, 1])
        wq_bd = sb("wq_bd", [P, P])
        wk_bd = sb("wk_bd", [P, P])
        wv_bd = sb("wv_bd", [P, P])
        wo_bd = sb("wo_bd", [P, P])
        wqT = sb("wqT", [P, P])
        wvT = sb("wvT", [P, P])
        woT2 = sb("woT2", [P, C])
        bq2 = sb("bq2", [P, 1])
        bk2 = sb("bk2", [P, 1])
        bv2 = sb("bv2", [P, 1])
        bo_r = sb("bo_r", [P, C])
        ln1g = sb("ln1g", [P, C])
        ln1b = sb("ln1b", [P, C])
        ln2g = sb("ln2g", [P, C])
        ln2b = sb("ln2b", [P, C])
        w_qkv = sb("w_qkv", [C, 3 * C])
        b_qk = sb("b_qk", [C, 2])
        b_v = sb("b_v", [P, C])
        scale1 = sb("scale1", [P, 1])
        w_proj = sb("w_proj", [C, C])
        b_proj = sb("b_proj", [P, C])
        w_pk = sb("w_pk", [C, 512])
        keys_n = sb("keys_n", [NKEY, 2, 256])
        keys_bd = sb("keys_bd", [P, 4, 256])
        w_q2 = sb("w_q2", [C, 512])
        w_o2 = sb("w_o2", [P, 4, C])
        w_q3 = sb("w_q3", [C, 256])
        w_kv3 = sb("w_kv3", [C, 512])
        w_g3 = sb("w_g3", [C, 256])
        w_out3 = sb("w_out3", [P, 2, C])
        b_out3 = sb("b_out3", [P, C])
        b_g3 = sb("b_g3", [P, 256])
        lqk = sb("lqk", [P, 4, 16])
        lprod = sb("lprod", [P, 2, 16])
        lsum = sb("lsum", [P, 2])
        lexp = sb("lexp", [P, 2])
        neg_lam = sb("neg_lam", [P, 1])
        gam3 = sb("gam3", [P, D3])
        bet3 = sb("bet3", [P, D3])
        wr_bc = sb("wr_bc", [C, P])
        wr_c = sb("wr_c", [C, 1])
        br_c = sb("br_c", [P, 1])
        w1 = sb("w1", [C, HID])
        b1c = sb("b1c", [P, 2])
        w2 = sb("w2", [P, 2, C])
        b2r = sb("b2r", [P, C])

        x2 = sb("x2", [P, 4096])
        xT = x2[:, :].rearrange("p (g x) -> p g x", g=GW)
        xw = sb("xw", [P, 4096])
        qsum = sb("qsum", [P, N])
        qT = sb("qT", [P, N])
        q_bd = sb("q_bd", [P, P])
        qp = sb("qp", [P, N])
        q_exp = sb("q_exp", [P, 1024])
        qk = sb("qk", [P, 1024])
        max_a = sb("max_a", [P, 8])
        sum_a = sb("sum_a", [P, 8])
        prob_a = sb("prob_a", [P, 1024])
        probT_a = sb("probT_a", [P, 1024])
        y_a = prob_a
        z_a = q_exp
        ctx_a = sb("ctx_a", [P, N])
        ctx_bd = sb("ctx_bd", [P, P])
        h_f = sb("h_f", [P, C])
        stats_f = sb("stats_f", [P, 6])
        mv_f = sb("mv_f", [P, 2])
        std_f = sb("std_f", [P, 1])
        xn_f = sb("xn_f", [P, C])
        hh = sb("hh", [P, C])
        hhT = sb("hhT", [C, P])
        q1 = sb("q1", [C, P])
        k1 = sb("k1", [C, P])
        v1 = sb("v1", [P, C])
        s1 = sb("s1", [P, P])
        max1 = sb("max1", [P, 1])
        sum1 = sb("sum1", [P, 1])
        p1 = sb("p1", [P, P])
        p1T = sb("p1T", [P, P])
        o1T = sb("o1T", [C, P])
        o1 = sb("o1", [P, C])
        xcT = sb("xcT", [C, P])
        qc_stage = sb("qc_stage", [C, 1024])
        qpkT = q_exp[:, 0:512]
        sim = probT_a[:, :].rearrange("p (g k) -> p g k", k=NKEY)
        sim_b = qk[:, :].rearrange("p (g k) -> p g k", k=NKEY)
        top = sb("top", [P, 2, NH, TOPK])
        topi_u = sb("topi_u", [P, 2, NH, TOPK], U32)
        topi = sb("topi", [P, 2, NH, TOPK])
        cand, candi, cand_b = (t[:, lo:lo + NH * NC].rearrange("p (h c) -> p h c", c=NC)
                               for t, lo in ((q_exp, 512), (q_exp, 0), (qk, 0)))
        fin = sb("fin", [P, NH, TOPK])
        pos_u = sb("pos_u", [P, NH, TOPK], U32)
        pos = sb("pos", [P, NH, TOPK])
        hot = prob_a[:, 0:TOPK * NC].rearrange("p (j c) -> p j c", c=NC)
        fidx = sb("fidx", [P, NH * TOPK])
        fexp = sb("fexp", [P, NH, TOPK])
        fsum = sb("fsum", [P, NH])
        idx_stage = sb("idx_stage", [P, P], U32)
        wT_stage = sb("wT_stage", [P, P])
        idx_live = sb("idx_live", [P, P], U32)
        w_live = sb("w_live", [P, P, NH])
        qc_live = sb("qc_live", [C, 1024])
        h_b = sb("h_b", [P, C])
        gath = sb("gath", [P, P, 2 * C])
        kv = sb("kv", [P, P, NH])
        v2 = sb("v2", [P, NH, C])
        sp2 = sb("sp2", [P, 2048])
        s2, p2T = sp2[:, 0:1024], sp2[:, 1024:2048]
        max2 = sb("max2", [P, 8])
        sum2 = sb("sum2", [P, 8])
        o2T = sb("o2T", [P, 512])
        stats_b = sb("stats_b", [P, 6])
        mv_b = sb("mv_b", [P, 2])
        std_b = sb("std_b", [P, 8])
        xn_b = sb("xn_b", [P, C])
        xbT = sb("xbT", [C, P])
        q3T = sb("q3T", [P, 256])
        v3 = sb("v3", [P, 256])
        g3 = sb("g3", [P, 256])
        k_exp = sb("k_exp", [P, 2, NH, P])
        s3 = sp2[:, :].rearrange("p (h x) -> p h x", x=P)
        max3 = sb("max3", [P, H3])
        sum3 = sb("sum3", [P, H3])
        a3 = k_exp[:, 0]
        a3b = k_exp[:, 1]
        a3T = kv[:, :, :].rearrange("p t h -> p (t h)")
        o3 = sb("o3", [P, 8, D3])
        sq3 = sb("sq3", [P, 8, D3])
        mean3 = sb("mean3", [P, 8])
        o3T = v3
        z1 = q3T
        z1b = g3
        wrow = sb("wrow", [P, P])
        wcmp = sb("wcmp", [P, P])
        wcol = sb("wcol", [P, 1])
        rank2 = sb("rank2", [P, 2])
        factor = sb("factor", [P, 1])
        y_o = sb("y_o", [P, C])
        out_sb = sb("out_sb", [P, C])

        FB = [ctx.enter_context(nc.psum_tensor(f"front{n}", [P, 512], F32)) for n in range(4)]
        BB = [ctx.enter_context(nc.psum_tensor(f"back{n}", [P, 512], F32)) for n in range(4)]

        s_x = sem("x_loaded")
        s_w = sem("weights_loaded")
        s_zero = sem("zeros_set")
        s_table = sem("table_built")
        s_const = sem("constants_set")
        s_tw = sem("weights_turned")
        s_twc = sem("turned_weights_copied")
        s_lam = sem("lambda_sums")
        s_lame = sem("lambda_exps")
        s_setup = sem("setup_done")
        n_setup = sem("setup_steps")
        n_pool = sem("gpsimd_steps")
        n_front = sem("front_steps")
        s_fpsum = sem("front_banks_free")
        s_xw = sem("x_regrouped")
        s_xt = sem("x_turned")
        s_xtc = sem("x_turned_copied")
        s_mean = sem("window_means")
        s_qp = sem("pool_queries")
        s_qexp = sem("pool_queries_spread")
        s_qk = sem("pool_query_keys")
        s_qkc = sem("pool_query_keys_copied")
        s_qkb = sem("pool_key_bias")
        s_qkbc = sem("pool_key_bias_copied")
        s_sa = sem("pool_scores")
        s_ma = sem("pool_maxima")
        s_ea = sem("pool_exps")
        s_pa = sem("pool_probs")
        s_pta = sem("pool_probs_turned")
        s_ptac = sem("pool_probs_turned_copied")
        s_ya = sem("pool_sums")
        s_yac = sem("pool_sums_copied")
        s_za = sem("pool_values")
        s_ctx = sem("pool_context")
        s_tok = sem("tokens")
        s_varf = sem("front_variances")
        s_stdf = sem("front_deviations")
        s_hh = sem("attn_input")
        s_hht = sem("attn_input_turned")
        s_hhtc = sem("attn_input_turned_copied")
        s_qkv = sem("attn_qkv")
        s_qkvc = sem("attn_qkv_copied")
        s_s1 = sem("attn_scores")
        s_m1 = sem("attn_maxima")
        s_e1 = sem("attn_exps")
        s_p1 = sem("attn_probs")
        s_p1t = sem("attn_probs_turned")
        s_p1tc = sem("attn_probs_turned_copied")
        s_o1 = sem("attn_out")
        s_o1c = sem("attn_out_copied")
        s_pr = sem("attn_projected")
        s_xc = sem("memory_input")
        s_xct = sem("memory_input_turned")
        s_xctc = sem("memory_input_turned_copied")
        s_qc = sem("memory_queries")
        s_qcc = sem("memory_queries_copied")
        s_sim = sem("key_scores")
        s_simc = sem("key_scores_copied")
        s_fm = sem("picks_found")
        s_fe = sem("picks_exps")
        s_fw = sem("pick_weights")
        s_ft = sem("picks_turned")
        s_idx = sem("pick_indices")
        s_idxl = sem("indices_taken")
        s_g = [sem(f"rows_fetched{c}") for c in range(CHUNKS)]
        s_gu = sem("row_parts_free")
        s_wl = sem("pick_weights_spread")
        s_ql = sem("memory_queries_taken")
        n_back = sem("back_steps")
        s_kvc = sem("keys_values_copied")
        s_s2 = sem("memory_scores")
        s_vt = sem("memory_values_turned")
        s_vtc = sem("memory_values_turned_copied")
        s_m2 = sem("memory_maxima")
        s_e2 = sem("memory_exps")
        s_p2 = sem("memory_probs")
        s_p2t = sem("memory_probs_turned")
        s_p2tc = sem("memory_probs_turned_copied")
        s_o2 = sem("memory_out")
        s_o2c = sem("memory_out_copied")
        s_wo = sem("memory_projected")
        s_varb = sem("back_variances")
        s_stdb = sem("back_deviations")
        s_xb = sem("back_input")
        s_xbt = sem("back_input_turned")
        s_xbtc = sem("back_input_turned_copied")
        s_qkvg = sem("diff_projections")
        s_q3c = sem("diff_queries_copied")
        s_k3 = sem("diff_keys_spread")
        s_g3e = sem("diff_gates_in")
        s_g3x = sem("diff_gates_exps")
        s_s3 = sem("diff_scores")
        s_m3 = sem("diff_maxima")
        s_e3 = sem("diff_exps")
        s_a3 = sem("diff_probs")
        s_a3t = sem("diff_probs_turned")
        s_a3tc = sem("diff_probs_turned_copied")
        s_o3 = sem("diff_out")
        s_o3g = sem("diff_out_gated")
        s_o3t = sem("diff_out_turned")
        s_o3tc = sem("diff_out_turned_copied")
        s_pr3 = sem("diff_projected")
        s_ff1 = sem("hidden_and_router")
        s_ge = sem("gelu_arguments")
        s_gx = sem("gelu_exps")
        s_gl = sem("gelu_done")
        s_ff2 = sem("feedforward_out")
        s_out = sem("output_ready")
        s_st = sem("output_stored")

        def bc(ap, dims, at):
            for n, axis in zip(dims, at):
                ap = ap.unsqueeze(axis)
                shape = list(ap.shape)
                shape[axis] = n
                ap = ap.broadcast_to(shape)
            return ap

        def window_pair(gw, q):
            return xw[:, gw * 512 + q * P:gw * 512 + (q + 1) * P]

        def row(name, n=C, lo=0):
            return a[name][lo:lo + n].rearrange("(o c) -> o c", o=1).broadcast_to([P, n])

        def col(name, n, lo=0):
            return a[name][lo:lo + n].rearrange("(c o) -> c o", o=1)

        weight_loads = []
        for t, name in ((wq_bd, "L0_tok_Wq"), (wk_bd, "L0_tok_Wk"), (wv_bd, "L0_tok_Wv"), (wo_bd, "L0_tok_Wo")):
            weight_loads += [(t[C * b:C * b + C, C * b:C * b + C], a[name]) for b in range(2)]
        for t, name in ((bq2, "L0_tok_bq"), (bk2, "L0_tok_bk"), (bv2, "L0_tok_bv")):
            weight_loads += [(t[C * b:C * b + C, :], col(name, C)) for b in range(2)]
        for t, name in ((bo_r, "L0_tok_bo"), (ln1g, "L0_attn_ln1_g"), (ln1b, "L0_attn_ln1_b"),
                        (ln2g, "L0_attn_ln2_g"), (ln2b, "L0_attn_ln2_b"), (b_proj, "L0_attn_proj_b"),
                        (b_out3, "L1_attn_bout"), (b2r, "L1_ffn_b2")):
            weight_loads.append((t[:, :], row(name)))
        weight_loads += [
            (w_qkv[:, :], a["L0_attn_qkv_w"]),
            (b_qk[:, 0:1], col("L0_attn_qkv_b", C)), (b_qk[:, 1:2], col("L0_attn_qkv_b", C, C)),
            (b_v[:, :], row("L0_attn_qkv_b", C, 2 * C)),
            (scale1[:, :], row("L0_attn_scale", 1)),
            (w_proj[:, :], a["L0_attn_proj_w"]),
            (rel_rows[:, :], bass.AP(a["L0_attn_bias_table"].tensor, 0, [[1, N], [1, N]])),
            (w_pk[:, :], a["L0_ffn_Wq_pk"]),
            (keys_n[:, :, :], a["L0_ffn_pk_keys"].rearrange("p k h d -> k p (h d)")),
            (w_q2[:, :], a["L0_ffn_Wq"]),
            (w_o2[:, :, :], a["L0_ffn_Wo"].rearrange("(c p) n -> p c n", p=P)),
            (w_q3[:, :], a["L1_attn_Wq"]), (w_kv3[:, :], a["L1_attn_Wkv"]), (w_g3[:, :], a["L1_attn_Wg"]),
            (w_out3[:, :, :], a["L1_attn_Wout"].rearrange("(c p) n -> p c n", p=P)),
            (b_g3[:, :], row("L1_attn_bg", 256)),
            (lqk[:, 0, :], row("L1_attn_lq1", 16)), (lqk[:, 1, :], row("L1_attn_lq2", 16)),
            (lqk[:, 2, :], row("L1_attn_lk1", 16)), (lqk[:, 3, :], row("L1_attn_lk2", 16)),
            (gam3[:, :], row("L1_attn_ln_gamma", D3)), (bet3[:, :], row("L1_attn_ln_beta", D3)),
            (wr_c[:, :], a["L1_ffn_wr"]), (br_c[:, :], row("L1_ffn_br", 1)),
            (w1[:, :], a["L1_ffn_w1"]),
            (b1c[:, 0:1], col("L1_ffn_b1", P)), (b1c[:, 1:2], col("L1_ffn_b1", P, P)),
            (w2[:, :, :], a["L1_ffn_w2"].rearrange("(c p) n -> p c n", p=P)),
        ]

        block = ctx.enter_context(nc.Block())

        @block.sync
        def _(eng):
            def load_x(p):
                eng.dma_start(x2[:, :], a["x"][bass.ds(p * 2, 2)].rearrange("b c w h -> (b c) (w h)"))\
                   .then_inc(s_x, 16)

            load_x(0)
            eng.wait_ge(s_w, 16 * len(weight_loads))
            for h in range(NH):
                rows = slice(h * NKV, (h + 1) * NKV)
                eng.dma_start(table[rows, 0:C], a["L0_ffn_keys_table"][rows, :]).then_inc(s_table, 16)
                eng.dma_start(table[rows, C:2 * C], a["L0_ffn_values_table"][rows, :]).then_inc(s_table, 16)
            with eng.Fori(1, pairs) as p:
                eng.wait_ge(s_ya, p)
                load_x(p)

        @block.gpsimd
        def _(eng):
            step = Steps(eng, n_pool, POOL_STEPS, 0)
            for t in (wq_bd, wk_bd, wv_bd, wo_bd):
                ins = eng.memset(t[:, :], 0.0)
            ins.then_inc(s_zero, 1)
            for t in (ident, m8, m16, mask_l, mask_r, anti):
                eng.memset(t[:, :], 0.0)
            for t in (q_bd, ctx_bd, keys_bd[:, :, :].rearrange("p a b -> p (a b)")):
                eng.memset(t[:, :], 0.0)
            eng.memset(eps[:, :], EPS)
            eng.memset(same01[:, :], 0.0)
            eng.memset(same_neg[:, :], NEG)
            eng.iota(pos50_i[:, :], pattern=[[1, NC]], base=0, channel_multiplier=0)
            step(eng.iota(head_off_i[:, :], pattern=[[NKV, NH], [0, TOPK]], base=0, channel_multiplier=0))
            for t, inside in ((same01, 1.0), (same_neg, 0.0)):
                eng.memset(t[0:N, 0:N], inside)
                ins = eng.memset(t[N:P, N:P], inside)
            step(ins)

            def mark(o, i, fill, base, pattern, keep=ALU.not_equal):
                return eng.affine_select(out=o, in_=i, compare_op=keep, fill=fill, base=base, pattern=pattern,
                                         channel_multiplier=1)

            mark(ident[:, :], ident[:, :], 1.0, 0, [[-1, P]])
            rev = anti[:, :].rearrange("p (b n) -> p b n", b=2)
            mark(rev, rev[0:N], 1.0, 1 - N, [[0, 2], [1, N]])
            mark(causal_neg[:, :], same_neg[:, :], NEG, 0, [[-1, P]], ALU.is_ge)
            mark(before01[:, :], same01[:, :], 0.0, 0, [[-1, P]], ALU.is_gt)
            ml = mask_l[:, :].rearrange("p (u g r) -> p u g r", g=2, r=16)
            mark(ml, ml, 1.0, -1, [[0, 32], [-1, 2], [0, 16]])
            mr = mask_r[:, :].rearrange("p (g x) -> p g x", g=2)
            step(mark(mr, mr, NEG, -2, [[1, 2], [0, N]]))
            step(eng.memset(mask_r[0:1, :], 1.0))
            for j in range(8):
                step(mark(m8[:, :], m8[:, :], 1.0, -j, [[-8, 16]]))
            for j in range(16):
                step(mark(m16[:, :], m16[:, :], 1.0, -j, [[-16, 8]]))
            step.end()
            eng.nop().then_inc(s_const, 1)

            eng.wait_ge(s_table, 16 * 2 * NH)
            with eng.Fori(0, pairs) as p:
                for c in range(CHUNKS):
                    eng.wait_ge(s_g[c], p * (16 * TC))
                eng.wait_ge(s_idx, p + 1)
                eng.nop(nofuse=True)
                eng.tensor_copy(idx_live[:, :], idx_stage[:, :]).then_inc(s_idxl, 1)
                eng.wait_ge(s_idxl, p + 1)
                for c in range(CHUNKS):
                    eng.wait_ge(s_gu, p * CHUNKS + c + 1)
                    eng.nop(nofuse=True)
                    for t in range(c * TC, (c + 1) * TC):
                        eng.indirect_dma_start(gath[:, t, :], None, table,
                                               bass.IndirectOffsetOnAxis(idx_live[:, t:t + 1], axis=0))\
                           .then_inc(s_g[c], 16)

        @block.tensor
        def _(eng):
            def front(p):
                eng.wait_ge(s_fpsum, p)
                for gw in range(GW):
                    eng.wait_ge(s_xw, p * GW + gw + 1)
                    if gw >= 2:
                        eng.wait_ge(s_xtc, p * GW + gw - 1)
                    for q in range(4):
                        ins = eng.transpose(FB[2 + gw % 2][:, q * P:(q + 1) * P], window_pair(gw, q), ident[:, :])
                    ins.then_inc(s_xt, 1)
                eng.wait_ge(s_mean, p + 1)
                eng.matmul(FB[0][:, 0:N], wqT[:, :], qT[:, :], start=True, stop=True).then_inc(s_qp, 1)
                eng.wait_ge(s_qexp, p + 1)
                for n in range(2):
                    ins = eng.matmul(FB[n][:, :], wk_bd[:, :], q_exp[:, n * 512:(n + 1) * 512], start=True, stop=True)
                ins.then_inc(s_qk, 1)
                eng.wait_ge(s_xtc, p * GW + GW)
                for n in range(2):
                    ins = eng.matmul(FB[2 + n][0:1, :], bk2[:, :], q_exp[:, n * 512:(n + 1) * 512], start=True, stop=True)
                ins.then_inc(s_qkb, 1)
                eng.wait_ge(s_qkc, 2 * p + 2)
                eng.wait_ge(s_qkbc, p + 1)
                for gw in range(GW):
                    o = FB[gw // 4][:, gw % 4 * P:(gw % 4 + 1) * P]
                    eng.matmul(o, mask_l[:, gw * P:(gw + 1) * P], mask_r[:, :], start=True, stop=False)
                    for q in range(4):
                        u = (gw * 4 + q) * 32
                        ins = eng.matmul(o[32 * q:32 * q + 32, :], qk[:, u:u + 32], window_pair(gw, q),
                                         start=False, stop=True)
                    if gw % 4 == 3:
                        ins.then_inc(s_sa, 1)
                eng.wait_ge(s_pa, p + 1)
                for gw in range(GW):
                    ins = eng.transpose(FB[gw // 4][:, gw % 4 * P:(gw % 4 + 1) * P], prob_a[:, gw * P:(gw + 1) * P],
                                        ident[:, :])
                ins.then_inc(s_pta, 1)
                eng.wait_ge(s_ptac, 2 * p + 2)
                for gw in range(GW):
                    for q in range(4):
                        u = (gw * 4 + q) * 32
                        ins = eng.matmul(FB[2 + u // 512][:, u % 512:u % 512 + 32], xT[:, gw, q * P:(q + 1) * P],
                                         probT_a[:, u:u + 32], start=True, stop=True)
                ins.then_inc(s_ya, 1)
                eng.wait_ge(s_yac, 2 * p + 2)
                for n in range(2):
                    ins = eng.matmul(FB[n][:, :], wvT[:, :], y_a[:, n * 512:(n + 1) * 512], start=True, stop=True)
                ins.then_inc(s_za, 1)
                eng.wait_ge(s_ctx, p + 1)
                eng.matmul(FB[2][:, 0:C], ctx_bd[:, :], woT2[:, :], start=True, stop=False)
                eng.matmul(FB[2][:, 0:C], q_bd[:, :], ident2[:, :], start=False, stop=True).then_inc(s_tok, 1)
                eng.wait_ge(s_hh, p + 1)
                eng.nop(nofuse=True)
                eng.transpose(FB[3][0:C, 0:P], hh[:, :], ident[:, :]).then_inc(s_hht, 1)
                eng.wait_ge(s_hhtc, p + 1)
                eng.nop(nofuse=True)
                eng.matmul(FB[0][0:C, 0:P], w_qkv[:, 0:C], hhT[:, :], start=True, stop=True)
                eng.matmul(FB[0][0:C, P:2 * P], w_qkv[:, C:2 * C], hhT[:, :], start=True, stop=True)
                eng.matmul(FB[0][:, 2 * P:2 * P + C], hhT[:, :], w_qkv[:, 2 * C:3 * C], start=True, stop=True)\
                   .then_inc(s_qkv, 1)
                eng.wait_ge(s_qkvc, p + 1)
                eng.matmul(FB[1][:, 0:P], q1[:, :], k1[:, :], start=True, stop=True).then_inc(s_s1, 1)
                eng.wait_ge(s_p1, p + 1)
                eng.transpose(FB[2][:, 0:P], p1[:, :], ident[:, :]).then_inc(s_p1t, 1)
                eng.wait_ge(s_p1tc, p + 1)
                eng.matmul(FB[3][0:C, 0:P], v1[:, :], p1T[:, :], start=True, stop=True).then_inc(s_o1, 1)
                eng.wait_ge(s_o1c, p + 1)
                eng.matmul(FB[0][:, 0:C], o1T[:, :], w_proj[:, :], start=True, stop=True).then_inc(s_pr, 1)
                eng.wait_ge(s_xc, p + 1)
                eng.nop(nofuse=True)
                eng.transpose(FB[1][0:C, 0:P], xn_f[:, :], ident[:, :]).then_inc(s_xct, 1)
                eng.wait_ge(s_xctc, p + 1)
                for m in range(4):
                    ins = eng.matmul(FB[0][:, m * P:(m + 1) * P], w_pk[:, m * P:(m + 1) * P], xcT[:, :],
                                     start=True, stop=True)
                ins.then_inc(s_qc, 1)
                for h in range(NH):
                    ins = eng.matmul(FB[2 + h // 4][0:C, h % 4 * P:(h % 4 + 1) * P], w_q2[:, h * C:(h + 1) * C],
                                     xcT[:, :], start=True, stop=True)
                ins.then_inc(s_qc, 1)
                eng.wait_ge(s_qcc, 3 * p + 1)
                for m in range(4):
                    ins = eng.matmul(FB[1 - m // 2][:, m % 2 * 256:(m % 2 + 1) * 256], qpkT[:, m * P:(m + 1) * P],
                                     keys_bd[:, m, :], start=True, stop=True)
                    if m % 2 == 1:
                        ins.then_inc(s_sim, 1)
                eng.wait_ge(s_qcc, 3 * p + 3)
                eng.wait_ge(s_fw, p + 1)
                eng.transpose(FB[2][:, 0:P], fidx[:, :], ident[:, :])
                eng.transpose(FB[3][:, 0:P], fexp[:, :, :].rearrange("p h j -> p (h j)"), ident[:, :])\
                   .then_inc(s_ft, 1)

            def back(p):
                eng.wait_ge(s_wl, p + 1)
                eng.wait_ge(s_ql, p + 1)
                for c in range(CHUNKS):
                    eng.wait_ge(s_g[c], (p + 1) * (16 * TC))
                    for t in range(c * TC, (c + 1) * TC):
                        ins = eng.matmul(BB[t // 64][:, t % 64 * 8:t % 64 * 8 + 8], gath[:, t, :], w_live[:, t, :],
                                         start=True, stop=True)
                    ins.then_inc(s_gu, 1)
                eng.wait_ge(s_kvc, 2 * p + 2)
                for h in range(NH):
                    ins = eng.matmul(BB[2 + h // 4][:, h % 4 * P:(h % 4 + 1) * P], qc_live[:, h * P:(h + 1) * P],
                                     kv[0:C, :, h], start=True, stop=True)
                ins.then_inc(s_s2, 1)
                for h in range(NH):
                    ins = eng.transpose(BB[h // 4][:, h % 4 * P:(h % 4 + 1) * P], kv[:, :, h], ident[:, :])
                ins.then_inc(s_vt, 1)
                eng.wait_ge(s_p2, p + 1)
                for h in range(NH):
                    ins = eng.transpose(BB[2 + h // 4][:, h % 4 * P:(h % 4 + 1) * P], s2[:, h * P:(h + 1) * P],
                                        ident[:, :])
                ins.then_inc(s_p2t, 1)
                eng.wait_ge(s_vtc, 2 * p + 2)
                eng.wait_ge(s_p2tc, 2 * p + 2)
                for h in range(NH):
                    lo = h % 2 * C
                    ins = eng.matmul(BB[0][lo:lo + C, h // 2 * P:(h // 2 + 1) * P], v2[:, h, :],
                                     p2T[:, h * P:(h + 1) * P], start=True, stop=True)
                ins.then_inc(s_o2, 1)
                eng.wait_ge(s_o2c, p + 1)
                for m in range(4):
                    ins = eng.matmul(BB[1][:, 0:C], o2T[:, m * P:(m + 1) * P], w_o2[:, m, :],
                                     start=(m == 0), stop=(m == 3))
                ins.then_inc(s_wo, 1)
                eng.wait_ge(s_xb, 2 * p + 1)
                eng.nop(nofuse=True)
                eng.transpose(BB[2][0:C, 0:P], xn_b[:, :], ident[:, :]).then_inc(s_xbt, 1)
                eng.wait_ge(s_xbtc, 2 * p + 1)
                for m in range(2):
                    eng.matmul(BB[0][:, m * P:(m + 1) * P], w_q3[:, m * P:(m + 1) * P], xbT[:, :],
                               start=True, stop=True)
                    eng.matmul(BB[2][:, m * P:(m + 1) * P], w_kv3[:, m * P:(m + 1) * P], xbT[:, :],
                               start=True, stop=True)
                eng.matmul(BB[3][:, 0:256], xbT[:, :], w_kv3[:, 256:512], start=True, stop=True)
                eng.matmul(BB[1][:, 0:256], xbT[:, :], w_g3[:, :], start=True, stop=True).then_inc(s_qkvg, 1)
                eng.wait_ge(s_q3c, 2 * p + 2)
                eng.wait_ge(s_g3e, p + 1)
                eng.wait_ge(s_k3, p + 1)
                for n in range(4):
                    m, half = n // 2, n % 2
                    eng.matmul(BB[n][:, :], q3T[:, m * P:(m + 1) * P], k_exp[:, m, half * 4:half * 4 + 4, :],
                               start=True, stop=True).then_inc(s_s3, 1)
                eng.wait_ge(s_a3, p + 1)
                for h in range(NH):
                    ins = eng.transpose(BB[h // 4][:, h % 4 * P:(h % 4 + 1) * P], a3[:, h, :], ident[:, :])
                ins.then_inc(s_a3t, 1)
                eng.wait_ge(s_a3tc, 2 * p + 2)
                for h in range(NH):
                    ins = eng.matmul(BB[2][:, h * D3:(h + 1) * D3], a3T[:, h * P:(h + 1) * P],
                                     v3[:, h * D3:(h + 1) * D3], start=True, stop=True)
                ins.then_inc(s_o3, 1)
                eng.wait_ge(s_o3g, p + 1)
                for m in range(2):
                    ins = eng.transpose(BB[3][:, m * P:(m + 1) * P],
                                        o3[:, 4 * m:4 * m + 4, :].rearrange("p h d -> p (h d)"), ident[:, :])
                ins.then_inc(s_o3t, 1)
                eng.wait_ge(s_o3tc, p + 1)
                for m in range(2):
                    ins = eng.matmul(BB[0][:, 0:C], o3T[:, m * P:(m + 1) * P], w_out3[:, m, :],
                                     start=(m == 0), stop=(m == 1))
                ins.then_inc(s_pr3, 1)
                eng.wait_ge(s_xb, 2 * p + 2)
                eng.nop(nofuse=True)
                eng.transpose(BB[1][0:C, 0:P], xn_b[:, :], ident[:, :]).then_inc(s_xbt, 1)
                eng.wait_ge(s_xbtc, 2 * p + 2)
                for m in range(2):
                    eng.matmul(BB[2][:, m * P:(m + 1) * P], w1[:, m * P:(m + 1) * P], xbT[:, :],
                               start=True, stop=True)
                eng.matmul(BB[3][:, 0:P], wr_bc[:, :], xbT[:, :], start=True, stop=True).then_inc(s_ff1, 1)
                eng.wait_ge(s_gl, p + 1)
                for m in range(2):
                    ins = eng.matmul(BB[0][:, 0:C], z1[:, m * P:(m + 1) * P], w2[:, m, :],
                                     start=(m == 0), stop=(m == 1))
                ins.then_inc(s_ff2, 1)

            eng.wait_ge(s_w, 16 * len(weight_loads))
            eng.wait_ge(s_const, 1)
            for n, w in enumerate((wq_bd, wv_bd, wo_bd)):
                eng.transpose(BB[0][:, n * P:(n + 1) * P], w[:, :], ident[:, :])
            for m in range(4):
                eng.transpose(BB[1][:, m * C:(m + 1) * C], keys_n[:, m // 2, m % 2 * P:(m % 2 + 1) * P],
                              ident[0:N, 0:N])
            eng.matmul(BB[2][:, 0:N], anti[:, :], rel_rows[:, :], start=True, stop=True).then_inc(s_tw, 1)
            eng.wait_ge(s_setup, 1)
            eng.nop().then_inc(s_gu, CHUNKS)
            front(0)
            with eng.Fori(0, pairs - 1) as i:
                front(i + 1)
                back(i)
            back(pairs - 1)

        @block.scalar
        def _(eng):
            def copy(o, i, s, scale=1.0):
                eng.activation(o, i, ACT.Copy, scale=scale).then_inc(s, 1)

            def front(p):
                for gw in range(GW):
                    eng.wait_ge(s_xt, p * GW + gw + 1)
                    copy(xT[:, gw, :], FB[2 + gw % 2][:, :], s_xtc)
                eng.wait_ge(s_qk, p + 1)
                for n in range(2):
                    copy(qk[:, n * 512:(n + 1) * 512], FB[n][:, :], s_qkc)
                for n in range(2):
                    eng.wait_ge(s_ma, 2 * p + n + 1)
                    for u in range(4):
                        g = 4 * n + u
                        ins = eng.activation(prob_a[:, g * P:(g + 1) * P], FB[n][:, u * P:(u + 1) * P], ACT.Exp,
                                             bias=max_a[:, g:g + 1], accum_out=sum_a[:, g:g + 1])
                    ins.then_inc(s_ea, 1)
                eng.wait_ge(s_pta, p + 1)
                for n in range(2):
                    copy(probT_a[:, n * 512:(n + 1) * 512], FB[n][:, :], s_ptac)
                eng.wait_ge(s_ya, p + 1)
                for n in range(2):
                    copy(y_a[:, n * 512:(n + 1) * 512], FB[2 + n][:, :], s_yac)

                def deviation(k):
                    eng.wait_ge(s_varf, 4 * p + k)
                    eng.activation(std_f[:, :], mv_f[:, 1:2], ACT.Sqrt, bias=eps[:, :]).then_inc(s_stdf, 1)

                deviation(1)
                deviation(2)
                eng.wait_ge(s_hht, p + 1)
                copy(hhT[:, :], FB[3][0:C, 0:P], s_hhtc)
                eng.wait_ge(s_m1, p + 1)
                eng.activation(p1[:, :], s1[:, :], ACT.Exp, bias=max1[:, :], accum_out=sum1[:, :]).then_inc(s_e1, 1)
                eng.wait_ge(s_p1t, p + 1)
                copy(p1T[:, :], FB[2][:, 0:P], s_p1tc)
                eng.wait_ge(s_o1, p + 1)
                copy(o1T[:, :], FB[3][0:C, 0:P], s_o1c)
                deviation(3)
                deviation(4)
                eng.wait_ge(s_xct, p + 1)
                copy(xcT[:, :], FB[1][0:C, 0:P], s_xctc)
                eng.wait_ge(s_qc, 2 * p + 1)
                copy(qpkT[:, :], FB[0][:, :], s_qcc)
                eng.wait_ge(s_qc, 2 * p + 2)
                for n in range(2):
                    copy(qc_stage[:, n * 512:(n + 1) * 512], FB[2 + n][0:C, :], s_qcc, scale=C ** -0.5)
                for n in range(2):
                    eng.wait_ge(s_sim, 2 * p + n + 1)
                    copy(probT_a[:, n * 512:(n + 1) * 512], FB[1 - n][:, :], s_simc)
                eng.wait_ge(s_fm, p + 1)
                eng.activation(fexp[:, :, :], fin[:, :, :], ACT.Exp).then_inc(s_fe, 1)

            def hand_over(p):
                eng.wait_ge(s_qcc, 3 * p + 3)
                copy(qc_live[:, :], qc_stage[:, :], s_ql)

            def back(p):
                kv_rows = kv[:, :, :].rearrange("p t h -> p (t h)")
                for n in range(2):
                    eng.wait_ge(s_gu, CHUNKS * (p + 1) + (n + 1) * (CHUNKS // 2))
                    copy(kv_rows[:, n * 512:(n + 1) * 512], BB[n][:, :], s_kvc)
                eng.wait_ge(s_vt, p + 1)
                for n in range(2):
                    copy(v2[:, 4 * n:4 * n + 4, :], BB[n][:, :].rearrange("p (h d) -> p h d", h=4)[:, :, C:P], s_vtc)
                eng.wait_ge(s_m2, p + 1)
                for h in range(NH):
                    ins = eng.activation(s2[:, h * P:(h + 1) * P], s2[:, h * P:(h + 1) * P], ACT.Exp,
                                         bias=max2[:, h:h + 1], accum_out=sum2[:, h:h + 1])
                ins.then_inc(s_e2, 1)
                eng.wait_ge(s_p2t, p + 1)
                for n in range(2):
                    copy(p2T[:, n * 512:(n + 1) * 512], BB[2 + n][:, :], s_p2tc)
                eng.wait_ge(s_o2, p + 1)
                copy(o2T[:, :], BB[0][:, :], s_o2c)
                eng.wait_ge(s_varb, 3 * p + 1)
                eng.activation(std_b[:, 0:1], mv_b[:, 1:2], ACT.Sqrt, bias=eps[:, :]).then_inc(s_stdb, 1)
                eng.wait_ge(s_xbt, 2 * p + 1)
                copy(xbT[:, :], BB[2][0:C, 0:P], s_xbtc)
                eng.wait_ge(s_qkvg, p + 1)
                copy(q3T[:, :], BB[0][:, 0:256], s_q3c, scale=16 ** -0.5)
                copy(v3[:, :], BB[3][:, 0:256], s_q3c)
                eng.wait_ge(s_g3e, p + 1)
                eng.activation(g3[:, :], g3[:, :], ACT.Exp, scale=-1.0).then_inc(s_g3x, 1)
                eng.wait_ge(s_m3, p + 1)
                for h in range(H3):
                    ins = eng.activation(s3[:, h, :], s3[:, h, :], ACT.Exp, bias=max3[:, h:h + 1],
                                         accum_out=sum3[:, h:h + 1])
                ins.then_inc(s_e3, 1)
                eng.wait_ge(s_a3t, p + 1)
                for n in range(2):
                    copy(a3T[:, n * 512:(n + 1) * 512], BB[n][:, :], s_a3tc)
                eng.wait_ge(s_varb, 3 * p + 2)
                eng.activation(std_b[:, :], mean3[:, :], ACT.Sqrt, bias=eps[:, :], scale=1.0 / D3).then_inc(s_stdb, 1)
                eng.wait_ge(s_o3t, p + 1)
                copy(o3T[:, :], BB[3][:, 0:256], s_o3tc)
                eng.wait_ge(s_varb, 3 * p + 3)
                eng.activation(std_b[:, 0:1], mv_b[:, 1:2], ACT.Sqrt, bias=eps[:, :]).then_inc(s_stdb, 1)
                eng.wait_ge(s_xbt, 2 * p + 2)
                copy(xbT[:, :], BB[1][0:C, 0:P], s_xbtc)
                eng.wait_ge(s_ge, p + 1)
                eng.activation(z1b[:, :], z1b[:, :], ACT.Exp, scale=-GELU_C).then_inc(s_gx, 1)
                eng.wait_ge(s_out, p + 1)
                eng.dma_start(out[bass.ds(p * 2, 2)].rearrange("b n c -> (b n) c"), out_sb[:, :]).then_inc(s_st, 16)

            eng.wait_ge(s_zero, 1)
            for dst, src in weight_loads:
                eng.dma_start(dst, src).then_inc(s_w, 16)
            eng.wait_ge(s_lam, 1)
            eng.activation(lexp[:, :], lsum[:, :], ACT.Exp).then_inc(s_lame, 1)
            eng.wait_ge(s_setup, 1)
            front(0)
            hand_over(0)
            with eng.Fori(0, pairs - 1) as i:
                front(i + 1)
                back(i)
                hand_over(i + 1)
            back(pairs - 1)
            eng.wait_ge(s_st, 16 * pairs)

        @block.vector
        def _(eng):
            def normalize(step, p, k, n, o, i, stats, mv, std, s_var, s_std):
                step(eng.bn_stats(stats[:, :], i), apart=True)
                eng.bn_aggr(mv[:, :], stats[:, :]).then_inc(s_var, 1)
                eng.wait_ge(s_var, n * p + k)
                eng.wait_ge(s_std, n * p + k)
                step(eng.reciprocal(std[:, 0:1], std[:, 0:1]))
                return eng.tensor_scalar(o, i, mv[:, 0:1], std[:, 0:1], ALU.subtract, ALU.mult)

            def front(p):
                step = Steps(eng, n_front, FRONT_STEPS, p)

                def norm(k, o, i):
                    return normalize(step, p, k, 4, o, i, stats_f, mv_f, std_f, s_varf, s_stdf)

                eng.wait_ge(s_x, 16 * (p + 1))
                for gw in range(GW):
                    r = slice(gw * 512, (gw + 1) * 512)
                    eng.tensor_copy(xw[:, r].rearrange("p (g i j) -> p g i j", i=GS, g=GW),
                                    x2[:, r].rearrange("p (i g j) -> p g i j", i=GS, g=GW)).then_inc(s_xw, 1)
                eng.wait_ge(s_xw, GW * (p + 1))
                step(eng.tensor_reduce(qsum[:, :], xw[:, :].rearrange("p (w x) -> p w x", w=N), AX.X, ALU.add))
                for b in range(2):
                    r = slice(b * C, b * C + C)
                    eng.tensor_scalar(q_bd[r, r], qsum[r, :], 1.0 / 64, None, ALU.mult)
                eng.tensor_scalar(qT[:, :], qsum[:, :], 1.0 / 64, None, ALU.mult).then_inc(s_mean, 1)
                eng.wait_ge(s_qp, p + 1)
                step(eng.tensor_scalar(qp[:, :], FB[0][:, 0:N], bq2[:, 0:1], 8 ** -0.5, ALU.add, ALU.mult))
                eng.tensor_tensor(q_exp[:, :].rearrange("p (g r) -> p g r", r=16), bc(qp[:, :], [16], [2]),
                                  bc(m8[:, :], [N], [1]), ALU.mult).then_inc(s_qexp, 1)
                eng.wait_ge(s_qkb, p + 1)
                for n in range(2):
                    ins = eng.tensor_copy(mask_l[0:1, n * 512:(n + 1) * 512], FB[2 + n][0:1, :])
                ins.then_inc(s_qkbc, 1)
                for n in range(2):
                    eng.wait_ge(s_sa, 2 * p + n + 1)
                    eng.tensor_reduce(max_a[:, 4 * n:4 * n + 4], FB[n][:, :].rearrange("p (u x) -> p u x", u=4),
                                      AX.X, ALU.max, negate=True).then_inc(s_ma, 1)
                eng.wait_ge(s_ea, 2 * p + 2)
                step(eng.reciprocal(sum_a[:, :], sum_a[:, :]))
                pv = prob_a[:, :].rearrange("p (u x) -> p u x", u=8)
                eng.tensor_tensor(pv, pv, bc(sum_a[:, :], [P], [2]), ALU.mult).then_inc(s_pa, 1)
                eng.wait_ge(s_za, p + 1)
                for n in range(2):
                    ins = eng.tensor_tensor(z_a[:, n * 512:(n + 1) * 512].rearrange("p (g r) -> p g r", r=16),
                                            FB[n][:, :].rearrange("p (g r) -> p g r", r=16),
                                            bc(m8[:, :], [32], [1]), ALU.mult)
                step(ins)
                step(eng.tensor_reduce(ctx_a[:, :], z_a[:, :].rearrange("p (g r) -> p g r", r=16), AX.X, ALU.add))
                for b in range(2):
                    r = slice(b * C, b * C + C)
                    ins = eng.tensor_scalar(ctx_bd[r, r], ctx_a[r, :], bv2[r, 0:1], None, ALU.add)
                ins.then_inc(s_ctx, 1)
                eng.wait_ge(s_tok, p + 1)
                step(eng.tensor_tensor(h_f[:, :], FB[2][:, 0:C], bo_r[:, :], ALU.add))
                step(norm(1, xn_f[:, :], h_f[:, :]))
                step(norm(2, hh[:, :], xn_f[:, :]))
                step(eng.tensor_tensor(hh[:, :], hh[:, :], ln1g[:, :], ALU.mult))
                eng.tensor_tensor(hh[:, :], hh[:, :], ln1b[:, :], ALU.add).then_inc(s_hh, 1)
                eng.wait_ge(s_qkv, p + 1)
                eng.tensor_scalar(q1[:, :], FB[0][0:C, 0:P], b_qk[:, 0:1], None, ALU.add)
                eng.tensor_scalar(k1[:, :], FB[0][0:C, P:2 * P], b_qk[:, 1:2], None, ALU.add)
                eng.tensor_tensor(v1[:, :], FB[0][:, 2 * P:2 * P + C], b_v[:, :], ALU.add).then_inc(s_qkvc, 1)
                eng.wait_ge(s_s1, p + 1)
                step(eng.tensor_tensor(s1[:, :], FB[1][:, 0:P], rel_bias[:, :], ALU.add))
                eng.tensor_reduce(max1[:, :], s1[:, :], AX.X, ALU.max, negate=True).then_inc(s_m1, 1)
                eng.wait_ge(s_e1, p + 1)
                step(eng.reciprocal(sum1[:, :], sum1[:, :]))
                eng.tensor_scalar(p1[:, :], p1[:, :], sum1[:, 0:1], scale1[:, 0:1], ALU.mult, ALU.mult).then_inc(s_p1, 1)
                eng.wait_ge(s_pr, p + 1)
                step(eng.tensor_tensor(o1[:, :], FB[0][:, 0:C], b_proj[:, :], ALU.add))
                step(norm(3, o1[:, :], o1[:, :]))
                step(eng.tensor_tensor(o1[:, :], o1[:, :], ln2g[:, :], ALU.mult))
                step(eng.tensor_tensor(o1[:, :], o1[:, :], ln2b[:, :], ALU.add))
                step(eng.tensor_tensor(h_f[:, :], h_f[:, :], o1[:, :], ALU.add))
                norm(4, xn_f[:, :], h_f[:, :]).then_inc(s_xc, 1)
                eng.wait_ge(s_simc, 2 * p + 2)
                eng.nop(nofuse=True)
                tops = [(top[:, g // 8, g % 8, :], topi_u[:, g // 8, g % 8, :], sim[:, g, :], sim_b[:, g, :])
                        for g in range(16)]
                best(step, tops)
                step(eng.tensor_copy(topi[:, :, :, :], topi_u[:, :, :, :]))
                i0, i1 = (topi[:, n, :, :].rearrange("p h j -> p (h j)") for n in range(2))
                step(eng.scalar_tensor_tensor(i1, i1, float(NKEY), head_off[:, :], ALU.mult, ALU.add))
                lo = 0
                for first, na, nb in RUNS:
                    for o, v in ((cand, top), (candi, topi)):
                        ins = eng.tensor_tensor(
                            o[:, :, lo:lo + na * nb].rearrange("p h (a b) -> p h a b", a=na),
                            bc(v[:, 0, :, first:first + na], [nb], [3]), bc(v[:, 1, :, 0:nb], [na], [2]), ALU.add)
                    lo += na * nb
                step(ins, apart=True)
                best(step, [(fin[:, h, :], pos_u[:, h, :], cand[:, h, :], cand_b[:, h, :]) for h in range(NH)])
                step(eng.tensor_copy(pos[:, :, :], pos_u[:, :, :]))
                step(eng.tensor_copy(fsum[:, :], fin[:, :, 0]))
                eng.tensor_tensor(fin[:, :, :], fin[:, :, :], bc(fsum[:, :], [TOPK], [2]), ALU.subtract)\
                   .then_inc(s_fm, 1)
                for h in range(NH):
                    step(eng.tensor_tensor(hot, bc(pos[:, h, :], [NC], [2]), bc(pos50[:, :], [TOPK], [1]),
                                           ALU.is_equal))
                    step(eng.tensor_tensor(hot, hot, bc(candi[:, h, :], [TOPK], [1]), ALU.mult))
                    step(eng.tensor_reduce(fidx[:, h * TOPK:(h + 1) * TOPK], hot, AX.X, ALU.add))
                eng.wait_ge(s_fe, p + 1)
                step(eng.tensor_reduce(fsum[:, :], fexp[:, :, :], AX.X, ALU.add))
                step(eng.reciprocal(fsum[:, :], fsum[:, :]))
                eng.tensor_tensor(fexp[:, :, :], fexp[:, :, :], bc(fsum[:, :], [TOPK], [2]), ALU.mult).then_inc(s_fw, 1)
                eng.wait_ge(s_ft, p + 1)
                eng.wait_ge(s_idxl, p)
                eng.tensor_copy(idx_stage[:, :], FB[2][:, 0:P]).then_inc(s_idx, 1)
                eng.tensor_copy(wT_stage[:, :], FB[3][:, 0:P]).then_inc(s_fpsum, 1)
                step.end()

            def best(step, rows):
                for o, oi, v, w in rows:
                    ins = eng.max(o[:, 0:8], v)
                step(ins, apart=True)
                for o, oi, v, w in rows:
                    eng.max_index(oi[:, 0:8], o[:, 0:8], v)
                    ins = eng.match_replace(w, o[:, 0:8], v, LOWEST)
                step(ins, apart=True)
                for o, oi, v, w in rows:
                    ins = eng.max(o[:, 8:16], w)
                step(ins, apart=True)
                for o, oi, v, w in rows:
                    ins = eng.max_index(oi[:, 8:16], o[:, 8:16], w)
                step(ins)

            def hand_over(p):
                eng.wait_ge(s_fpsum, p + 1)
                eng.wait_ge(s_out, p)
                eng.tensor_copy(h_b[:, :], h_f[:, :])
                eng.tensor_tensor(w_live[:, :, :], bc(wT_stage[:, :], [NH], [2]), bc(m16[:, :], [P], [1]), ALU.mult)\
                   .then_inc(s_wl, 1)

            def back(p):
                step = Steps(eng, n_back, BACK_STEPS, p)

                def norm(k, o, i):
                    return normalize(step, p, k, 3, o, i, stats_b, mv_b, std_b, s_varb, s_stdb)

                eng.wait_ge(s_s2, p + 1)
                for n in range(2):
                    ins = eng.tensor_tensor(s2[:, n * 512:(n + 1) * 512].rearrange("p (h x) -> p h x", h=4),
                                            BB[2 + n][:, :].rearrange("p (h x) -> p h x", h=4),
                                            bc(causal_neg[:, :], [4], [1]), ALU.add)
                step(ins)
                sv = s2[:, :].rearrange("p (h x) -> p h x", h=NH)
                eng.tensor_reduce(max2[:, :], sv, AX.X, ALU.max, negate=True).then_inc(s_m2, 1)
                eng.wait_ge(s_e2, p + 1)
                step(eng.reciprocal(sum2[:, :], sum2[:, :]))
                eng.tensor_tensor(sv, sv, bc(sum2[:, :], [P], [2]), ALU.mult).then_inc(s_p2, 1)
                eng.wait_ge(s_wo, p + 1)
                step(eng.tensor_tensor(h_b[:, :], h_b[:, :], BB[1][:, 0:C], ALU.add))
                norm(1, xn_b[:, :], h_b[:, :]).then_inc(s_xb, 1)
                eng.wait_ge(s_qkvg, p + 1)
                eng.tensor_tensor(g3[:, :], BB[1][:, 0:256], b_g3[:, :], ALU.add).then_inc(s_g3e, 1)
                for m in range(2):
                    ins = eng.tensor_tensor(k_exp[:, m, :, :], bc(BB[2][:, m * P:(m + 1) * P], [NH], [1]),
                                            bc(m16[:, :], [P], [2]), ALU.mult)
                ins.then_inc(s_k3, 1)
                for n in range(4):
                    eng.wait_ge(s_s3, 4 * p + n + 1)
                    ins = eng.tensor_tensor(s3[:, 4 * n:4 * n + 4, :], BB[n][:, :].rearrange("p (h x) -> p h x", h=4),
                                            bc(same_neg[:, :], [4], [1]), ALU.add)
                step(ins)
                eng.tensor_reduce(max3[:, :], s3, AX.X, ALU.max, negate=True).then_inc(s_m3, 1)
                eng.wait_ge(s_e3, p + 1)
                step(eng.reciprocal(sum3[:, :], sum3[:, :]))
                se = sum3[:, :].rearrange("p (h e) -> p h e", e=2)
                step(eng.tensor_scalar(se[:, :, 1], se[:, :, 1], neg_lam[:, 0:1], None, ALU.mult))
                s3v = s3.rearrange("p (h e) x -> p h e x", e=2)
                eng.tensor_tensor(a3, s3v[:, :, 0, :], bc(se[:, :, 0], [P], [2]), ALU.mult)
                step(eng.tensor_tensor(a3b, s3v[:, :, 1, :], bc(se[:, :, 1], [P], [2]), ALU.mult))
                eng.tensor_tensor(a3, a3, a3b, ALU.add).then_inc(s_a3, 1)
                eng.wait_ge(s_o3, p + 1)
                ov = BB[2][:, 0:256].rearrange("p (h d) -> p h d", d=D3)
                step(eng.tensor_reduce(mean3[:, :], ov, AX.X, ALU.add))
                step(eng.tensor_scalar(mean3[:, :], mean3[:, :], 1.0 / D3, None, ALU.mult))
                step(eng.tensor_tensor(o3[:, :, :], ov, bc(mean3[:, :], [D3], [2]), ALU.subtract))
                step(eng.tensor_tensor(sq3[:, :, :], o3[:, :, :], o3[:, :, :], ALU.mult))
                eng.tensor_reduce(mean3[:, :], sq3[:, :, :], AX.X, ALU.add).then_inc(s_varb, 1)
                eng.wait_ge(s_stdb, 3 * p + 2)
                step(eng.reciprocal(std_b[:, :], std_b[:, :]))
                step(eng.tensor_tensor(o3[:, :, :], o3[:, :, :], bc(std_b[:, :], [D3], [2]), ALU.mult))
                step(eng.tensor_tensor(o3[:, :, :], o3[:, :, :], bc(gam3[:, :], [8], [1]), ALU.mult))
                step(eng.tensor_tensor(o3[:, :, :], o3[:, :, :], bc(bet3[:, :], [8], [1]), ALU.add))
                eng.wait_ge(s_g3x, p + 1)
                step(eng.tensor_scalar(g3[:, :], g3[:, :], 1.0, None, ALU.add))
                step(eng.reciprocal(g3[:, :], g3[:, :]))
                o3r = o3[:, :, :].rearrange("p h d -> p (h d)")
                eng.scalar_tensor_tensor(o3r, o3r, 1.0 - LAMBDA_INIT, g3[:, :], ALU.mult, ALU.mult).then_inc(s_o3g, 1)
                eng.wait_ge(s_pr3, p + 1)
                step(eng.tensor_tensor(h_b[:, :], h_b[:, :], BB[0][:, 0:C], ALU.add))
                step(eng.tensor_tensor(h_b[:, :], h_b[:, :], b_out3[:, :], ALU.add))
                norm(3, xn_b[:, :], h_b[:, :]).then_inc(s_xb, 1)
                eng.wait_ge(s_ff1, p + 1)
                for m in range(2):
                    ins = eng.tensor_scalar(z1[:, m * P:(m + 1) * P], BB[2][:, m * P:(m + 1) * P], b1c[:, m:m + 1],
                                            None, ALU.add)
                step(ins)
                step(eng.tensor_tensor(z1b[:, :], z1[:, :], z1[:, :], ALU.mult))
                step(eng.tensor_scalar(z1b[:, :], z1b[:, :], 0.044715, 1.0, ALU.mult, ALU.add))
                step(eng.tensor_tensor(z1b[:, :], z1b[:, :], z1[:, :], ALU.mult))
                eng.tensor_scalar(z1b[:, :], z1b[:, :], -54.0, None, ALU.max).then_inc(s_ge, 1)
                step(eng.tensor_scalar(wrow[:, :], BB[3][:, 0:P], br_c[:, 0:1], None, ALU.add))
                step(eng.tensor_tensor(wcmp[:, :], wrow[:, :], ident[:, :], ALU.mult))
                step(eng.tensor_reduce(wcol[:, :], wcmp[:, :], AX.X, ALU.add))
                step(eng.scalar_tensor_tensor(wcmp[:, :], wrow[:, :], wcol[:, 0:1], same01[:, :], ALU.is_gt, ALU.mult))
                step(eng.tensor_reduce(rank2[:, 0:1], wcmp[:, :], AX.X, ALU.add))
                step(eng.scalar_tensor_tensor(wcmp[:, :], wrow[:, :], wcol[:, 0:1], before01[:, :], ALU.is_equal, ALU.mult))
                step(eng.tensor_reduce(rank2[:, 1:2], wcmp[:, :], AX.X, ALU.add))
                step(eng.tensor_tensor(factor[:, :], rank2[:, 0:1], rank2[:, 1:2], ALU.add))
                step(eng.scalar_tensor_tensor(factor[:, :], factor[:, :], float(KEEP), wcol[:, :], ALU.is_lt, ALU.mult))
                eng.wait_ge(s_gx, p + 1)
                step(eng.tensor_scalar(z1b[:, :], z1b[:, :], 1.0, None, ALU.add))
                step(eng.reciprocal(z1b[:, :], z1b[:, :]))
                eng.tensor_tensor(z1[:, :], z1[:, :], z1b[:, :], ALU.mult).then_inc(s_gl, 1)
                eng.wait_ge(s_ff2, p + 1)
                step(eng.tensor_tensor(y_o[:, :], BB[0][:, 0:C], b2r[:, :], ALU.add))
                step(eng.scalar_tensor_tensor(y_o[:, :], y_o[:, :], factor[:, 0:1], xn_b[:, :], ALU.mult, ALU.add))
                eng.wait_ge(s_st, 16 * p)
                eng.tensor_tensor(out_sb[:, :], y_o[:, :], h_b[:, :], ALU.add).then_inc(s_out, 1)
                step.end()

            step = Steps(eng, n_setup, SETUP_STEPS, 0)
            eng.wait_ge(s_w, 16 * len(weight_loads))
            eng.wait_ge(s_const, 1)
            eng.tensor_copy(pos50[:, :], pos50_i[:, :])
            eng.tensor_copy(head_off[:, :], head_off_i[:, :])
            eng.tensor_tensor(ident2[:, :], ident[:, 0:C], ident[:, C:P], ALU.add)
            eng.tensor_copy(wr_bc[:, :], wr_c[:, :].broadcast_to([C, P]))
            step(eng.tensor_tensor(lprod[:, :, :], lqk[:, 0:2, :], lqk[:, 2:4, :], ALU.mult))
            eng.tensor_reduce(lsum[:, :], lprod[:, :, :], AX.X, ALU.add).then_inc(s_lam, 1)
            eng.wait_ge(s_lame, 1)
            step(eng.tensor_tensor(neg_lam[:, :], lexp[:, 1:2], lexp[:, 0:1], ALU.subtract))
            eng.tensor_scalar(neg_lam[:, :], neg_lam[:, :], -LAMBDA_INIT, None, ALU.add)
            eng.wait_ge(s_tw, 1)
            eng.tensor_copy(wqT[:, :], BB[0][:, 0:P])
            eng.tensor_copy(wvT[:, :], BB[0][:, P:2 * P])
            for b in range(2):
                eng.tensor_copy(woT2[b * C:b * C + C, :], BB[0][b * C:b * C + C, 2 * P + b * C:2 * P + b * C + C])
            for m in range(4):
                for h in range(4):
                    r = slice(32 * h, 32 * h + 32)
                    eng.tensor_copy(keys_bd[r, m, h * NKEY:(h + 1) * NKEY], BB[1][r, m * C:(m + 1) * C])
            eng.tensor_tensor(rel_bias[:, :].rearrange("p (b n) -> p b n", b=2), bc(BB[2][:, 0:N], [2], [1]),
                              same_neg[:, :].rearrange("p (b n) -> p b n", b=2), ALU.add).then_inc(s_setup, 1)
            step.end()
            front(0)
            hand_over(0)
            with eng.Fori(0, pairs - 1) as i:
                front(i + 1)
                back(i)
                hand_over(i + 1)
            back(pairs - 1)


SETUP_STEPS = 2
POOL_STEPS = 28
FRONT_STEPS = 63
BACK_STEPS = 40

_OUT = ((16, 64, 64), "float32")


def kernel(**inputs):
    import numpy as _np
    import concourse.bacc as _bacc
    from concourse import mybir as _mybir
    from concourse.bass_utils import run_bass_kernel_spmd as _run

    nc = _bacc.Bacc("TRN2", target_bir_lowering=False, num_devices=1)
    arrays, aps = {}, {}
    for name, value in inputs.items():
        if name == "L1_ffn_attention_mask":
            continue
        v = _np.ascontiguousarray(value)
        if v.ndim == 0:
            v = v.reshape(1)
        arrays[f"in_{name}"] = v
        aps[name] = nc.dram_tensor(f"in_{name}", v.shape, _mybir.dt.from_np(v.dtype), kind="ExternalInput").ap()
    out = nc.dram_tensor("out_h", _OUT[0], _mybir.dt.from_np(_np.dtype(_OUT[1])), kind="ExternalOutput").ap()
    vit_tower_kernel(nc, aps, out)
    r = _run(nc, [arrays], core_ids=[0])
    return r.results[0]["out_h"]
```

```python
from contextlib import ExitStack

import concourse.bass as bass
from concourse import mybir

F32 = mybir.dt.float32
BF16 = mybir.dt.bfloat16
U32 = mybir.dt.uint32
ALU = mybir.AluOpType
ACT = mybir.ActivationFunctionType
AX = mybir.AxisListType

P = 128
C = 64
N = 64
GS = 8
GW = 8
NH = 8
TOPK = 16
NKEY = 64
NKV = NKEY * NKEY
H3 = 16
D3 = 32
HID = 256
KEEP = N // 2 - 1
EPS = 1e-5
NEG = -1e30
LOWEST = -3.0e38
ROWS_AT = 18
LAMBDA_INIT = 0.8 - 0.6 * 2.718281828459045 ** (-0.3)
GELU_C = 2.0 * 0.7978845608028654
RUNS = [(0, 1, 16), (1, 1, 8), (2, 1, 5), (3, 1, 4), (4, 1, 3), (5, 3, 2), (8, 8, 1)]
RUNS8 = [(0, 1, 8), (1, 1, 4), (2, 2, 2), (4, 4, 1)]
NC8 = sum(na * nb for _, na, nb in RUNS8)
NC = sum(na * nb for _, na, nb in RUNS)
CHUNKS = 8
TC = P // CHUNKS

FIRST = [("ident", P), ("ident2", C), ("m8", 16), ("m16", 8), ("same_neg", P), ("rel_bias", P),
         ("mask_l", 1024), ("mask_r", P), ("pos20", NC8), ("pos50", NC), ("head_off", NH * TOPK), ("eps", 1),
         ("wqT", P), ("wk_bd", P), ("wvT", P), ("woT2", C), ("bq2", 1), ("bk2", 1), ("bv2", 1), ("bo_r", C),
         ("ln1g", C), ("ln1b", C), ("ln2g", C), ("ln2b", C), ("w_qkv", 3 * C), ("b_qk", 2), ("b_v", C),
         ("scale1", 1), ("w_proj", C), ("b_proj", C), ("w_pk", 512), ("keys_bd", 1024)]
REST = [("same01", P), ("before01", P), ("causal_neg", P), ("w_q2", 512), ("w_o2", 256), ("w_q3", 256),
        ("w_kv3", 512), ("w_g3", 256), ("w_out3", 2 * C), ("b_out3", C), ("b_g3", 256), ("gam3", D3),
        ("bet3", D3), ("lqk", 64), ("wr_bc", P), ("br_c", 1), ("w1", HID), ("b1c", 2), ("w2", 2 * C), ("b2r", C)]


def places():
    at, lo = {}, 0
    for name, n in FIRST + REST:
        at[name] = (lo, n)
        lo += n
    return at, sum(n for _, n in FIRST)


class Steps:

    def __init__(self, eng, sem, n, p):
        self.eng, self.sem, self.n, self.base, self.k = eng, sem, n, p * n, 0

    def __call__(self, ins, apart=False):
        self.k += 1
        ins.then_inc(self.sem, 1)
        self.eng.wait_ge(self.sem, self.base + self.k)
        if apart:
            self.eng.nop(nofuse=True)

    def end(self):
        assert self.k == self.n, (self.k, self.n)


def vit_tower_kernel(nc, a, out):
    pairs = a["xw"].shape[0] // P
    with ExitStack() as ctx:
        def sb(name, shape, dt=F32):
            return ctx.enter_context(nc.sbuf_tensor(name, shape, dt))

        def sem(name):
            return ctx.enter_context(nc.semaphore(name))

        packed = sb("packed", [P, a["packed"].shape[1]])
        at, split = places()

        def part(name, rows=P):
            lo, n = at[name]
            return packed[0:rows, lo:lo + n]

        ident, ident2, m8, m16 = part("ident"), part("ident2"), part("m8"), part("m16")
        same01, before01 = part("same01"), part("before01")
        same_neg, causal_neg = part("same_neg"), part("causal_neg")
        rel_bias, mask_l, mask_r = part("rel_bias"), part("mask_l"), part("mask_r")
        pos20, pos50, head_off, eps = part("pos20"), part("pos50"), part("head_off"), part("eps")
        wqT, wk_bd, wvT, woT2 = part("wqT"), part("wk_bd"), part("wvT"), part("woT2")
        bq2, bk2, bv2, bo_r = part("bq2"), part("bk2"), part("bv2"), part("bo_r")
        ln1g, ln1b, ln2g, ln2b = part("ln1g"), part("ln1b"), part("ln2g"), part("ln2b")
        w_qkv, b_qk, b_v, scale1 = part("w_qkv", C), part("b_qk", C), part("b_v"), part("scale1")
        w_proj, b_proj = part("w_proj", C), part("b_proj")
        w_pk, keys_bd = part("w_pk", C), part("keys_bd").rearrange("p (m x) -> p m x", m=4)
        w_q2, w_o2 = part("w_q2", C), part("w_o2").rearrange("p (m x) -> p m x", m=4)
        w_q3, w_kv3, w_g3 = part("w_q3", C), part("w_kv3", C), part("w_g3", C)
        w_out3, b_out3 = part("w_out3").rearrange("p (m x) -> p m x", m=2), part("b_out3")
        b_g3, gam3, bet3 = part("b_g3"), part("gam3"), part("bet3")
        lqk = part("lqk").rearrange("p (n x) -> p n x", n=4)
        wr_bc, br_c, w1, b1c = part("wr_bc", C), part("br_c"), part("w1", C), part("b1c")
        w2, b2r = part("w2").rearrange("p (m x) -> p m x", m=2), part("b2r")
        ident_b = sb("ident_b", [P, P], BF16)
        same_b = sb("same_b", [P, P], BF16)
        causal_b = sb("causal_b", [P, P], BF16)
        lprod = sb("lprod", [P, 2, 16])
        lsum = sb("lsum", [P, 2])
        lexp = sb("lexp", [P, 2])
        neg_lam = sb("neg_lam", [P, 1])

        xw = sb("xw", [P, 4096])
        xT = sb("xT", [P, GW, 512])
        qsum = sb("qsum", [P, N])
        qT = sb("qT", [P, N])
        q_bd = sb("q_bd", [P, P])
        qp = sb("qp", [P, N])
        q_exp = sb("q_exp", [P, 1024])
        qk = sb("qk", [P, 1024])
        max_a = sb("max_a", [P, 8])
        sum_a = sb("sum_a", [P, 8])
        prob_a = sb("prob_a", [P, 1024])
        probT_a = sb("probT_a", [P, 1024])
        y_a = prob_a
        z_a = q_exp
        ctx_a = sb("ctx_a", [P, N])
        ctx_bd = sb("ctx_bd", [P, P])
        h_f = sb("h_f", [P, C])
        stats_f = sb("stats_f", [P, 6])
        mv_f = sb("mv_f", [P, 2])
        std_f = sb("std_f", [P, 1])
        xn_f = sb("xn_f", [P, C])
        hh = sb("hh", [P, C])
        hhT = sb("hhT", [C, P])
        q1 = sb("q1", [C, P])
        k1 = sb("k1", [C, P])
        v1 = sb("v1", [P, C])
        s1 = sb("s1", [P, P])
        max1 = sb("max1", [P, 1])
        sum1 = sb("sum1", [P, 1])
        p1 = sb("p1", [P, P])
        p1T = sb("p1T", [P, P])
        o1T = sb("o1T", [C, P])
        o1 = sb("o1", [P, C])
        xcT = sb("xcT", [C, P])
        qpkT = q_exp[:, 0:512]
        sim = probT_a[:, :].rearrange("p (g k) -> p g k", k=NKEY)
        sim_b = qk[:, :].rearrange("p (g k) -> p g k", k=NKEY)
        top = sb("top", [P, 2, NH, TOPK])
        topi_u = sb("topi_u", [P, 2, NH, TOPK], U32)
        topi = sb("topi", [P, 2, NH, TOPK])
        cand, candi, cand_b = (t[:, lo:lo + NH * NC].rearrange("p (h c) -> p h c", c=NC)
                               for t, lo in ((q_exp, 512), (q_exp, 0), (qk, 0)))
        fin = sb("fin", [P, NH, TOPK])
        pos_u = sb("pos_u", [P, NH, TOPK], U32)
        pos = sb("pos", [P, NH, TOPK])
        candi8 = sb("candi8", [P, NH, NC8])
        hot = prob_a
        fidx = sb("fidx", [P, NH * TOPK])
        fexp = sb("fexp", [P, NH, TOPK])
        fsum = sb("fsum", [P, NH])
        idx_stage = sb("idx_stage", [P, P], U32)
        h_mid = sb("h_mid", [P, C])
        xcT_mid = sb("xcT_mid", [C, P])
        w_mid = sb("w_mid", [P, P])
        idx_live = sb("idx_live", [P, P], U32)
        w_live = sb("w_live", [P, P, NH])
        xcT_b = sb("xcT_b", [C, P])
        qc = sb("qc", [C, 1024])
        h_b = sb("h_b", [P, C])
        gath = sb("gath", [P, P, 2 * C])
        kv = sb("kv", [P, P, NH])
        v2 = sb("v2", [P, NH, C])
        sp2 = sb("sp2", [P, 2048])
        s2, p2T = sp2[:, 0:1024], sp2[:, 1024:2048]
        max2 = sb("max2", [P, 8])
        sum2 = sb("sum2", [P, 8])
        o2T = sb("o2T", [P, 512])
        stats_b = sb("stats_b", [P, 6])
        mv_b = sb("mv_b", [P, 2])
        std_b = sb("std_b", [P, 8])
        xn_b = sb("xn_b", [P, C])
        xbT = sb("xbT", [C, P])
        q3T = sb("q3T", [P, 256])
        v3 = sb("v3", [P, 256])
        g3 = sb("g3", [P, 256])
        k_exp = sb("k_exp", [P, 2, NH, P])
        s3 = sp2[:, :].rearrange("p (h x) -> p h x", x=P)
        max3 = sb("max3", [P, H3])
        sum3 = sb("sum3", [P, H3])
        a3 = k_exp[:, 0]
        a3b = k_exp[:, 1]
        a3T = kv[:, :, :].rearrange("p t h -> p (t h)")
        o3 = sb("o3", [P, 8, D3])
        sq3 = sb("sq3", [P, 8, D3])
        mean3 = sb("mean3", [P, 8])
        o3T = v3
        z1 = q3T
        z1b = g3
        wrow = sb("wrow", [P, P])
        wcmp = sb("wcmp", [P, P])
        wcol = sb("wcol", [P, 1])
        rank2 = sb("rank2", [P, 2])
        factor = sb("factor", [P, 1])
        y_o = sb("y_o", [P, C])
        out_sb = sb("out_sb", [P, C])

        FB = [ctx.enter_context(nc.psum_tensor(f"front{n}", [P, 512], F32)) for n in range(4)]
        BB = [ctx.enter_context(nc.psum_tensor(f"back{n}", [P, 512], F32)) for n in range(4)]

        s_x = sem("x_loaded")
        s_cf = sem("constants_loaded_for_front")
        s_cb = sem("constants_loaded_for_rest")
        s_zero = sem("zeros_set")
        s_lam = sem("lambda_sums")
        s_lame = sem("lambda_exps")
        s_setup = sem("setup_done")
        n_setup = sem("setup_steps")
        n_front = sem("front_steps")
        s_front = sem("front_done")
        s_xt = sem("x_turned_loaded")
        s_mean = sem("window_means")
        s_qp = sem("pool_queries")
        s_qexp = sem("pool_queries_spread")
        s_qk = sem("pool_query_keys")
        s_qkc = sem("pool_query_keys_copied")
        s_qkb = sem("pool_key_bias")
        s_qkbc = sem("pool_key_bias_copied")
        s_sa = sem("pool_scores")
        s_ma = sem("pool_maxima")
        s_ea = sem("pool_exps")
        s_pa = sem("pool_probs")
        s_pta = sem("pool_probs_turned")
        s_ptac = sem("pool_probs_turned_copied")
        s_ya = sem("pool_sums")
        s_yac = sem("pool_sums_copied")
        s_za = sem("pool_values")
        s_ctx = sem("pool_context")
        s_tok = sem("tokens")
        s_varf = sem("front_variances")
        s_stdf = sem("front_deviations")
        s_hh = sem("attn_input")
        s_hht = sem("attn_input_turned")
        s_hhtc = sem("attn_input_turned_copied")
        s_qkv = sem("attn_qkv")
        s_qkvc = sem("attn_qkv_copied")
        s_s1 = sem("attn_scores")
        s_m1 = sem("attn_maxima")
        s_e1 = sem("attn_exps")
        s_p1 = sem("attn_probs")
        s_p1t = sem("attn_probs_turned")
        s_p1tc = sem("attn_probs_turned_copied")
        s_o1 = sem("attn_out")
        s_o1c = sem("attn_out_copied")
        s_pr = sem("attn_projected")
        s_xc = sem("memory_input")
        s_xct = sem("memory_input_turned")
        s_xctc = sem("memory_input_turned_copied")
        s_qc = sem("memory_queries")
        s_qcc = sem("memory_queries_copied")
        s_sim = sem("key_scores")
        s_simc = sem("key_scores_copied")
        s_fm = sem("picks_found")
        s_fe = sem("picks_exps")
        s_fw = sem("pick_weights")
        s_ft = sem("picks_turned")
        s_idx = sem("pick_indices")
        s_idxl = sem("indices_taken")
        s_g = [sem(f"rows_fetched{c}") for c in range(CHUNKS)]
        s_gu = sem("row_parts_free")
        s_wl = sem("pick_weights_spread")
        s_rot = sem("carried_over")
        s_keep = sem("kept_for_later")
        n_back = sem("back_steps")
        s_kvc = sem("keys_values_copied")
        s_qb = sem("memory_queries_made")
        s_qbc = sem("memory_queries_scaled")
        s_s2 = sem("memory_scores")
        s_vt = sem("memory_values_turned")
        s_vtc = sem("memory_values_turned_copied")
        s_m2 = sem("memory_maxima")
        s_e2 = sem("memory_exps")
        s_p2 = sem("memory_probs")
        s_p2t = sem("memory_probs_turned")
        s_p2tc = sem("memory_probs_turned_copied")
        s_o2 = sem("memory_out")
        s_o2c = sem("memory_out_copied")
        s_wo = sem("memory_projected")
        s_varb = sem("back_variances")
        s_stdb = sem("back_deviations")
        s_xb = sem("back_input")
        s_xbt = sem("back_input_turned")
        s_xbtc = sem("back_input_turned_copied")
        s_qkvg = sem("diff_projections")
        s_q3c = sem("diff_queries_copied")
        s_k3 = sem("diff_keys_spread")
        s_g3e = sem("diff_gates_in")
        s_g3x = sem("diff_gates_exps")
        s_s3 = sem("diff_scores")
        s_m3 = sem("diff_maxima")
        s_e3 = sem("diff_exps")
        s_a3 = sem("diff_probs")
        s_a3t = sem("diff_probs_turned")
        s_a3tc = sem("diff_probs_turned_copied")
        s_o3 = sem("diff_out")
        s_o3g = sem("diff_out_gated")
        s_o3t = sem("diff_out_turned")
        s_o3tc = sem("diff_out_turned_copied")
        s_pr3 = sem("diff_projected")
        s_ff1 = sem("hidden_and_router")
        s_ge = sem("gelu_arguments")
        s_gx = sem("gelu_exps")
        s_gl = sem("gelu_done")
        s_ff2 = sem("feedforward_out")
        s_out = sem("output_ready")
        s_st = sem("output_stored")

        def bc(ap, dims, at):
            for n, axis in zip(dims, at):
                ap = ap.unsqueeze(axis)
                shape = list(ap.shape)
                shape[axis] = n
                ap = ap.broadcast_to(shape)
            return ap

        def window_pair(gw, q):
            return xw[:, gw * 512 + q * P:gw * 512 + (q + 1) * P]

        def in_turns(*parts):
            parts = list(parts)
            while parts:
                parts = [part for part in parts if next(part, "over") != "over"]

        block = ctx.enter_context(nc.Block())

        @block.sync
        def _(eng):
            def load_x(p):
                eng.dma_start(xw[:, :], a["xw"][bass.ds(p * P, P)]).then_inc(s_x, 16)
                eng.dma_start(xT[:, :, :].rearrange("p g x -> p (g x)"), a["xT"][bass.ds(p * P, P)])\
                   .then_inc(s_xt, 16)

            load_x(0)
            with eng.Fori(1, pairs) as p:
                eng.wait_ge(s_ya, p)
                load_x(p)

        @block.gpsimd
        def _(eng):
            with eng.Fori(0, pairs) as p:
                for c in range(CHUNKS):
                    eng.wait_ge(s_g[c], p * (16 * TC))
                eng.wait_ge(s_idx, p + 1)
                eng.nop(nofuse=True)
                eng.tensor_copy(idx_live[:, :], idx_stage[:, :]).then_inc(s_idxl, 1)
                eng.wait_ge(s_idxl, p + 1)
                for c in range(CHUNKS):
                    eng.wait_ge(s_gu, p * CHUNKS + c + 1)
                    eng.nop(nofuse=True)
                    for t in range(c * TC, (c + 1) * TC):
                        eng.indirect_dma_start(gath[:, t, :], None, a["table"],
                                               bass.IndirectOffsetOnAxis(idx_live[:, t:t + 1], axis=0))\
                           .then_inc(s_g[c], 16)

        @block.tensor
        def _(eng):
            def front(p):
                eng.wait_ge(s_front, p)
                eng.wait_ge(s_mean, p + 1)
                eng.matmul(FB[0][:, 0:N], wqT[:, :], qT[:, :], start=True, stop=True).then_inc(s_qp, 1)
                yield
                eng.wait_ge(s_qexp, p + 1)
                for n in range(2):
                    ins = eng.matmul(FB[n][:, :], wk_bd[:, :], q_exp[:, n * 512:(n + 1) * 512], start=True, stop=True)
                ins.then_inc(s_qk, 1)
                for n in range(2):
                    ins = eng.matmul(FB[2 + n][0:1, :], bk2[:, :], q_exp[:, n * 512:(n + 1) * 512], start=True, stop=True)
                ins.then_inc(s_qkb, 1)
                yield
                eng.wait_ge(s_qkc, 2 * p + 2)
                eng.wait_ge(s_qkbc, p + 1)
                for gw in range(GW):
                    o = FB[gw // 4][:, gw % 4 * P:(gw % 4 + 1) * P]
                    eng.matmul(o, mask_l[:, gw * P:(gw + 1) * P], mask_r[:, :], start=True, stop=False)
                    for q in range(4):
                        u = (gw * 4 + q) * 32
                        ins = eng.matmul(o[32 * q:32 * q + 32, :], qk[:, u:u + 32], window_pair(gw, q),
                                         start=False, stop=True)
                    if gw % 4 == 3:
                        ins.then_inc(s_sa, 1)
                yield
                eng.wait_ge(s_pa, p + 1)
                for gw in range(GW):
                    ins = eng.transpose(FB[gw // 4][:, gw % 4 * P:(gw % 4 + 1) * P], prob_a[:, gw * P:(gw + 1) * P],
                                        ident[:, :])
                ins.then_inc(s_pta, 1)
                yield
                eng.wait_ge(s_xt, 16 * (p + 1))
                eng.wait_ge(s_ptac, 2 * p + 2)
                for gw in range(GW):
                    for q in range(4):
                        u = (gw * 4 + q) * 32
                        ins = eng.matmul(FB[2 + u // 512][:, u % 512:u % 512 + 32], xT[:, gw, q * P:(q + 1) * P],
                                         probT_a[:, u:u + 32], start=True, stop=True)
                ins.then_inc(s_ya, 1)
                yield
                eng.wait_ge(s_yac, 2 * p + 2)
                for n in range(2):
                    ins = eng.matmul(FB[n][:, :], wvT[:, :], y_a[:, n * 512:(n + 1) * 512], start=True, stop=True)
                ins.then_inc(s_za, 1)
                yield
                eng.wait_ge(s_ctx, p + 1)
                eng.matmul(FB[2][:, 0:C], ctx_bd[:, :], woT2[:, :], start=True, stop=False)
                eng.matmul(FB[2][:, 0:C], q_bd[:, :], ident2[:, :], start=False, stop=True).then_inc(s_tok, 1)
                yield
                yield
                eng.wait_ge(s_hh, p + 1)
                eng.nop(nofuse=True)
                eng.transpose(FB[3][0:C, 0:P], hh[:, :], ident[:, :]).then_inc(s_hht, 1)
                yield
                eng.wait_ge(s_hhtc, p + 1)
                eng.nop(nofuse=True)
                eng.matmul(FB[0][0:C, 0:P], w_qkv[:, 0:C], hhT[:, :], start=True, stop=True)
                eng.matmul(FB[0][0:C, P:2 * P], w_qkv[:, C:2 * C], hhT[:, :], start=True, stop=True)
                eng.matmul(FB[0][:, 2 * P:2 * P + C], hhT[:, :], w_qkv[:, 2 * C:3 * C], start=True, stop=True)\
                   .then_inc(s_qkv, 1)
                yield
                eng.wait_ge(s_qkvc, p + 1)
                eng.matmul(FB[1][:, 0:P], q1[:, :], k1[:, :], start=True, stop=True).then_inc(s_s1, 1)
                yield
                eng.wait_ge(s_p1, p + 1)
                eng.transpose(FB[2][:, 0:P], p1[:, :], ident[:, :]).then_inc(s_p1t, 1)
                yield
                eng.wait_ge(s_p1tc, p + 1)
                eng.matmul(FB[3][0:C, 0:P], v1[:, :], p1T[:, :], start=True, stop=True).then_inc(s_o1, 1)
                yield
                eng.wait_ge(s_o1c, p + 1)
                eng.matmul(FB[0][:, 0:C], o1T[:, :], w_proj[:, :], start=True, stop=True).then_inc(s_pr, 1)
                yield
                yield
                eng.wait_ge(s_xc, p + 1)
                eng.nop(nofuse=True)
                eng.transpose(FB[1][0:C, 0:P], xn_f[:, :], ident[:, :]).then_inc(s_xct, 1)
                yield
                eng.wait_ge(s_xctc, p + 1)
                for m in range(4):
                    ins = eng.matmul(FB[0][:, m * P:(m + 1) * P], w_pk[:, m * P:(m + 1) * P], xcT[:, :],
                                     start=True, stop=True)
                ins.then_inc(s_qc, 1)
                yield
                eng.wait_ge(s_qcc, p + 1)
                for m in range(4):
                    ins = eng.matmul(FB[1 - m // 2][:, m % 2 * 256:(m % 2 + 1) * 256], qpkT[:, m * P:(m + 1) * P],
                                     keys_bd[:, m, :], start=True, stop=True)
                    if m % 2 == 1:
                        ins.then_inc(s_sim, 1)
                for _ in range(6):
                    yield
                eng.wait_ge(s_fw, p + 1)
                eng.transpose(FB[2][:, 0:P], fidx[:, :], ident[:, :])
                eng.transpose(FB[3][:, 0:P], fexp[:, :, :].rearrange("p h j -> p (h j)"), ident[:, :])\
                   .then_inc(s_ft, 1)

            def take(p, c):
                eng.wait_ge(s_g[c], (p + 1) * (16 * TC))
                for t in range(c * TC, (c + 1) * TC):
                    ins = eng.matmul(BB[t // 64][:, t % 64 * 8:t % 64 * 8 + 8], gath[:, t, :], w_live[:, t, :],
                                     start=True, stop=True)
                ins.then_inc(s_gu, 1)

            def rows(p):
                for _ in range(ROWS_AT):
                    yield
                eng.wait_ge(s_out, p)
                eng.wait_ge(s_wl, p + 1)
                for parts in ((0, 1), (2, 3), (4,), (5,), (6,)):
                    for c in parts:
                        take(p, c)
                    yield

            def back(p):
                take(p, CHUNKS - 1)
                eng.wait_ge(s_rot, p + 1)
                eng.nop(nofuse=True)
                for h in range(NH):
                    ins = eng.matmul(BB[2 + h // 4][0:C, h % 4 * P:(h % 4 + 1) * P], w_q2[:, h * C:(h + 1) * C],
                                     xcT_b[:, :], start=True, stop=True)
                ins.then_inc(s_qb, 1)
                yield
                eng.wait_ge(s_kvc, 2 * p + 2)
                eng.wait_ge(s_qbc, 2 * p + 2)
                for n in range(2):
                    eng.matmul(BB[2 + n][:, :], ident_b[:, :], bc(causal_b[:, :], [4], [1]), start=True, stop=False)
                    for h in range(4 * n, 4 * n + 4):
                        ins = eng.matmul(BB[2 + n][:, h % 4 * P:(h % 4 + 1) * P], qc[:, h * P:(h + 1) * P],
                                         kv[0:C, :, h], start=False, stop=(h % 4 == 3))
                    ins.then_inc(s_s2, 1)
                for h in range(NH):
                    ins = eng.transpose(BB[h // 4][:, h % 4 * P:(h % 4 + 1) * P], kv[:, :, h], ident[:, :])
                ins.then_inc(s_vt, 1)
                yield
                eng.wait_ge(s_p2, p + 1)
                for h in range(NH):
                    ins = eng.transpose(BB[2 + h // 4][:, h % 4 * P:(h % 4 + 1) * P], s2[:, h * P:(h + 1) * P],
                                        ident[:, :])
                ins.then_inc(s_p2t, 1)
                yield
                eng.wait_ge(s_vtc, 2 * p + 2)
                eng.wait_ge(s_p2tc, 2 * p + 2)
                for h in range(NH):
                    lo = h % 2 * C
                    ins = eng.matmul(BB[0][lo:lo + C, h // 2 * P:(h // 2 + 1) * P], v2[:, h, :],
                                     p2T[:, h * P:(h + 1) * P], start=True, stop=True)
                ins.then_inc(s_o2, 1)
                yield
                eng.wait_ge(s_o2c, p + 1)
                for m in range(4):
                    ins = eng.matmul(BB[1][:, 0:C], o2T[:, m * P:(m + 1) * P], w_o2[:, m, :],
                                     start=(m == 0), stop=(m == 3))
                ins.then_inc(s_wo, 1)
                yield
                eng.wait_ge(s_xb, 2 * p + 1)
                eng.nop(nofuse=True)
                eng.transpose(BB[2][0:C, 0:P], xn_b[:, :], ident[:, :]).then_inc(s_xbt, 1)
                yield
                eng.wait_ge(s_xbtc, 2 * p + 1)
                for m in range(2):
                    eng.matmul(BB[0][:, m * P:(m + 1) * P], w_q3[:, m * P:(m + 1) * P], xbT[:, :],
                               start=True, stop=True)
                    eng.matmul(BB[2 + m][:, 256:384], w_kv3[:, m * P:(m + 1) * P], xbT[:, :],
                               start=True, stop=True)
                eng.matmul(BB[3][:, 0:256], xbT[:, :], w_kv3[:, 256:512], start=True, stop=True)
                eng.matmul(BB[1][:, 0:256], xbT[:, :], w_g3[:, :], start=True, stop=True).then_inc(s_qkvg, 1)
                yield
                eng.wait_ge(s_q3c, 2 * p + 2)
                eng.wait_ge(s_g3e, p + 1)
                eng.wait_ge(s_k3, 2 * p + 2)
                for n in range(4):
                    m, half = n // 2, n % 2
                    eng.matmul(BB[n][:, :], ident_b[:, :], bc(same_b[:, :], [4], [1]), start=True, stop=False)
                    eng.matmul(BB[n][:, :], q3T[:, m * P:(m + 1) * P], k_exp[:, m, half * 4:half * 4 + 4, :],
                               start=False, stop=True).then_inc(s_s3, 1)
                yield
                eng.wait_ge(s_a3, p + 1)
                for h in range(NH):
                    ins = eng.transpose(BB[h // 4][:, h % 4 * P:(h % 4 + 1) * P], a3[:, h, :], ident[:, :])
                ins.then_inc(s_a3t, 1)
                yield
                eng.wait_ge(s_a3tc, 2 * p + 2)
                for h in range(NH):
                    ins = eng.matmul(BB[2][:, h * D3:(h + 1) * D3], a3T[:, h * P:(h + 1) * P],
                                     v3[:, h * D3:(h + 1) * D3], start=True, stop=True)
                ins.then_inc(s_o3, 1)
                yield
                eng.wait_ge(s_o3g, p + 1)
                for m in range(2):
                    ins = eng.transpose(BB[3][:, m * P:(m + 1) * P],
                                        o3[:, 4 * m:4 * m + 4, :].rearrange("p h d -> p (h d)"), ident[:, :])
                ins.then_inc(s_o3t, 1)
                yield
                eng.wait_ge(s_o3tc, p + 1)
                for m in range(2):
                    ins = eng.matmul(BB[0][:, 0:C], o3T[:, m * P:(m + 1) * P], w_out3[:, m, :],
                                     start=(m == 0), stop=(m == 1))
                ins.then_inc(s_pr3, 1)
                yield
                eng.wait_ge(s_xb, 2 * p + 2)
                eng.nop(nofuse=True)
                eng.transpose(BB[1][0:C, 0:P], xn_b[:, :], ident[:, :]).then_inc(s_xbt, 1)
                yield
                eng.wait_ge(s_xbtc, 2 * p + 2)
                for m in range(2):
                    eng.matmul(BB[2][:, m * P:(m + 1) * P], w1[:, m * P:(m + 1) * P], xbT[:, :],
                               start=True, stop=True)
                eng.matmul(BB[3][:, 0:P], wr_bc[:, :], xbT[:, :], start=True, stop=True).then_inc(s_ff1, 1)
                yield
                yield
                eng.wait_ge(s_gl, p + 1)
                for m in range(2):
                    ins = eng.matmul(BB[0][:, 0:C], z1[:, m * P:(m + 1) * P], w2[:, m, :],
                                     start=(m == 0), stop=(m == 1))
                ins.then_inc(s_ff2, 1)

            eng.wait_ge(s_cf, 16)
            eng.wait_ge(s_zero, 1)
            eng.nop().then_inc(s_gu, CHUNKS)
            in_turns(front(0))
            eng.wait_ge(s_cb, 16)
            in_turns(front(1), rows(0))
            with eng.Fori(1, pairs - 1) as i:
                in_turns(front(i + 1), back(i - 1), rows(i))
            in_turns(back(pairs - 2), rows(pairs - 1))
            in_turns(back(pairs - 1))

        @block.scalar
        def _(eng):
            def copy(o, i, s, scale=1.0):
                eng.activation(o, i, ACT.Copy, scale=scale).then_inc(s, 1)

            def front(p):
                yield
                eng.wait_ge(s_qk, p + 1)
                for n in range(2):
                    copy(qk[:, n * 512:(n + 1) * 512], FB[n][:, :], s_qkc)
                yield
                for n in range(2):
                    eng.wait_ge(s_ma, 2 * p + n + 1)
                    for u in range(4):
                        g = 4 * n + u
                        ins = eng.activation(prob_a[:, g * P:(g + 1) * P], FB[n][:, u * P:(u + 1) * P], ACT.Exp,
                                             bias=max_a[:, g:g + 1], accum_out=sum_a[:, g:g + 1])
                    ins.then_inc(s_ea, 1)
                yield
                eng.wait_ge(s_pta, p + 1)
                for n in range(2):
                    copy(probT_a[:, n * 512:(n + 1) * 512], FB[n][:, :], s_ptac)
                yield
                eng.wait_ge(s_ya, p + 1)
                for n in range(2):
                    copy(y_a[:, n * 512:(n + 1) * 512], FB[2 + n][:, :], s_yac)
                yield
                yield

                def deviation(k):
                    eng.wait_ge(s_varf, 4 * p + k)
                    eng.activation(std_f[:, :], mv_f[:, 1:2], ACT.Sqrt, bias=eps[:, :]).then_inc(s_stdf, 1)

                deviation(1)
                yield
                deviation(2)
                yield
                eng.wait_ge(s_hht, p + 1)
                copy(hhT[:, :], FB[3][0:C, 0:P], s_hhtc)
                yield
                yield
                eng.wait_ge(s_m1, p + 1)
                eng.activation(p1[:, :], s1[:, :], ACT.Exp, bias=max1[:, :], accum_out=sum1[:, :]).then_inc(s_e1, 1)
                yield
                eng.wait_ge(s_p1t, p + 1)
                copy(p1T[:, :], FB[2][:, 0:P], s_p1tc)
                yield
                eng.wait_ge(s_o1, p + 1)
                copy(o1T[:, :], FB[3][0:C, 0:P], s_o1c)
                yield
                deviation(3)
                yield
                deviation(4)
                yield
                eng.wait_ge(s_xct, p + 1)
                copy(xcT[:, :], FB[1][0:C, 0:P], s_xctc)
                yield
                eng.wait_ge(s_qc, p + 1)
                copy(qpkT[:, :], FB[0][:, :], s_qcc)
                yield
                for n in range(2):
                    eng.wait_ge(s_sim, 2 * p + n + 1)
                    copy(probT_a[:, n * 512:(n + 1) * 512], FB[1 - n][:, :], s_simc)
                for _ in range(4):
                    yield
                eng.wait_ge(s_fm, p + 1)
                eng.activation(fexp[:, :, :], fin[:, :, :], ACT.Exp).then_inc(s_fe, 1)

            def half(p, n):
                eng.wait_ge(s_gu, CHUNKS * (p + 1) + (n + 1) * (CHUNKS // 2))
                copy(kv[:, :, :].rearrange("p t h -> p (t h)")[:, n * 512:(n + 1) * 512], BB[n][:, :], s_kvc)

            def rows(p):
                for _ in range(ROWS_AT + 2):
                    yield
                half(p, 0)

            def back(p):
                eng.wait_ge(s_qb, p + 1)
                for n in range(2):
                    copy(qc[:, n * 512:(n + 1) * 512], BB[2 + n][0:C, :], s_qbc, scale=C ** -0.5)
                half(p, 1)
                yield
                eng.wait_ge(s_vt, p + 1)
                for n in range(2):
                    copy(v2[:, 4 * n:4 * n + 4, :], BB[n][:, :].rearrange("p (h d) -> p h d", h=4)[:, :, C:P], s_vtc)
                for h in range(NH):
                    eng.wait_ge(s_m2, 2 * p + h // 4 + 1)
                    ins = eng.activation(s2[:, h * P:(h + 1) * P], BB[2 + h // 4][:, h % 4 * P:(h % 4 + 1) * P],
                                         ACT.Exp, bias=max2[:, h:h + 1], accum_out=sum2[:, h:h + 1])
                ins.then_inc(s_e2, 1)
                yield
                eng.wait_ge(s_p2t, p + 1)
                for n in range(2):
                    copy(p2T[:, n * 512:(n + 1) * 512], BB[2 + n][:, :], s_p2tc)
                yield
                eng.wait_ge(s_o2, p + 1)
                copy(o2T[:, :], BB[0][:, :], s_o2c)
                yield
                eng.wait_ge(s_varb, 3 * p + 1)
                eng.activation(std_b[:, 0:1], mv_b[:, 1:2], ACT.Sqrt, bias=eps[:, :]).then_inc(s_stdb, 1)
                yield
                eng.wait_ge(s_xbt, 2 * p + 1)
                copy(xbT[:, :], BB[2][0:C, 0:P], s_xbtc)
                yield
                eng.wait_ge(s_qkvg, p + 1)
                copy(q3T[:, :], BB[0][:, 0:256], s_q3c, scale=16 ** -0.5)
                copy(v3[:, :], BB[3][:, 0:256], s_q3c)
                for h in range(NH):
                    ins = eng.activation(k_exp[:, 1, h, :], BB[3][:, 256:384], ACT.Copy, scale=m16[:, h:h + 1])
                ins.then_inc(s_k3, 1)
                eng.wait_ge(s_g3e, p + 1)
                eng.activation(g3[:, :], g3[:, :], ACT.Exp, scale=-1.0).then_inc(s_g3x, 1)
                yield
                for h in range(H3):
                    eng.wait_ge(s_m3, 4 * p + h // 4 + 1)
                    ins = eng.activation(s3[:, h, :], BB[h // 4][:, h % 4 * P:(h % 4 + 1) * P], ACT.Exp,
                                         bias=max3[:, h:h + 1], accum_out=sum3[:, h:h + 1])
                ins.then_inc(s_e3, 1)
                yield
                eng.wait_ge(s_a3t, p + 1)
                for n in range(2):
                    copy(a3T[:, n * 512:(n + 1) * 512], BB[n][:, :], s_a3tc)
                yield
                eng.wait_ge(s_varb, 3 * p + 2)
                eng.activation(std_b[:, :], mean3[:, :], ACT.Sqrt, bias=eps[:, :], scale=1.0 / D3).then_inc(s_stdb, 1)
                yield
                eng.wait_ge(s_o3t, p + 1)
                copy(o3T[:, :], BB[3][:, 0:256], s_o3tc)
                yield
                eng.wait_ge(s_varb, 3 * p + 3)
                eng.activation(std_b[:, 0:1], mv_b[:, 1:2], ACT.Sqrt, bias=eps[:, :]).then_inc(s_stdb, 1)
                yield
                eng.wait_ge(s_xbt, 2 * p + 2)
                copy(xbT[:, :], BB[1][0:C, 0:P], s_xbtc)
                yield
                eng.wait_ge(s_ge, p + 1)
                eng.activation(z1b[:, :], z1b[:, :], ACT.Exp, scale=-GELU_C).then_inc(s_gx, 1)
                yield
                yield
                eng.wait_ge(s_out, p + 1)
                eng.dma_start(out[bass.ds(p * 2, 2)].rearrange("b n c -> (b n) c"), out_sb[:, :]).then_inc(s_st, 16)

            eng.dma_start(packed[:, 0:split], a["packed"][:, 0:split]).then_inc(s_cf, 16)
            eng.dma_start(packed[:, split:], a["packed"][:, split:]).then_inc(s_cb, 16)
            eng.wait_ge(s_cf, 16)
            in_turns(front(0))
            eng.wait_ge(s_lam, 1)
            eng.activation(lexp[:, :], lsum[:, :], ACT.Exp).then_inc(s_lame, 1)
            in_turns(front(1), rows(0))
            with eng.Fori(1, pairs - 1) as i:
                in_turns(front(i + 1), back(i - 1), rows(i))
            in_turns(back(pairs - 2), rows(pairs - 1))
            in_turns(back(pairs - 1))
            eng.wait_ge(s_st, 16 * pairs)

        @block.vector
        def _(eng):
            def normalize(step, p, k, n, o, i, stats, mv, std, s_var, s_std):
                step(eng.bn_stats(stats[:, :], i), apart=True)
                eng.bn_aggr(mv[:, :], stats[:, :]).then_inc(s_var, 1)
                yield
                eng.wait_ge(s_var, n * p + k)
                eng.wait_ge(s_std, n * p + k)
                step(eng.reciprocal(std[:, 0:1], std[:, 0:1]))
                return eng.tensor_scalar(o, i, mv[:, 0:1], std[:, 0:1], ALU.subtract, ALU.mult)

            def front(p):
                step = Steps(eng, n_front, FRONT_STEPS, p)

                def norm(k, o, i):
                    return normalize(step, p, k, 4, o, i, stats_f, mv_f, std_f, s_varf, s_stdf)

                eng.wait_ge(s_x, 16 * (p + 1))
                step(eng.tensor_reduce(qsum[:, :], xw[:, :].rearrange("p (w x) -> p w x", w=N), AX.X, ALU.add))
                for b in range(2):
                    r = slice(b * C, b * C + C)
                    eng.tensor_scalar(q_bd[r, r], qsum[r, :], 1.0 / 64, None, ALU.mult)
                eng.tensor_scalar(qT[:, :], qsum[:, :], 1.0 / 64, None, ALU.mult).then_inc(s_mean, 1)
                eng.wait_ge(s_qp, p + 1)
                step(eng.tensor_scalar(qp[:, :], FB[0][:, 0:N], bq2[:, 0:1], 8 ** -0.5, ALU.add, ALU.mult))
                eng.tensor_tensor(q_exp[:, :].rearrange("p (g r) -> p g r", r=16), bc(qp[:, :], [16], [2]),
                                  bc(m8[:, :], [N], [1]), ALU.mult).then_inc(s_qexp, 1)
                yield
                eng.wait_ge(s_qkb, p + 1)
                for n in range(2):
                    ins = eng.tensor_copy(mask_l[0:1, n * 512:(n + 1) * 512], FB[2 + n][0:1, :])
                ins.then_inc(s_qkbc, 1)
                yield
                for n in range(2):
                    eng.wait_ge(s_sa, 2 * p + n + 1)
                    eng.tensor_reduce(max_a[:, 4 * n:4 * n + 4], FB[n][:, :].rearrange("p (u x) -> p u x", u=4),
                                      AX.X, ALU.max, negate=True).then_inc(s_ma, 1)
                yield
                eng.wait_ge(s_ea, 2 * p + 2)
                step(eng.reciprocal(sum_a[:, :], sum_a[:, :]))
                pv = prob_a[:, :].rearrange("p (u x) -> p u x", u=8)
                eng.tensor_tensor(pv, pv, bc(sum_a[:, :], [P], [2]), ALU.mult).then_inc(s_pa, 1)
                yield
                yield
                eng.wait_ge(s_za, p + 1)
                for n in range(2):
                    ins = eng.tensor_tensor(z_a[:, n * 512:(n + 1) * 512].rearrange("p (g r) -> p g r", r=16),
                                            FB[n][:, :].rearrange("p (g r) -> p g r", r=16),
                                            bc(m8[:, :], [32], [1]), ALU.mult)
                step(ins)
                step(eng.tensor_reduce(ctx_a[:, :], z_a[:, :].rearrange("p (g r) -> p g r", r=16), AX.X, ALU.add))
                for b in range(2):
                    r = slice(b * C, b * C + C)
                    ins = eng.tensor_scalar(ctx_bd[r, r], ctx_a[r, :], bv2[r, 0:1], None, ALU.add)
                ins.then_inc(s_ctx, 1)
                yield
                eng.wait_ge(s_tok, p + 1)
                step(eng.tensor_tensor(h_f[:, :], FB[2][:, 0:C], bo_r[:, :], ALU.add))
                step((yield from norm(1, xn_f[:, :], h_f[:, :])))
                step((yield from norm(2, hh[:, :], xn_f[:, :])))
                step(eng.tensor_tensor(hh[:, :], hh[:, :], ln1g[:, :], ALU.mult))
                eng.tensor_tensor(hh[:, :], hh[:, :], ln1b[:, :], ALU.add).then_inc(s_hh, 1)
                yield
                eng.wait_ge(s_qkv, p + 1)
                eng.tensor_scalar(q1[:, :], FB[0][0:C, 0:P], b_qk[:, 0:1], None, ALU.add)
                eng.tensor_scalar(k1[:, :], FB[0][0:C, P:2 * P], b_qk[:, 1:2], None, ALU.add)
                eng.tensor_tensor(v1[:, :], FB[0][:, 2 * P:2 * P + C], b_v[:, :], ALU.add).then_inc(s_qkvc, 1)
                yield
                eng.wait_ge(s_s1, p + 1)
                step(eng.tensor_tensor(s1[:, :], FB[1][:, 0:P], rel_bias[:, :], ALU.add))
                eng.tensor_reduce(max1[:, :], s1[:, :], AX.X, ALU.max, negate=True).then_inc(s_m1, 1)
                yield
                eng.wait_ge(s_e1, p + 1)
                step(eng.reciprocal(sum1[:, :], sum1[:, :]))
                eng.tensor_scalar(p1[:, :], p1[:, :], sum1[:, 0:1], scale1[:, 0:1], ALU.mult, ALU.mult).then_inc(s_p1, 1)
                yield
                yield
                eng.wait_ge(s_pr, p + 1)
                step(eng.tensor_tensor(o1[:, :], FB[0][:, 0:C], b_proj[:, :], ALU.add))
                step((yield from norm(3, o1[:, :], o1[:, :])))
                step(eng.tensor_tensor(o1[:, :], o1[:, :], ln2g[:, :], ALU.mult))
                step(eng.tensor_tensor(o1[:, :], o1[:, :], ln2b[:, :], ALU.add))
                step(eng.tensor_tensor(h_f[:, :], h_f[:, :], o1[:, :], ALU.add))
                (yield from norm(4, xn_f[:, :], h_f[:, :])).then_inc(s_xc, 1)
                yield
                yield
                eng.wait_ge(s_simc, 2 * p + 2)
                eng.nop(nofuse=True)
                tops = [(top[:, g // 8, g % 8, :], topi_u[:, g // 8, g % 8, :], sim[:, g, :], sim_b[:, g, :])
                        for g in range(16)]
                yield
                best(step, tops)
                yield
                step(eng.tensor_copy(topi[:, :, :, :], topi_u[:, :, :, :]))
                i0, i1 = (topi[:, n, :, :].rearrange("p h j -> p (h j)") for n in range(2))
                step(eng.scalar_tensor_tensor(i1, i1, float(NKEY), head_off[:, :], ALU.mult, ALU.add))
                for runs, pairs_of in ((RUNS, ((cand, top), (candi, topi))), (RUNS8, ((candi8, topi),))):
                    lo = 0
                    for first, na, nb in runs:
                        for o, v in pairs_of:
                            ins = eng.tensor_tensor(
                                o[:, :, lo:lo + na * nb].rearrange("p h (a b) -> p h a b", a=na),
                                bc(v[:, 0, :, first:first + na], [nb], [3]), bc(v[:, 1, :, 0:nb], [na], [2]), ALU.add)
                        lo += na * nb
                step(ins, apart=True)
                yield
                best(step, [(fin[:, h, :], pos_u[:, h, :], cand[:, h, :], cand_b[:, h, :]) for h in range(NH)])
                step(eng.tensor_copy(pos[:, :, :], pos_u[:, :, :]))
                step(eng.tensor_copy(fsum[:, :], fin[:, :, 0]))
                eng.tensor_tensor(fin[:, :, :], fin[:, :, :], bc(fsum[:, :], [TOPK], [2]), ALU.subtract)\
                   .then_inc(s_fm, 1)
                yield
                lookups = [(h, 4, 0, NC8, pos20, candi8) for h in (0, 4)] + \
                          [(h, 2, 8, NC, pos50, candi) for h in (0, 2, 4, 6)]
                for h, n, j, nc_, places_of, rows_of in lookups:
                    o = hot[:, 0:n * 8 * nc_].rearrange("p (h j c) -> p h j c", h=n, c=nc_)
                    step(eng.tensor_tensor(o, bc(pos[:, h:h + n, j:j + 8], [nc_], [3]),
                                           bc(places_of[:, :], [n, 8], [1, 2]), ALU.is_equal))
                    step(eng.tensor_tensor(o, o, bc(rows_of[:, h:h + n, :], [8], [2]), ALU.mult))
                    step(eng.tensor_reduce(fidx[:, :].rearrange("p (h j) -> p h j", h=NH)[:, h:h + n, j:j + 8], o,
                                           AX.X, ALU.add))
                    if h == 0 and j:
                        yield
                eng.wait_ge(s_fe, p + 1)
                step(eng.tensor_reduce(fsum[:, :], fexp[:, :, :], AX.X, ALU.add))
                step(eng.reciprocal(fsum[:, :], fsum[:, :]))
                eng.tensor_tensor(fexp[:, :, :], fexp[:, :, :], bc(fsum[:, :], [TOPK], [2]), ALU.mult).then_inc(s_fw, 1)
                eng.wait_ge(s_ft, p + 1)
                eng.wait_ge(s_idxl, p)
                eng.tensor_copy(idx_stage[:, :], FB[2][:, 0:P]).then_inc(s_idx, 1)
                eng.wait_ge(s_wl, p)
                eng.tensor_copy(w_mid[:, :], FB[3][:, 0:P]).then_inc(s_front, 1)
                step.end()

            def best(step, rows):
                for o, oi, v, w in rows:
                    ins = eng.max(o[:, 0:8], v)
                step(ins, apart=True)
                for o, oi, v, w in rows:
                    eng.max_index(oi[:, 0:8], o[:, 0:8], v)
                    ins = eng.match_replace(w, o[:, 0:8], v, LOWEST)
                step(ins, apart=True)
                for o, oi, v, w in rows:
                    ins = eng.max(o[:, 8:16], w)
                step(ins, apart=True)
                for o, oi, v, w in rows:
                    ins = eng.max_index(oi[:, 8:16], o[:, 8:16], w)
                step(ins)

            def rows(p):
                for _ in range(3):
                    yield
                eng.wait_ge(s_gu, CHUNKS * (p + 1))
                eng.wait_ge(s_front, p + 1)
                eng.tensor_tensor(w_live[:, :, :], bc(w_mid[:, :], [NH], [2]), bc(m16[:, :], [P], [1]), ALU.mult)\
                   .then_inc(s_wl, 1)

            def keep(n):
                eng.tensor_copy(h_mid[:, :], h_f[:, :])
                eng.tensor_copy(xcT_mid[:, :], xcT[:, :]).then_inc(s_keep, 1)
                eng.wait_ge(s_keep, n)

            def carry(p):
                eng.wait_ge(s_out, p)
                eng.tensor_copy(h_b[:, :], h_mid[:, :])
                eng.tensor_copy(xcT_b[:, :], xcT_mid[:, :]).then_inc(s_rot, 1)
                eng.wait_ge(s_rot, p + 1)

            def back(p):
                step = Steps(eng, n_back, BACK_STEPS, p)

                def norm(k, o, i):
                    return normalize(step, p, k, 3, o, i, stats_b, mv_b, std_b, s_varb, s_stdb)

                yield
                sv = s2[:, :].rearrange("p (h x) -> p h x", h=NH)
                for n in range(2):
                    eng.wait_ge(s_s2, 2 * p + n + 1)
                    eng.tensor_reduce(max2[:, 4 * n:4 * n + 4], BB[2 + n][:, :].rearrange("p (h x) -> p h x", h=4),
                                      AX.X, ALU.max, negate=True).then_inc(s_m2, 1)
                yield
                eng.wait_ge(s_e2, p + 1)
                step(eng.reciprocal(sum2[:, :], sum2[:, :]))
                eng.tensor_tensor(sv, sv, bc(sum2[:, :], [P], [2]), ALU.mult).then_inc(s_p2, 1)
                yield
                yield
                eng.wait_ge(s_wo, p + 1)
                step(eng.tensor_tensor(h_b[:, :], h_b[:, :], BB[1][:, 0:C], ALU.add))
                (yield from norm(1, xn_b[:, :], h_b[:, :])).then_inc(s_xb, 1)
                yield
                eng.wait_ge(s_qkvg, p + 1)
                eng.tensor_tensor(g3[:, :], BB[1][:, 0:256], b_g3[:, :], ALU.add).then_inc(s_g3e, 1)
                ins = eng.tensor_tensor(k_exp[:, 0, :, :], bc(BB[2][:, 256:384], [NH], [1]), bc(m16[:, :], [P], [2]),
                                        ALU.mult)
                ins.then_inc(s_k3, 1)
                yield
                for n in range(4):
                    eng.wait_ge(s_s3, 4 * p + n + 1)
                    eng.tensor_reduce(max3[:, 4 * n:4 * n + 4], BB[n][:, :].rearrange("p (h x) -> p h x", h=4),
                                      AX.X, ALU.max, negate=True).then_inc(s_m3, 1)
                yield
                eng.wait_ge(s_e3, p + 1)
                step(eng.reciprocal(sum3[:, :], sum3[:, :]))
                se = sum3[:, :].rearrange("p (h e) -> p h e", e=2)
                step(eng.tensor_scalar(se[:, :, 1], se[:, :, 1], neg_lam[:, 0:1], None, ALU.mult))
                s3v = s3.rearrange("p (h e) x -> p h e x", e=2)
                eng.tensor_tensor(a3, s3v[:, :, 0, :], bc(se[:, :, 0], [P], [2]), ALU.mult)
                step(eng.tensor_tensor(a3b, s3v[:, :, 1, :], bc(se[:, :, 1], [P], [2]), ALU.mult))
                eng.tensor_tensor(a3, a3, a3b, ALU.add).then_inc(s_a3, 1)
                yield
                eng.wait_ge(s_o3, p + 1)
                ov = BB[2][:, 0:256].rearrange("p (h d) -> p h d", d=D3)
                step(eng.tensor_reduce(mean3[:, :], ov, AX.X, ALU.add))
                step(eng.tensor_scalar(mean3[:, :], mean3[:, :], 1.0 / D3, None, ALU.mult))
                step(eng.tensor_tensor(o3[:, :, :], ov, bc(mean3[:, :], [D3], [2]), ALU.subtract))
                step(eng.tensor_tensor(sq3[:, :, :], o3[:, :, :], o3[:, :, :], ALU.mult))
                eng.tensor_reduce(mean3[:, :], sq3[:, :, :], AX.X, ALU.add).then_inc(s_varb, 1)
                yield
                eng.wait_ge(s_stdb, 3 * p + 2)
                step(eng.reciprocal(std_b[:, :], std_b[:, :]))
                step(eng.tensor_tensor(o3[:, :, :], o3[:, :, :], bc(std_b[:, :], [D3], [2]), ALU.mult))
                step(eng.tensor_tensor(o3[:, :, :], o3[:, :, :], bc(gam3[:, :], [8], [1]), ALU.mult))
                step(eng.tensor_tensor(o3[:, :, :], o3[:, :, :], bc(bet3[:, :], [8], [1]), ALU.add))
                eng.wait_ge(s_g3x, p + 1)
                step(eng.tensor_scalar(g3[:, :], g3[:, :], 1.0, None, ALU.add))
                step(eng.reciprocal(g3[:, :], g3[:, :]))
                o3r = o3[:, :, :].rearrange("p h d -> p (h d)")
                eng.scalar_tensor_tensor(o3r, o3r, 1.0 - LAMBDA_INIT, g3[:, :], ALU.mult, ALU.mult).then_inc(s_o3g, 1)
                yield
                eng.wait_ge(s_pr3, p + 1)
                step(eng.tensor_tensor(h_b[:, :], h_b[:, :], BB[0][:, 0:C], ALU.add))
                step(eng.tensor_tensor(h_b[:, :], h_b[:, :], b_out3[:, :], ALU.add))
                (yield from norm(3, xn_b[:, :], h_b[:, :])).then_inc(s_xb, 1)
                yield
                eng.wait_ge(s_ff1, p + 1)
                for m in range(2):
                    ins = eng.tensor_scalar(z1[:, m * P:(m + 1) * P], BB[2][:, m * P:(m + 1) * P], b1c[:, m:m + 1],
                                            None, ALU.add)
                step(ins)
                step(eng.tensor_tensor(z1b[:, :], z1[:, :], z1[:, :], ALU.mult))
                step(eng.tensor_scalar(z1b[:, :], z1b[:, :], 0.044715, 1.0, ALU.mult, ALU.add))
                step(eng.tensor_tensor(z1b[:, :], z1b[:, :], z1[:, :], ALU.mult))
                eng.tensor_scalar(z1b[:, :], z1b[:, :], -54.0, None, ALU.max).then_inc(s_ge, 1)
                yield
                step(eng.tensor_scalar(wrow[:, :], BB[3][:, 0:P], br_c[:, 0:1], None, ALU.add))
                step(eng.tensor_tensor(wcmp[:, :], wrow[:, :], ident[:, :], ALU.mult))
                step(eng.tensor_reduce(wcol[:, :], wcmp[:, :], AX.X, ALU.add))
                step(eng.scalar_tensor_tensor(wcmp[:, :], wrow[:, :], wcol[:, 0:1], same01[:, :], ALU.is_gt, ALU.mult))
                step(eng.tensor_reduce(rank2[:, 0:1], wcmp[:, :], AX.X, ALU.add))
                step(eng.scalar_tensor_tensor(wcmp[:, :], wrow[:, :], wcol[:, 0:1], before01[:, :], ALU.is_equal, ALU.mult))
                step(eng.tensor_reduce(rank2[:, 1:2], wcmp[:, :], AX.X, ALU.add))
                step(eng.tensor_tensor(factor[:, :], rank2[:, 0:1], rank2[:, 1:2], ALU.add))
                step(eng.scalar_tensor_tensor(factor[:, :], factor[:, :], float(KEEP), wcol[:, :], ALU.is_lt, ALU.mult))
                eng.wait_ge(s_gx, p + 1)
                step(eng.tensor_scalar(z1b[:, :], z1b[:, :], 1.0, None, ALU.add))
                step(eng.reciprocal(z1b[:, :], z1b[:, :]))
                eng.tensor_tensor(z1[:, :], z1[:, :], z1b[:, :], ALU.mult).then_inc(s_gl, 1)
                yield
                eng.wait_ge(s_ff2, p + 1)
                step(eng.tensor_tensor(y_o[:, :], BB[0][:, 0:C], b2r[:, :], ALU.add))
                step(eng.scalar_tensor_tensor(y_o[:, :], y_o[:, :], factor[:, 0:1], xn_b[:, :], ALU.mult, ALU.add))
                eng.wait_ge(s_st, 16 * p)
                eng.tensor_tensor(out_sb[:, :], y_o[:, :], h_b[:, :], ALU.add).then_inc(s_out, 1)
                step.end()

            eng.memset(q_bd[:, :], 0.0)
            eng.memset(ctx_bd[:, :], 0.0).then_inc(s_zero, 1)
            eng.wait_ge(s_zero, 1)
            eng.wait_ge(s_cf, 16)
            step = Steps(eng, n_setup, SETUP_STEPS, 0)
            step(eng.tensor_tensor(rel_bias[:, :], rel_bias[:, :], same_neg[:, :], ALU.add))
            in_turns(front(0))
            keep(1)
            eng.tensor_copy(ident_b[:, :], ident[:, :])
            eng.tensor_copy(same_b[:, :], same_neg[:, :])
            eng.wait_ge(s_cb, 16)
            eng.tensor_copy(causal_b[:, :], causal_neg[:, :])
            step(eng.tensor_tensor(lprod[:, :, :], lqk[:, 0:2, :], lqk[:, 2:4, :], ALU.mult))
            eng.tensor_reduce(lsum[:, :], lprod[:, :, :], AX.X, ALU.add).then_inc(s_lam, 1)
            eng.wait_ge(s_lame, 1)
            step(eng.tensor_tensor(neg_lam[:, :], lexp[:, 1:2], lexp[:, 0:1], ALU.subtract))
            step(eng.tensor_scalar(neg_lam[:, :], neg_lam[:, :], -LAMBDA_INIT, None, ALU.add))
            step.end()
            in_turns(front(1), rows(0))
            carry(0)
            keep(2)
            with eng.Fori(1, pairs - 1) as i:
                in_turns(front(i + 1), back(i - 1), rows(i))
                carry(i)
                keep(i + 2)
            in_turns(back(pairs - 2), rows(pairs - 1))
            carry(pairs - 1)
            in_turns(back(pairs - 1))


SETUP_STEPS = 4
FRONT_STEPS = 57
BACK_STEPS = 38

_OUT = ((16, 64, 64), "float32")


def packed_columns(v):
    import numpy as np

    def diag(w, n=2):
        o = np.zeros((n * w.shape[0], n * w.shape[1]), np.float32)
        for b in range(n):
            o[b * w.shape[0]:(b + 1) * w.shape[0], b * w.shape[1]:(b + 1) * w.shape[1]] = w
        return o

    def row(w):
        return np.broadcast_to(np.reshape(w, (1, -1)), (P, np.size(w)))

    def split(w, n):
        return np.concatenate(np.split(w, n, axis=0), axis=1)

    part, cols = np.arange(P)[:, None], np.arange(P)[None, :]
    same = part // N == cols // N
    ml = np.zeros((P, 1024), np.float32)
    mr = np.zeros((P, P), np.float32)
    odd = np.arange(1024) // 16 % 2
    ml[1], ml[2] = odd == 0, odd == 1
    mr[0] = 1.0
    mr[1], mr[2] = np.where(np.arange(P) >= N, NEG, 0.0), np.where(np.arange(P) < N, NEG, 0.0)
    rel = np.stack([v["L0_attn_bias_table"][N - 1 - n:2 * N - 1 - n] for n in range(N)])
    keys = v["L0_ffn_pk_keys"]
    bd = np.concatenate([diag4([keys[m // 2, :, 4 * (m % 2) + h, :].T for h in range(4)]) for m in range(4)], axis=1)
    b = v["L0_attn_qkv_b"]
    at = np.cumsum([0] + [nb for _, na, nb in RUNS for _ in range(na)])
    return {
        "ident": np.eye(P), "ident2": np.concatenate([np.eye(C)] * 2), "m8": part // 8 == np.arange(16),
        "m16": part // 16 == np.arange(8), "same_neg": np.where(same, 0.0, NEG),
        "rel_bias": np.tile(rel, (2, 2)), "mask_l": ml, "mask_r": mr, "pos50": row(np.arange(NC)),
        "pos20": row(np.concatenate([at[a] + np.arange(nb) for first, na, nb in RUNS8 for a in range(first, first + na)])),
        "head_off": row(np.repeat(np.arange(NH) * NKV, TOPK)), "eps": np.full((P, 1), EPS),
        "wqT": diag(v["L0_tok_Wq"].T), "wk_bd": diag(v["L0_tok_Wk"]), "wvT": diag(v["L0_tok_Wv"].T),
        "woT2": np.tile(v["L0_tok_Wo"].T, (2, 1)), "bq2": np.tile(v["L0_tok_bq"], 2)[:, None],
        "bk2": np.tile(v["L0_tok_bk"], 2)[:, None], "bv2": np.tile(v["L0_tok_bv"], 2)[:, None],
        "bo_r": row(v["L0_tok_bo"]), "ln1g": row(v["L0_attn_ln1_g"]), "ln1b": row(v["L0_attn_ln1_b"]),
        "ln2g": row(v["L0_attn_ln2_g"]), "ln2b": row(v["L0_attn_ln2_b"]), "w_qkv": v["L0_attn_qkv_w"],
        "b_qk": np.stack([b[0:C], b[C:2 * C]], axis=1), "b_v": row(b[2 * C:]), "scale1": row(v["L0_attn_scale"]),
        "w_proj": v["L0_attn_proj_w"], "b_proj": row(v["L0_attn_proj_b"]), "w_pk": v["L0_ffn_Wq_pk"], "keys_bd": bd,
        "same01": same, "before01": same & (cols < part), "causal_neg": np.where(same & (cols <= part), 0.0, NEG),
        "w_q2": v["L0_ffn_Wq"], "w_o2": split(v["L0_ffn_Wo"], 4), "w_q3": v["L1_attn_Wq"], "w_kv3": v["L1_attn_Wkv"],
        "w_g3": v["L1_attn_Wg"], "w_out3": split(v["L1_attn_Wout"], 2), "b_out3": row(v["L1_attn_bout"]),
        "b_g3": row(v["L1_attn_bg"]), "gam3": row(v["L1_attn_ln_gamma"]), "bet3": row(v["L1_attn_ln_beta"]),
        "lqk": row(np.concatenate([v["L1_attn_" + n] for n in ("lq1", "lq2", "lk1", "lk2")])),
        "wr_bc": np.broadcast_to(v["L1_ffn_wr"], (C, P)), "br_c": row(v["L1_ffn_br"]), "w1": v["L1_ffn_w1"],
        "b1c": v["L1_ffn_b1"].reshape(2, P).T, "w2": split(v["L1_ffn_w2"], 2), "b2r": row(v["L1_ffn_b2"]),
    }


def diag4(blocks):
    import numpy as np

    o = np.zeros((P, 4 * NKEY), np.float32)
    for h, w in enumerate(blocks):
        o[32 * h:32 * h + 32, h * NKEY:(h + 1) * NKEY] = w
    return o


def kernel(**inputs):
    import numpy as _np
    import concourse.bacc as _bacc
    from concourse import mybir as _mybir
    from concourse.bass_utils import run_bass_kernel_spmd as _run

    v = {name: _np.asarray(value) for name, value in inputs.items()}
    at, _ = places()
    packed = _np.zeros((P, sum(n for _, n in at.values())), _np.float32)
    for name, value in packed_columns(v).items():
        lo, n = at[name]
        assert value.shape[1] == n, name
        packed[0:value.shape[0], lo:lo + n] = value
    x = v["x"].reshape(-1, 2, C, GW, GS, GW, GS)
    pairs = x.shape[0]
    arrays = {
        "packed": packed,
        "xw": _np.ascontiguousarray(x.transpose(0, 1, 2, 3, 5, 4, 6)).reshape(pairs * P, 4096),
        "xT": _np.ascontiguousarray(x.reshape(pairs, 2, C, GW, GS, 4, 2, GS).transpose(0, 6, 4, 7, 3, 5, 1, 2))
        .reshape(pairs * P, 4096),
        "table": _np.concatenate([v["L0_ffn_keys_table"], v["L0_ffn_values_table"]], axis=1),
    }
    nc = _bacc.Bacc("TRN2", target_bir_lowering=False, num_devices=1)
    aps = {name: nc.dram_tensor(f"in_{name}", w.shape, _mybir.dt.from_np(w.dtype), kind="ExternalInput").ap()
           for name, w in arrays.items()}
    out = nc.dram_tensor("out_h", _OUT[0], _mybir.dt.from_np(_np.dtype(_OUT[1])), kind="ExternalOutput").ap()
    vit_tower_kernel(nc, aps, out)
    r = _run(nc, [{f"in_{name}": w for name, w in arrays.items()}], core_ids=[0])
    return r.results[0]["out_h"]
```

```python
from contextlib import ExitStack

import concourse.bass as bass
from concourse import mybir

F32 = mybir.dt.float32
BF16 = mybir.dt.bfloat16
U32 = mybir.dt.uint32
ALU = mybir.AluOpType
ACT = mybir.ActivationFunctionType
AX = mybir.AxisListType

P = 128
C = 64
N = 64
GS = 8
GW = 8
NH = 8
TOPK = 16
NKEY = 64
NKV = NKEY * NKEY
H3 = 16
D3 = 32
HID = 256
KEEP = N // 2 - 1
EPS = 1e-5
NEG = -1e30
LOWEST = -3.0e38
EXP_AT = 7
TURN_AT = 13
HALF = P // 2
TPAD = 3 * NH
TW = NH + TPAD
PACE = (2, 3, 2, 2, 2, 0, 2, 2)
ROWS_AT = (4, 6, 8, 10, 13, 16, 19)
ROWS_AT_0 = (5, 8, 11, 14, 18, 20, 22)
LAMBDA_INIT = 0.8 - 0.6 * 2.718281828459045 ** (-0.3)
GELU_C = 2.0 * 0.7978845608028654
RUNS = [(0, 1, 16), (1, 1, 8), (2, 1, 5), (3, 1, 4), (4, 1, 3), (5, 3, 2), (8, 8, 1)]
RUNS8 = [(0, 1, 8), (1, 1, 4), (2, 2, 2), (4, 4, 1)]
NC8 = sum(na * nb for _, na, nb in RUNS8)
NC = sum(na * nb for _, na, nb in RUNS)
CHUNKS = 8
TC = P // CHUNKS

FIRST = [("m8", 16), ("wqT", P), ("bq2", 1), ("wk_bd", P), ("bk2", 1), ("mask_l", 1024), ("mask_r", P),
         ("ident", P), ("wvT", P), ("bv2", 1), ("woT2", C), ("ident2", C), ("bo_r", C), ("eps", 1)]
SECOND = [("m16", 8), ("same_neg", P), ("rel_bias", P), ("pos20", NC8), ("pos50", NC), ("head_off", NH * TOPK),
          ("ln1g", C), ("ln1b", C), ("ln2g", C), ("ln2b", C), ("w_qkv", 3 * C), ("b_qk", 2), ("b_v", C),
          ("scale1", 1), ("w_proj", C), ("b_proj", C), ("w_pk", 512), ("keys_bd", 1024)]
REST = [("same01", P), ("before01", P), ("causal_neg", P), ("w_q2", 512), ("w_o2", 256), ("w_q3", 256),
        ("w_kv3", 512), ("w_g3", 256), ("w_out3", 2 * C), ("b_out3", C), ("b_g3", 256), ("gam3", D3),
        ("bet3", D3), ("lqk", 64), ("wr_bc", P), ("br_c", 1), ("w1", HID), ("b1c", 2), ("w2", 2 * C), ("b2r", C)]


def places():
    at, starts, lo = {}, [], 0
    for group in (FIRST, SECOND, REST):
        starts.append(lo)
        for name, n in group:
            at[name] = (lo, n)
            lo += n
    return at, starts + [lo]


class Steps:

    def __init__(self, eng, sem, n, p):
        self.eng, self.sem, self.n, self.base, self.k = eng, sem, n, p * n, 0

    def __call__(self, ins, apart=False):
        self.k += 1
        ins.then_inc(self.sem, 1)
        self.eng.wait_ge(self.sem, self.base + self.k)
        if apart:
            self.eng.nop(nofuse=True)

    def end(self):
        assert self.k == self.n, (self.k, self.n)


def vit_tower_kernel(nc, a, out):
    pairs = a["xw"].shape[0] // P
    with ExitStack() as ctx:
        def sb(name, shape, dt=F32):
            return ctx.enter_context(nc.sbuf_tensor(name, shape, dt))

        def sem(name):
            return ctx.enter_context(nc.semaphore(name))

        packed = sb("packed", [P, a["packed"].shape[1]])
        at, starts = places()

        def part(name, rows=P):
            lo, n = at[name]
            return packed[0:rows, lo:lo + n]

        ident, ident2, m8, m16 = part("ident"), part("ident2"), part("m8"), part("m16")
        same01, before01 = part("same01"), part("before01")
        same_neg, causal_neg = part("same_neg"), part("causal_neg")
        rel_bias, mask_l, mask_r = part("rel_bias"), part("mask_l"), part("mask_r")
        pos20, pos50, head_off, eps = part("pos20"), part("pos50"), part("head_off"), part("eps")
        wqT, wk_bd, wvT, woT2 = part("wqT"), part("wk_bd"), part("wvT"), part("woT2")
        bq2, bk2, bv2, bo_r = part("bq2"), part("bk2"), part("bv2"), part("bo_r")
        ln1g, ln1b, ln2g, ln2b = part("ln1g"), part("ln1b"), part("ln2g"), part("ln2b")
        w_qkv, b_qk, b_v, scale1 = part("w_qkv", C), part("b_qk", C), part("b_v"), part("scale1")
        w_proj, b_proj = part("w_proj", C), part("b_proj")
        w_pk, keys_bd = part("w_pk", C), part("keys_bd").rearrange("p (m x) -> p m x", m=4)
        w_q2, w_o2 = part("w_q2", C), part("w_o2").rearrange("p (m x) -> p m x", m=4)
        w_q3, w_kv3, w_g3 = part("w_q3", C), part("w_kv3", C), part("w_g3", C)
        w_out3, b_out3 = part("w_out3").rearrange("p (m x) -> p m x", m=2), part("b_out3")
        b_g3, gam3, bet3 = part("b_g3"), part("gam3"), part("bet3")
        lqk = part("lqk").rearrange("p (n x) -> p n x", n=4)
        wr_bc, br_c, w1, b1c = part("wr_bc", C), part("br_c"), part("w1", C), part("b1c")
        w2, b2r = part("w2").rearrange("p (m x) -> p m x", m=2), part("b2r")
        ident_b = sb("ident_b", [P, P], BF16)
        same_b = sb("same_b", [P, P], BF16)
        causal_b = sb("causal_b", [P, P], BF16)
        lprod = sb("lprod", [P, 2, 16])
        lsum = sb("lsum", [P, 2])
        lexp = sb("lexp", [P, 2])
        neg_lam = sb("neg_lam", [P, 1])

        xw = sb("xw", [P, 4096])
        xT = sb("xT", [P, GW, 512])
        qsum = sb("qsum", [P, N])
        qT = sb("qT", [P, N])
        q_bd = sb("q_bd", [P, P])
        qp = sb("qp", [P, N])
        q_exp = sb("q_exp", [P, 1024])
        qk = sb("qk", [P, 1024])
        max_a = sb("max_a", [P, 8])
        sum_a = sb("sum_a", [P, 8])
        prob_a = sb("prob_a", [P, 1024])
        probT_a = sb("probT_a", [P, 1024])
        y_a = prob_a
        z_a = q_exp
        ctx_a = sb("ctx_a", [P, N])
        ctx_bd = sb("ctx_bd", [P, P])
        h_f = sb("h_f", [P, C])
        stats_f = sb("stats_f", [P, 6])
        mv_f = sb("mv_f", [P, 2])
        std_f = sb("std_f", [P, 1])
        xn_f = sb("xn_f", [P, C])
        hh = sb("hh", [P, C])
        hhT = sb("hhT", [C, P])
        q1 = sb("q1", [C, P])
        k1 = sb("k1", [C, P])
        v1 = sb("v1", [P, C])
        s1 = sb("s1", [P, P])
        max1 = sb("max1", [P, 1])
        sum1 = sb("sum1", [P, 1])
        p1 = s1
        p1T = sb("p1T", [P, P])
        o1T = q1
        o1 = sb("o1", [P, C])
        xcT = sb("xcT", [C, P])
        qpkT = q_exp[:, 0:512]
        sims = sb("sims", [P, 1024])
        sims_b = sb("sims_b", [P, 1024])
        sim, sim_b = (t[:, :].rearrange("p (g k) -> p g k", k=NKEY) for t in (sims, sims_b))
        top = sb("top", [P, 2, NH, TOPK])
        topi_u = sb("topi_u", [P, 2, NH, TOPK], U32)
        topi = sb("topi", [P, 2, NH, TOPK])
        cand, candi, cand_b = (t[:, lo:lo + NH * NC].rearrange("p (h c) -> p h c", c=NC)
                               for t, lo in ((sims_b, 0), (sims_b, 512), (sims, 0)))
        fin = sb("fin", [P, NH, TOPK])
        pos_u = sb("pos_u", [P, NH, TOPK], U32)
        pos = sb("pos", [P, NH, TOPK])
        candi8 = sb("candi8", [P, NH, NC8])
        hot = sims
        fidx = sb("fidx", [P, NH * TOPK])
        fexp = sb("fexp", [P, NH, TOPK])
        fsum = sb("fsum", [P, NH])
        idx_stage = sb("idx_stage", [P, P], U32)
        h_next = sb("h_next", [P, C])
        xcT_next = sb("xcT_next", [C, P])
        h_mid = sb("h_mid", [P, C])
        xcT_mid = sb("xcT_mid", [C, P])
        w_mid = sb("w_mid", [P, P])
        idx_live = sb("idx_live", [P, 2, P], U32)
        w_next = sb("w_next", [P, P])
        w_live = sb("w_live", [P, TPAD + HALF * TW])
        xcT_b = sb("xcT_b", [C, P])
        h_b = sb("h_b", [P, C])
        gath = sb("gath", [P, P, 2 * C])
        kv = sb("kv", [P, P, NH])
        v2 = sb("v2", [P, NH, C])
        sp2 = sb("sp2", [P, 2048])
        s2, p2T = sp2[:, 0:1024], sp2[:, 1024:2048]
        max2 = sb("max2", [P, 8])
        sum2 = sb("sum2", [P, 8])
        o2T = sb("o2T", [P, 512])
        stats_b = sb("stats_b", [P, 6])
        mv_b = sb("mv_b", [P, 2])
        std_b = sb("std_b", [P, 8])
        xn_b = sb("xn_b", [P, C])
        xbT = sb("xbT", [C, P])
        q3T = sb("q3T", [P, 256])
        v3 = sb("v3", [P, 256])
        g3 = sb("g3", [P, 256])
        k_exp = sb("k_exp", [P, 2, NH, P])
        qc = k_exp[0:C, 0, :, :].rearrange("p h x -> p (h x)")
        sums_sb = prob_a[:, 0:512]
        table_seed = sb("table_seed", [P, 1])
        s3 = sp2[:, :].rearrange("p (h x) -> p h x", x=P)
        max3 = sb("max3", [P, H3])
        sum3 = sb("sum3", [P, H3])
        rec3 = sb("rec3", [P, H3])
        fac3 = sb("fac3", [P, 8])
        a3 = k_exp[:, 0]
        a3T = sp2[:, 0:1024]
        o3 = sb("o3", [P, 8, D3])
        sq3 = sb("sq3", [P, 8, D3])
        mean3 = sb("mean3", [P, 8])
        o3T = v3
        z1 = q3T
        z1b = g3
        wrow, wcmp = (sq3[:, 4 * n:4 * n + 4, :].rearrange("p h d -> p (h d)") for n in range(2))
        wcol = sb("wcol", [P, 1])
        rank2 = sb("rank2", [P, 2])
        factor = sb("factor", [P, 1])
        y_o = o3[:, 0:2, :].rearrange("p h d -> p (h d)")
        out_sb = sb("out_sb", [P, C])

        FB = [ctx.enter_context(nc.psum_tensor(f"front{n}", [P, 512], F32)) for n in range(4)]
        BB = [ctx.enter_context(nc.psum_tensor(f"back{n}", [P, 512], F32)) for n in range(3)]
        sums = ctx.enter_context(nc.psum_tensor("sums", [P, 512], F32))

        s_x = [sem(f"x_loaded{n}") for n in range(2)]
        s_cf = sem("constants_loaded_for_front")
        s_cs = sem("constants_loaded_for_attention")
        s_cb = sem("constants_loaded_for_rest")
        s_zero = sem("zeros_set")
        s_lam = sem("lambda_sums")
        s_lame = sem("lambda_exps")
        n_setup = sem("setup_steps")
        n_front = sem("front_steps")
        s_xt = sem("x_turned_loaded")
        s_mean = sem("window_means")
        s_qp = sem("pool_queries")
        s_qexp = sem("pool_queries_spread")
        s_qk = sem("pool_query_keys")
        s_qkc = sem("pool_query_keys_copied")
        s_qkb = sem("pool_key_bias")
        s_qkbc = sem("pool_key_bias_copied")
        s_sa = sem("pool_scores")
        s_ma = sem("pool_maxima")
        s_ea = sem("pool_exps")
        s_pa = sem("pool_probs")
        s_pta = sem("pool_probs_turned")
        s_ptac = sem("pool_probs_turned_copied")
        s_ya = sem("pool_sums")
        s_yac = sem("pool_sums_copied")
        s_za = sem("pool_values")
        s_ctx = sem("pool_context")
        s_tok = sem("tokens")
        s_varf = sem("front_variances")
        s_stdf = sem("front_deviations")
        s_hh = sem("attn_input")
        s_hht = sem("attn_input_turned")
        s_hhtc = sem("attn_input_turned_copied")
        s_qkv = sem("attn_qkv")
        s_qkvc = sem("attn_qkv_copied")
        s_s1 = sem("attn_scores")
        s_m1 = sem("attn_maxima")
        s_e1 = sem("attn_exps")
        s_p1 = sem("attn_probs")
        s_p1t = sem("attn_probs_turned")
        s_p1tc = sem("attn_probs_turned_copied")
        s_o1 = sem("attn_out")
        s_o1c = sem("attn_out_copied")
        s_pr = sem("attn_projected")
        s_xc = sem("memory_input")
        s_xct = sem("memory_input_turned")
        s_xctc = sem("memory_input_turned_copied")
        s_qc = sem("memory_queries")
        s_qcc = sem("memory_queries_copied")
        s_sim = sem("key_scores")
        s_simc = sem("key_scores_copied")
        n_search = sem("search_steps")
        s_fm = sem("picks_found")
        s_fe = sem("picks_exps")
        s_fw = sem("pick_weights")
        s_ft = sem("picks_turned")
        s_idx = sem("pick_indices")
        s_search = sem("search_done")
        s_idxl = sem("indices_taken")
        s_g = [[sem(f"rows_fetched{c}_{half}") for half in range(2)] for c in range(CHUNKS)]
        s_gu = sem("row_parts_free")
        s_wm = sem("pick_weights_passed_on")
        s_wl = sem("pick_weights_spread")
        s_sc = sem("sums_copied")
        s_st2 = sem("sums_turned")
        s_rot = sem("carried_over")
        s_keep = sem("kept_for_later")
        s_shift = sem("shifted_on")
        n_back = sem("back_steps")
        s_kvc = sem("keys_values_copied")
        s_qb = sem("memory_queries_made")
        s_qbc = sem("memory_queries_scaled")
        s_s2 = sem("memory_scores")
        s_vt = sem("memory_values_turned")
        s_vtc = sem("memory_values_turned_copied")
        s_m2 = sem("memory_maxima")
        s_e2 = sem("memory_exps")
        s_p2 = sem("memory_probs")
        s_p2t = sem("memory_probs_turned")
        s_p2tc = sem("memory_probs_turned_copied")
        s_o2 = sem("memory_out")
        s_o2c = sem("memory_out_copied")
        s_wo = sem("memory_projected")
        s_varb = sem("back_variances")
        s_stdb = sem("back_deviations")
        s_xb = sem("back_input")
        s_xbt = sem("back_input_turned")
        s_xbtc = sem("back_input_turned_copied")
        s_qkvg = sem("diff_projections")
        s_q3c = sem("diff_queries_copied")
        s_k3 = sem("diff_keys_spread")
        s_g3e = sem("diff_gates_in")
        s_g3x = sem("diff_gates_exps")
        s_s3 = sem("diff_scores")
        s_m3 = sem("diff_maxima")
        s_e3 = sem("diff_exps")
        s_a3 = sem("diff_probs")
        s_a3t = sem("diff_probs_turned")
        s_a3tc = sem("diff_probs_turned_copied")
        s_o3 = sem("diff_out")
        s_o3g = sem("diff_out_gated")
        s_o3t = sem("diff_out_turned")
        s_o3tc = sem("diff_out_turned_copied")
        s_pr3 = sem("diff_projected")
        s_ff1 = sem("hidden_and_router")
        s_ge = sem("gelu_arguments")
        s_gx = sem("gelu_exps")
        s_gl = sem("gelu_done")
        s_ff2 = sem("feedforward_out")
        s_out = sem("output_ready")
        s_st = sem("output_stored")

        def bc(ap, dims, at):
            for n, axis in zip(dims, at):
                ap = ap.unsqueeze(axis)
                shape = list(ap.shape)
                shape[axis] = n
                ap = ap.broadcast_to(shape)
            return ap

        def window_pair(gw, q):
            return xw[:, gw * 512 + q * P:gw * 512 + (q + 1) * P]

        def in_turns(*parts):
            parts = list(parts)
            while parts:
                parts = [part for part in parts if next(part, "over") != "over"]

        def paced(part, pace):
            for n in pace:
                for _ in range(n):
                    next(part, None)
                yield

        block = ctx.enter_context(nc.Block())

        @block.sync
        def _(eng):
            def load_x(p):
                for n, loaded in enumerate(s_x):
                    eng.dma_start(xw[:, n * 2048:(n + 1) * 2048], a["xw"][bass.ds(p * P, P), n * 2048:(n + 1) * 2048])\
                       .then_inc(loaded, 16)
                eng.dma_start(xT[:, :, :].rearrange("p g x -> p (g x)"), a["xT"][bass.ds(p * P, P)])\
                   .then_inc(s_xt, 16)

            load_x(0)
            with eng.Fori(1, pairs) as p:
                eng.wait_ge(s_ya, 2 * p)
                load_x(p)

        @block.gpsimd
        def _(eng):
            def gather(p, side):
                eng.wait_ge(s_idx, p + 1)
                eng.nop(nofuse=True)
                eng.tensor_copy(idx_live[:, side, :], idx_stage[:, :]).then_inc(s_idxl, 1)
                eng.wait_ge(s_idxl, p + 1)
                for c in range(CHUNKS):
                    eng.wait_ge(s_gu, p * CHUNKS + c + 1)
                    eng.nop(nofuse=True)
                    for t in range(c * TC, (c + 1) * TC):
                        eng.indirect_dma_start(gath[:, t, :], None, a["table"],
                                               bass.IndirectOffsetOnAxis(idx_live[:, side, t:t + 1], axis=0))\
                           .then_inc(s_g[c][t % TC // (TC // 2)], 16)

            def landed(p):
                for c in range(CHUNKS):
                    for half in range(2):
                        eng.wait_ge(s_g[c][half], (p + 1) * (8 * TC))

            gather(0, 0)
            with eng.Fori(0, (pairs - 2) // 2) as n:
                for u in (1, 2):
                    gather(n * 2 + u, u % 2)
                    landed(n * 2 + (u - 1))
            gather(pairs - 1, 1)
            landed(pairs - 1)

        @block.tensor
        def _(eng):
            def front(p):
                eng.wait_ge(s_simc, 2 * p)
                eng.wait_ge(s_mean, p + 1)
                eng.matmul(FB[0][:, 0:N], wqT[:, :], qT[:, :], start=True, stop=True).then_inc(s_qp, 1)
                yield
                eng.wait_ge(s_qexp, p + 1)
                for n in range(2):
                    ins = eng.matmul(FB[2 + n][0:1, :], bk2[:, :], q_exp[:, n * 512:(n + 1) * 512], start=True, stop=True)
                ins.then_inc(s_qkb, 1)
                for n in range(2):
                    eng.matmul(FB[n][:, :], wk_bd[:, :], q_exp[:, n * 512:(n + 1) * 512], start=True, stop=True)\
                       .then_inc(s_qk, 1)
                yield
                eng.wait_ge(s_qkc, 2 * p + 2)
                eng.wait_ge(s_qkbc, p + 1)
                for gw in range(GW):
                    o = FB[gw // 4][:, gw % 4 * P:(gw % 4 + 1) * P]
                    eng.matmul(o, mask_l[:, gw * P:(gw + 1) * P], mask_r[:, :], start=True, stop=False)
                    for q in range(4):
                        u = (gw * 4 + q) * 32
                        ins = eng.matmul(o[32 * q:32 * q + 32, :], qk[:, u:u + 32], window_pair(gw, q),
                                         start=False, stop=True)
                    if gw % 4 == 3:
                        ins.then_inc(s_sa, 1)
                yield
                for gw in range(GW):
                    eng.wait_ge(s_pa, 2 * p + gw // 4 + 1)
                    ins = eng.transpose(FB[gw // 4][:, gw % 4 * P:(gw % 4 + 1) * P], prob_a[:, gw * P:(gw + 1) * P],
                                        ident[:, :])
                    if gw % 4 == 3:
                        ins.then_inc(s_pta, 1)
                yield
                eng.wait_ge(s_xt, 16 * (p + 1))
                for gw in range(GW):
                    eng.wait_ge(s_ptac, 2 * p + gw // 4 + 1)
                    for q in range(4):
                        u = (gw * 4 + q) * 32
                        ins = eng.matmul(FB[2 + u // 512][:, u % 512:u % 512 + 32], xT[:, gw, q * P:(q + 1) * P],
                                         probT_a[:, u:u + 32], start=True, stop=True)
                    if gw % 4 == 3:
                        ins.then_inc(s_ya, 1)
                yield
                for n in range(2):
                    eng.wait_ge(s_yac, 2 * p + n + 1)
                    eng.matmul(FB[n][:, :], wvT[:, :], y_a[:, n * 512:(n + 1) * 512], start=True, stop=True)\
                       .then_inc(s_za, 1)
                yield
                eng.wait_ge(s_ctx, p + 1)
                eng.matmul(FB[2][:, 0:C], ctx_bd[:, :], woT2[:, :], start=True, stop=False)
                eng.matmul(FB[2][:, 0:C], q_bd[:, :], ident2[:, :], start=False, stop=True).then_inc(s_tok, 1)
                yield
                yield
                eng.wait_ge(s_hh, p + 1)
                eng.nop(nofuse=True)
                eng.transpose(FB[3][0:C, 0:P], hh[:, :], ident[:, :]).then_inc(s_hht, 1)
                yield
                eng.wait_ge(s_hhtc, p + 1)
                eng.nop(nofuse=True)
                eng.matmul(FB[0][0:C, 0:P], w_qkv[:, 0:C], hhT[:, :], start=True, stop=True)
                eng.matmul(FB[0][0:C, P:2 * P], w_qkv[:, C:2 * C], hhT[:, :], start=True, stop=True)
                eng.matmul(FB[0][:, 2 * P:2 * P + C], hhT[:, :], w_qkv[:, 2 * C:3 * C], start=True, stop=True)\
                   .then_inc(s_qkv, 1)
                yield
                eng.wait_ge(s_qkvc, p + 1)
                eng.matmul(FB[1][:, 0:P], q1[:, :], k1[:, :], start=True, stop=True).then_inc(s_s1, 1)
                yield
                eng.wait_ge(s_p1, p + 1)
                eng.transpose(FB[2][:, 0:P], p1[:, :], ident[:, :]).then_inc(s_p1t, 1)
                yield
                eng.wait_ge(s_p1tc, p + 1)
                eng.matmul(FB[3][0:C, 0:P], v1[:, :], p1T[:, :], start=True, stop=True).then_inc(s_o1, 1)
                yield
                eng.wait_ge(s_o1c, p + 1)
                eng.matmul(FB[0][:, 0:C], o1T[:, :], w_proj[:, :], start=True, stop=True).then_inc(s_pr, 1)
                yield
                yield
                eng.wait_ge(s_xc, p + 1)
                eng.nop(nofuse=True)
                eng.transpose(FB[1][0:C, 0:P], xn_f[:, :], ident[:, :]).then_inc(s_xct, 1)
                yield
                eng.wait_ge(s_xctc, p + 1)
                for m in range(4):
                    ins = eng.matmul(FB[0][:, m * P:(m + 1) * P], w_pk[:, m * P:(m + 1) * P], xcT[:, :],
                                     start=True, stop=True)
                ins.then_inc(s_qc, 1)
                yield
                eng.wait_ge(s_qcc, p + 1)
                eng.wait_ge(s_search, p)
                for m in range(4):
                    ins = eng.matmul(FB[1 - m // 2][:, m % 2 * 256:(m % 2 + 1) * 256], qpkT[:, m * P:(m + 1) * P],
                                     keys_bd[:, m, :], start=True, stop=True)
                    if m % 2 == 1:
                        ins.then_inc(s_sim, 1)

            def search(p):
                for _ in range(TURN_AT):
                    yield
                eng.wait_ge(s_fw, p + 1)
                eng.transpose(FB[1][:, 256:384], fidx[:, :], ident[:, :])
                eng.transpose(FB[1][:, 384:512], fexp[:, :, :].rearrange("p h j -> p (h j)"), ident[:, :])\
                   .then_inc(s_ft, 1)

            def take(p, c, halves=(0, 1)):
                if 0 in halves and c % (CHUNKS // 2) == 0:
                    eng.wait_ge(s_kvc, 2 * p + c // (CHUNKS // 2))
                    eng.wait_ge(s_wl, 2 * p + c // (CHUNKS // 2) + 1)
                for half in halves:
                    eng.wait_ge(s_g[c][half], (p + 1) * (8 * TC))
                    for t in range(c * TC + half * TC // 2, c * TC + (half + 1) * TC // 2):
                        g, lo = t % TC // 4 * 32, TPAD + t % HALF * TW - t % 4 * NH
                        ins = eng.matmul(sums[g:g + 32, c % 4 * P:(c % 4 + 1) * P], w_live[:, lo:lo + 32],
                                         gath[:, t, :], start=(t % 4 == 0), stop=(t % 4 == 3))
                if 1 in halves:
                    ins.then_inc(s_gu, 1)

            def turn_sums(p, n):
                eng.wait_ge(s_sc, 2 * p + n + 1)
                for m in range(4):
                    ins = eng.transpose(sums[:, m * P:(m + 1) * P], sums_sb[:, m * P:(m + 1) * P], ident[:, :])
                ins.then_inc(s_st2, 1)

            def rows(p, at=ROWS_AT):
                turn = 0
                for c, first in enumerate(at):
                    for _ in range(first - turn):
                        yield
                    take(p, c, (0,))
                    yield
                    take(p, c, (1,))
                    turn = first + 1
                    if c == CHUNKS // 2 - 1:
                        yield
                        turn_sums(p, 0)
                        turn += 1

            def back(p):
                eng.wait_ge(s_rot, p + 1)
                eng.nop(nofuse=True)
                for h in range(NH):
                    ins = eng.matmul(BB[1 + h // 4][0:C, h % 4 * P:(h % 4 + 1) * P], w_q2[:, h * C:(h + 1) * C],
                                     xcT_b[:, :], start=True, stop=True)
                ins.then_inc(s_qb, 1)
                take(p, CHUNKS - 1)
                turn_sums(p, 1)
                yield
                eng.wait_ge(s_kvc, 2 * p + 2)
                eng.wait_ge(s_qbc, 2 * p + 2)
                for n in range(2):
                    eng.matmul(BB[1 + n][:, :], ident_b[:, :], bc(causal_b[:, :], [4], [1]), start=True, stop=False)
                    for h in range(4 * n, 4 * n + 4):
                        ins = eng.matmul(BB[1 + n][:, h % 4 * P:(h % 4 + 1) * P], qc[:, h * P:(h + 1) * P],
                                         kv[0:C, :, h], start=False, stop=(h % 4 == 3))
                    ins.then_inc(s_s2, 1)
                for h in range(NH):
                    ins = eng.transpose(BB[0][:, h * C:(h + 1) * C], kv[C:P, :, h], ident[C:P, C:P])
                ins.then_inc(s_vt, 1)
                yield
                for h in range(NH):
                    eng.wait_ge(s_p2, 2 * p + h // 4 + 1)
                    ins = eng.transpose(BB[1 + h // 4][:, h % 4 * P:(h % 4 + 1) * P], s2[:, h * P:(h + 1) * P],
                                        ident[:, :])
                    if h % 4 == 3:
                        ins.then_inc(s_p2t, 1)
                yield
                eng.wait_ge(s_vtc, p + 1)
                for h in range(NH):
                    if h % 4 == 0:
                        eng.wait_ge(s_p2tc, 2 * p + h // 4 + 1)
                        eng.nop(nofuse=True)
                    lo = h % 2 * C
                    ins = eng.matmul(BB[0][lo:lo + C, h // 2 * P:(h // 2 + 1) * P], v2[:, h, :],
                                     p2T[:, h * P:(h + 1) * P], start=True, stop=True)
                ins.then_inc(s_o2, 1)
                yield
                eng.wait_ge(s_o2c, p + 1)
                for m in range(4):
                    ins = eng.matmul(BB[1][:, 0:C], o2T[:, m * P:(m + 1) * P], w_o2[:, m, :],
                                     start=(m == 0), stop=(m == 3))
                ins.then_inc(s_wo, 1)
                yield
                eng.wait_ge(s_xb, 2 * p + 1)
                eng.nop(nofuse=True)
                eng.transpose(BB[2][0:C, 0:P], xn_b[:, :], ident[:, :]).then_inc(s_xbt, 1)
                yield
                eng.wait_ge(s_xbtc, 2 * p + 1)
                for m in range(2):
                    eng.matmul(BB[0][:, m * P:(m + 1) * P], w_q3[:, m * P:(m + 1) * P], xbT[:, :],
                               start=True, stop=True)
                    eng.matmul(BB[1 + m][:, 256:384], w_kv3[:, m * P:(m + 1) * P], xbT[:, :],
                               start=True, stop=True)
                eng.matmul(BB[2][:, 0:256], xbT[:, :], w_kv3[:, 256:512], start=True, stop=True)
                eng.matmul(BB[1][:, 0:256], xbT[:, :], w_g3[:, :], start=True, stop=True).then_inc(s_qkvg, 1)
                yield
                eng.wait_ge(s_q3c, 2 * p + 2)
                eng.wait_ge(s_g3e, p + 1)
                eng.wait_ge(s_k3, 2 * p + 2)
                for n in range(4):
                    m, half = n // 2, n % 2
                    if n == 3:
                        eng.wait_ge(s_e3, 4 * p + 1)
                    eng.matmul(BB[n % 3][:, :], ident_b[:, :], bc(same_b[:, :], [4], [1]), start=True, stop=False)
                    eng.matmul(BB[n % 3][:, :], q3T[:, m * P:(m + 1) * P], k_exp[:, m, half * 4:half * 4 + 4, :],
                               start=False, stop=True).then_inc(s_s3, 1)
                yield
                for h in range(NH):
                    eng.wait_ge(s_a3, 2 * p + h // 4 + 1)
                    ins = eng.transpose(BB[1 + h // 4][:, h % 4 * P:(h % 4 + 1) * P], a3[:, h, :], ident[:, :])
                    if h % 4 == 3:
                        ins.then_inc(s_a3t, 1)
                yield
                for h in range(NH):
                    eng.wait_ge(s_a3tc, 2 * p + h // 4 + 1)
                    ins = eng.matmul(BB[0][:, h * D3:(h + 1) * D3], a3T[:, h * P:(h + 1) * P],
                                     v3[:, h * D3:(h + 1) * D3], start=True, stop=True)
                ins.then_inc(s_o3, 1)
                yield
                eng.wait_ge(s_o3g, p + 1)
                for m in range(2):
                    ins = eng.transpose(BB[1][:, m * P:(m + 1) * P],
                                        o3[:, 4 * m:4 * m + 4, :].rearrange("p h d -> p (h d)"), ident[:, :])
                ins.then_inc(s_o3t, 1)
                yield
                eng.wait_ge(s_o3tc, p + 1)
                for m in range(2):
                    ins = eng.matmul(BB[2][:, 0:C], o3T[:, m * P:(m + 1) * P], w_out3[:, m, :],
                                     start=(m == 0), stop=(m == 1))
                ins.then_inc(s_pr3, 1)
                yield
                eng.wait_ge(s_xb, 2 * p + 2)
                eng.nop(nofuse=True)
                eng.transpose(BB[0][0:C, 0:P], xn_b[:, :], ident[:, :]).then_inc(s_xbt, 1)
                yield
                eng.wait_ge(s_xbtc, 2 * p + 2)
                for m in range(2):
                    eng.matmul(BB[1][:, m * P:(m + 1) * P], w1[:, m * P:(m + 1) * P], xbT[:, :],
                               start=True, stop=True)
                eng.matmul(BB[2][:, 0:P], wr_bc[:, :], xbT[:, :], start=True, stop=True).then_inc(s_ff1, 1)
                yield
                yield
                eng.wait_ge(s_gl, p + 1)
                for m in range(2):
                    ins = eng.matmul(BB[0][:, 0:C], z1[:, m * P:(m + 1) * P], w2[:, m, :],
                                     start=(m == 0), stop=(m == 1))
                ins.then_inc(s_ff2, 1)

            eng.wait_ge(s_cf, 16)
            eng.wait_ge(s_zero, 1)
            eng.nop().then_inc(s_gu, CHUNKS)

            def second():
                for _ in range(7):
                    yield
                eng.wait_ge(s_cs, 16)

            in_turns(front(0), second())
            in_turns(search(0))
            eng.wait_ge(s_cb, 16)
            in_turns(front(1), rows(0, ROWS_AT_0))
            in_turns(search(1))
            in_turns(front(2))
            with eng.Fori(1, pairs - 2) as i:
                in_turns(front(i + 2), paced(search(i + 1), PACE), back(i - 1), rows(i))
            in_turns(search(pairs - 1), back(pairs - 3), rows(pairs - 2))
            in_turns(back(pairs - 2), rows(pairs - 1))
            in_turns(back(pairs - 1))

        @block.scalar
        def _(eng):
            def copy(o, i, s, scale=1.0):
                eng.activation(o, i, ACT.Copy, scale=scale).then_inc(s, 1)

            def preload(func):
                eng.activation(table_seed[:, :], eps[:, :], func)

            def front(p, alone=False):
                yield
                for n in range(2):
                    eng.wait_ge(s_qk, 2 * p + n + 1)
                    copy(qk[:, n * 512:(n + 1) * 512], FB[n][:, :], s_qkc)
                yield
                for n in range(2):
                    eng.wait_ge(s_ma, 2 * p + n + 1)
                    for u in range(4):
                        g = 4 * n + u
                        ins = eng.activation(prob_a[:, g * P:(g + 1) * P], FB[n][:, u * P:(u + 1) * P], ACT.Exp,
                                             bias=max_a[:, g:g + 1], accum_out=sum_a[:, g:g + 1])
                    ins.then_inc(s_ea, 1)
                yield
                for n in range(2):
                    eng.wait_ge(s_pta, 2 * p + n + 1)
                    copy(probT_a[:, n * 512:(n + 1) * 512], FB[n][:, :], s_ptac)
                if alone:
                    preload(ACT.Sqrt)
                yield
                for n in range(2):
                    eng.wait_ge(s_ya, 2 * p + n + 1)
                    copy(y_a[:, n * 512:(n + 1) * 512], FB[2 + n][:, :], s_yac)
                yield
                yield

                def deviation(k):
                    eng.wait_ge(s_varf, 4 * p + k)
                    eng.activation(std_f[:, :], mv_f[:, 1:2], ACT.Sqrt, bias=eps[:, :]).then_inc(s_stdf, 1)

                deviation(1)
                yield
                deviation(2)
                if alone:
                    preload(ACT.Exp)
                yield
                eng.wait_ge(s_hht, p + 1)
                copy(hhT[:, :], FB[3][0:C, 0:P], s_hhtc)
                yield
                yield
                eng.wait_ge(s_m1, p + 1)
                eng.activation(p1[:, :], s1[:, :], ACT.Exp, bias=max1[:, :], accum_out=sum1[:, :]).then_inc(s_e1, 1)
                yield
                eng.wait_ge(s_p1t, p + 1)
                copy(p1T[:, :], FB[2][:, 0:P], s_p1tc)
                yield
                eng.wait_ge(s_o1, p + 1)
                copy(o1T[:, :], FB[3][0:C, 0:P], s_o1c)
                if alone:
                    preload(ACT.Sqrt)
                yield
                deviation(3)
                yield
                deviation(4)
                if alone:
                    preload(ACT.Exp)
                yield
                eng.wait_ge(s_xct, p + 1)
                copy(xcT[:, :], FB[1][0:C, 0:P], s_xctc)
                yield
                eng.wait_ge(s_qc, p + 1)
                copy(qpkT[:, :], FB[0][:, :], s_qcc)
                yield
                for n in range(2):
                    eng.wait_ge(s_sim, 2 * p + n + 1)
                    copy(sims[:, n * 512:(n + 1) * 512], FB[1 - n][:, :], s_simc)

            def search(p):
                for _ in range(EXP_AT):
                    yield
                eng.wait_ge(s_fm, p + 1)
                eng.activation(fexp[:, :, :], fin[:, :, :], ACT.Exp).then_inc(s_fe, 1)

            def copy_sums(p, n):
                eng.wait_ge(s_gu, CHUNKS * (p + 1) + (n + 1) * (CHUNKS // 2))
                copy(sums_sb[:, :], sums[:, :], s_sc)

            def copy_turned(p, n):
                eng.wait_ge(s_st2, 2 * p + n + 1)
                copy(kv[:, :, :].rearrange("p t h -> p (t h)")[:, n * 512:(n + 1) * 512], sums[:, :], s_kvc)

            def rows(p, at=ROWS_AT):
                for _ in range(at[CHUNKS // 2 - 1] + 1):
                    yield
                copy_sums(p, 0)
                yield
                copy_turned(p, 0)

            def back(p, alone=False):
                eng.wait_ge(s_qb, p + 1)
                for n in range(2):
                    copy(qc[:, n * 512:(n + 1) * 512], BB[1 + n][0:C, :], s_qbc, scale=C ** -0.5)
                copy_sums(p, 1)
                copy_turned(p, 1)
                yield
                eng.wait_ge(s_vt, p + 1)
                copy(v2[:, :, :].rearrange("p h d -> p (h d)"), BB[0][:, :], s_vtc)
                for h in range(NH):
                    eng.wait_ge(s_m2, 2 * p + h // 4 + 1)
                    ins = eng.activation(s2[:, h * P:(h + 1) * P], BB[1 + h // 4][:, h % 4 * P:(h % 4 + 1) * P],
                                         ACT.Exp, bias=max2[:, h:h + 1], accum_out=sum2[:, h:h + 1])
                    if h % 4 == 3:
                        ins.then_inc(s_e2, 1)
                yield
                for n in range(2):
                    eng.wait_ge(s_p2t, 2 * p + n + 1)
                    copy(p2T[:, n * 512:(n + 1) * 512], BB[1 + n][:, :], s_p2tc)
                yield
                eng.wait_ge(s_o2, p + 1)
                copy(o2T[:, :], BB[0][:, :], s_o2c)
                if alone:
                    preload(ACT.Sqrt)
                yield
                eng.wait_ge(s_varb, 3 * p + 1)
                eng.activation(std_b[:, 0:1], mv_b[:, 1:2], ACT.Sqrt, bias=eps[:, :]).then_inc(s_stdb, 1)
                yield
                eng.wait_ge(s_xbt, 2 * p + 1)
                copy(xbT[:, :], BB[2][0:C, 0:P], s_xbtc)
                if alone:
                    preload(ACT.Exp)
                yield
                eng.wait_ge(s_qkvg, p + 1)
                copy(q3T[:, :], BB[0][:, 0:256], s_q3c, scale=16 ** -0.5)
                copy(v3[:, :], BB[2][:, 0:256], s_q3c)
                for h in range(NH):
                    ins = eng.activation(k_exp[:, 1, h, :], BB[2][:, 256:384], ACT.Copy, scale=m16[:, h:h + 1])
                ins.then_inc(s_k3, 1)
                eng.wait_ge(s_g3e, p + 1)
                eng.activation(g3[:, :], g3[:, :], ACT.Exp, scale=-1.0).then_inc(s_g3x, 1)
                yield
                for h in range(H3):
                    eng.wait_ge(s_m3, 4 * p + h // 4 + 1)
                    ins = eng.activation(s3[:, h, :], BB[h // 4 % 3][:, h % 4 * P:(h % 4 + 1) * P],
                                         ACT.Exp, bias=max3[:, h:h + 1], accum_out=sum3[:, h:h + 1])
                    if h % 4 == 3:
                        ins.then_inc(s_e3, 1)
                yield
                eng.wait_ge(s_a3t, 2 * p + 2)
                for n in range(2):
                    copy(a3T[:, n * 512:(n + 1) * 512], BB[1 + n][:, :], s_a3tc)
                if alone:
                    preload(ACT.Sqrt)
                yield
                eng.wait_ge(s_varb, 3 * p + 2)
                eng.activation(std_b[:, :], mean3[:, :], ACT.Sqrt, bias=eps[:, :], scale=1.0 / D3).then_inc(s_stdb, 1)
                yield
                eng.wait_ge(s_o3t, p + 1)
                copy(o3T[:, :], BB[1][:, 0:256], s_o3tc)
                yield
                eng.wait_ge(s_varb, 3 * p + 3)
                eng.activation(std_b[:, 0:1], mv_b[:, 1:2], ACT.Sqrt, bias=eps[:, :]).then_inc(s_stdb, 1)
                yield
                eng.wait_ge(s_xbt, 2 * p + 2)
                copy(xbT[:, :], BB[0][0:C, 0:P], s_xbtc)
                if alone:
                    preload(ACT.Exp)
                yield
                eng.wait_ge(s_ge, p + 1)
                eng.activation(z1b[:, :], z1b[:, :], ACT.Exp, scale=-GELU_C).then_inc(s_gx, 1)
                yield
                yield
                eng.wait_ge(s_out, p + 1)
                eng.dma_start(out[bass.ds(p * 2, 2)].rearrange("b n c -> (b n) c"), out_sb[:, :]).then_inc(s_st, 16)

            for lo, hi, loaded in zip(starts, starts[1:], (s_cf, s_cs, s_cb)):
                eng.dma_start(packed[:, lo:hi], a["packed"][:, lo:hi]).then_inc(loaded, 16)
            eng.nop().then_inc(s_st, 16)
            eng.wait_ge(s_cf, 16)
            preload(ACT.Exp)
            in_turns(front(0, alone=True))
            in_turns(search(0))
            eng.wait_ge(s_lam, 1)
            eng.activation(lexp[:, :], lsum[:, :], ACT.Exp).then_inc(s_lame, 1)
            in_turns(front(1), rows(0, ROWS_AT_0))
            in_turns(search(1))
            in_turns(front(2))
            with eng.Fori(1, pairs - 2) as i:
                in_turns(front(i + 2), paced(search(i + 1), PACE), back(i - 1), rows(i))
            in_turns(search(pairs - 1), back(pairs - 3), rows(pairs - 2))
            in_turns(back(pairs - 2), rows(pairs - 1))
            in_turns(back(pairs - 1, alone=True))
            eng.wait_ge(s_st, 16 * (pairs + 1))

        @block.vector
        def _(eng):
            def normalize(step, p, k, n, o, i, stats, mv, std, s_var, s_std):
                step(eng.bn_stats(stats[:, :], i), apart=True)
                eng.bn_aggr(mv[:, :], stats[:, :]).then_inc(s_var, 1)
                yield
                eng.wait_ge(s_var, n * p + k)
                eng.wait_ge(s_std, n * p + k)
                step(eng.reciprocal(std[:, 0:1], std[:, 0:1]))
                return eng.tensor_scalar(o, i, mv[:, 0:1], std[:, 0:1], ALU.subtract, ALU.mult)

            def front(p):
                step = Steps(eng, n_front, FRONT_STEPS, p)

                def norm(k, o, i):
                    return normalize(step, p, k, 4, o, i, stats_f, mv_f, std_f, s_varf, s_stdf)

                for n, loaded in enumerate(s_x):
                    eng.wait_ge(loaded, 16 * (p + 1))
                    ins = eng.tensor_reduce(qsum[:, n * 32:(n + 1) * 32],
                                            xw[:, n * 2048:(n + 1) * 2048].rearrange("p (w x) -> p w x", w=32),
                                            AX.X, ALU.add)
                step(ins)
                for b in range(2):
                    r = slice(b * C, b * C + C)
                    eng.tensor_scalar(q_bd[r, r], qsum[r, :], 1.0 / 64, None, ALU.mult)
                eng.tensor_scalar(qT[:, :], qsum[:, :], 1.0 / 64, None, ALU.mult).then_inc(s_mean, 1)
                eng.wait_ge(s_qp, p + 1)
                step(eng.tensor_scalar(qp[:, :], FB[0][:, 0:N], bq2[:, 0:1], 8 ** -0.5, ALU.add, ALU.mult))
                eng.tensor_tensor(q_exp[:, :].rearrange("p (g r) -> p g r", r=16), bc(qp[:, :], [16], [2]),
                                  bc(m8[:, :], [N], [1]), ALU.mult).then_inc(s_qexp, 1)
                yield
                eng.wait_ge(s_qkb, p + 1)
                for n in range(2):
                    ins = eng.tensor_copy(mask_l[0:1, n * 512:(n + 1) * 512], FB[2 + n][0:1, :])
                ins.then_inc(s_qkbc, 1)
                yield
                for n in range(2):
                    eng.wait_ge(s_sa, 2 * p + n + 1)
                    eng.tensor_reduce(max_a[:, 4 * n:4 * n + 4], FB[n][:, :].rearrange("p (u x) -> p u x", u=4),
                                      AX.X, ALU.max, negate=True).then_inc(s_ma, 1)
                yield
                for n in range(2):
                    eng.wait_ge(s_ea, 2 * p + n + 1)
                    step(eng.reciprocal(sum_a[:, 4 * n:4 * n + 4], sum_a[:, 4 * n:4 * n + 4]))
                    pv = prob_a[:, n * 512:(n + 1) * 512].rearrange("p (u x) -> p u x", u=4)
                    eng.tensor_tensor(pv, pv, bc(sum_a[:, 4 * n:4 * n + 4], [P], [2]), ALU.mult).then_inc(s_pa, 1)
                yield
                yield
                for n in range(2):
                    eng.wait_ge(s_za, 2 * p + n + 1)
                    ins = eng.tensor_tensor(z_a[:, n * 512:(n + 1) * 512].rearrange("p (g r) -> p g r", r=16),
                                            FB[n][:, :].rearrange("p (g r) -> p g r", r=16),
                                            bc(m8[:, :], [32], [1]), ALU.mult)
                step(ins)
                step(eng.tensor_reduce(ctx_a[:, :], z_a[:, :].rearrange("p (g r) -> p g r", r=16), AX.X, ALU.add))
                for b in range(2):
                    r = slice(b * C, b * C + C)
                    ins = eng.tensor_scalar(ctx_bd[r, r], ctx_a[r, :], bv2[r, 0:1], None, ALU.add)
                ins.then_inc(s_ctx, 1)
                yield
                eng.wait_ge(s_tok, p + 1)
                step(eng.tensor_tensor(h_f[:, :], FB[2][:, 0:C], bo_r[:, :], ALU.add))
                step((yield from norm(1, xn_f[:, :], h_f[:, :])))
                step((yield from norm(2, hh[:, :], xn_f[:, :])))
                step(eng.tensor_tensor(hh[:, :], hh[:, :], ln1g[:, :], ALU.mult))
                eng.tensor_tensor(hh[:, :], hh[:, :], ln1b[:, :], ALU.add).then_inc(s_hh, 1)
                yield
                eng.wait_ge(s_qkv, p + 1)
                eng.tensor_scalar(q1[:, :], FB[0][0:C, 0:P], b_qk[:, 0:1], None, ALU.add)
                eng.tensor_scalar(k1[:, :], FB[0][0:C, P:2 * P], b_qk[:, 1:2], None, ALU.add)
                eng.tensor_tensor(v1[:, :], FB[0][:, 2 * P:2 * P + C], b_v[:, :], ALU.add).then_inc(s_qkvc, 1)
                yield
                eng.wait_ge(s_s1, p + 1)
                step(eng.tensor_tensor(s1[:, :], FB[1][:, 0:P], rel_bias[:, :], ALU.add))
                eng.tensor_reduce(max1[:, :], s1[:, :], AX.X, ALU.max, negate=True).then_inc(s_m1, 1)
                yield
                eng.wait_ge(s_e1, p + 1)
                step(eng.reciprocal(sum1[:, :], sum1[:, :]))
                eng.tensor_scalar(p1[:, :], p1[:, :], sum1[:, 0:1], scale1[:, 0:1], ALU.mult, ALU.mult).then_inc(s_p1, 1)
                yield
                yield
                eng.wait_ge(s_pr, p + 1)
                step(eng.tensor_tensor(o1[:, :], FB[0][:, 0:C], b_proj[:, :], ALU.add))
                step((yield from norm(3, o1[:, :], o1[:, :])))
                step(eng.tensor_tensor(o1[:, :], o1[:, :], ln2g[:, :], ALU.mult))
                step(eng.tensor_tensor(o1[:, :], o1[:, :], ln2b[:, :], ALU.add))
                step(eng.tensor_tensor(h_f[:, :], h_f[:, :], o1[:, :], ALU.add))
                (yield from norm(4, xn_f[:, :], h_f[:, :])).then_inc(s_xc, 1)
                step.end()

            def search(p):
                step = Steps(eng, n_search, SEARCH_STEPS, p)
                eng.wait_ge(s_simc, 2 * p + 2)
                eng.nop(nofuse=True)
                tops = [(top[:, g // 8, g % 8, :], topi_u[:, g // 8, g % 8, :], sim[:, g, :], sim_b[:, g, :])
                        for g in range(16)]
                yield from best(step, tops)
                yield
                step(eng.tensor_copy(topi[:, :, :, :], topi_u[:, :, :, :]))
                i0, i1 = (topi[:, n, :, :].rearrange("p h j -> p (h j)") for n in range(2))
                step(eng.scalar_tensor_tensor(i1, i1, float(NKEY), head_off[:, :], ALU.mult, ALU.add))
                for runs, pairs_of in ((RUNS, ((cand, top), (candi, topi))), (RUNS8, ((candi8, topi),))):
                    lo = 0
                    for first, na, nb in runs:
                        for o, v in pairs_of:
                            ins = eng.tensor_tensor(
                                o[:, :, lo:lo + na * nb].rearrange("p h (a b) -> p h a b", a=na),
                                bc(v[:, 0, :, first:first + na], [nb], [3]), bc(v[:, 1, :, 0:nb], [na], [2]), ALU.add)
                        lo += na * nb
                step(ins, apart=True)
                yield
                yield from best(step, [(fin[:, h, :], pos_u[:, h, :], cand[:, h, :], cand_b[:, h, :]) for h in range(NH)])
                step(eng.tensor_copy(pos[:, :, :], pos_u[:, :, :]))
                step(eng.tensor_copy(fsum[:, :], fin[:, :, 0]))
                eng.tensor_tensor(fin[:, :, :], fin[:, :, :], bc(fsum[:, :], [TOPK], [2]), ALU.subtract)\
                   .then_inc(s_fm, 1)
                yield
                lookups = [(h, 4, 0, NC8, pos20, candi8) for h in (0, 4)] + \
                          [(h, 2, 8, NC, pos50, candi) for h in (0, 2, 4, 6)]
                for h, n, j, nc_, places_of, rows_of in lookups:
                    o = hot[:, 0:n * 8 * nc_].rearrange("p (h j c) -> p h j c", h=n, c=nc_)
                    step(eng.tensor_tensor(o, bc(pos[:, h:h + n, j:j + 8], [nc_], [3]),
                                           bc(places_of[:, :], [n, 8], [1, 2]), ALU.is_equal))
                    step(eng.tensor_tensor(o, o, bc(rows_of[:, h:h + n, :], [8], [2]), ALU.mult))
                    step(eng.tensor_reduce(fidx[:, :].rearrange("p (h j) -> p h j", h=NH)[:, h:h + n, j:j + 8], o,
                                           AX.X, ALU.add))
                    yield
                eng.wait_ge(s_fe, p + 1)
                step(eng.tensor_reduce(fsum[:, :], fexp[:, :, :], AX.X, ALU.add))
                step(eng.reciprocal(fsum[:, :], fsum[:, :]))
                eng.tensor_tensor(fexp[:, :, :], fexp[:, :, :], bc(fsum[:, :], [TOPK], [2]), ALU.mult).then_inc(s_fw, 1)
                yield
                eng.wait_ge(s_ft, p + 1)
                eng.wait_ge(s_idxl, p)
                eng.tensor_copy(idx_stage[:, :], FB[1][:, 256:384]).then_inc(s_idx, 1)
                eng.tensor_copy(w_next[:, :], FB[1][:, 384:512]).then_inc(s_search, 1)
                step.end()

            def best(step, rows):
                for o, oi, v, w in rows:
                    ins = eng.max(o[:, 0:8], v)
                step(ins, apart=True)
                yield
                for o, oi, v, w in rows:
                    eng.max_index(oi[:, 0:8], o[:, 0:8], v)
                    ins = eng.match_replace(w, o[:, 0:8], v, LOWEST)
                step(ins, apart=True)
                yield
                for o, oi, v, w in rows:
                    ins = eng.max(o[:, 8:16], w)
                step(ins, apart=True)
                for o, oi, v, w in rows:
                    ins = eng.max_index(oi[:, 8:16], o[:, 8:16], w)
                step(ins)

            def rows(p, at=ROWS_AT):
                yield
                eng.wait_ge(s_wm, p + 1)
                for n in range(2):
                    eng.wait_ge(s_gu, CHUNKS * (p + 1) + n * (CHUNKS // 2))
                    eng.tensor_tensor(w_live[:, TPAD:].rearrange("p (t x) -> p t x", x=TW)[:, :, 0:NH],
                                      bc(w_mid[:, n * HALF:(n + 1) * HALF], [NH], [2]), bc(m16[:, :], [HALF], [1]),
                                      ALU.mult).then_inc(s_wl, 1)
                    if n == 0:
                        for _ in range(at[CHUNKS // 2 - 1] + 1):
                            yield

            def keep(n):
                eng.wait_ge(s_xctc, n)
                eng.tensor_copy(h_next[:, :], h_f[:, :])
                eng.tensor_copy(xcT_next[:, :], xcT[:, :]).then_inc(s_keep, 1)
                eng.wait_ge(s_keep, n)

            def pass_weights(n):
                eng.wait_ge(s_search, n)
                eng.wait_ge(s_wl, 2 * n - 2)
                eng.tensor_copy(w_mid[:, :], w_next[:, :]).then_inc(s_wm, 1)

            def shift(n):
                eng.tensor_copy(h_mid[:, :], h_next[:, :])
                eng.tensor_copy(xcT_mid[:, :], xcT_next[:, :]).then_inc(s_shift, 1)
                eng.wait_ge(s_shift, n)

            def carry(p):
                eng.wait_ge(s_out, p)
                eng.tensor_copy(h_b[:, :], h_mid[:, :])
                eng.tensor_copy(xcT_b[:, :], xcT_mid[:, :]).then_inc(s_rot, 1)
                eng.wait_ge(s_rot, p + 1)

            def back(p):
                step = Steps(eng, n_back, BACK_STEPS, p)

                def norm(k, o, i):
                    return normalize(step, p, k, 3, o, i, stats_b, mv_b, std_b, s_varb, s_stdb)

                yield
                sv = s2[:, :].rearrange("p (h x) -> p h x", h=NH)
                for n in range(2):
                    eng.wait_ge(s_s2, 2 * p + n + 1)
                    eng.tensor_reduce(max2[:, 4 * n:4 * n + 4], BB[1 + n][:, :].rearrange("p (h x) -> p h x", h=4),
                                      AX.X, ALU.max, negate=True).then_inc(s_m2, 1)
                yield
                for h in (0, 4):
                    eng.wait_ge(s_e2, 2 * p + h // 4 + 1)
                    step(eng.reciprocal(sum2[:, h:h + 4], sum2[:, h:h + 4]))
                    eng.tensor_tensor(sv[:, h:h + 4, :], sv[:, h:h + 4, :], bc(sum2[:, h:h + 4], [P], [2]), ALU.mult)\
                       .then_inc(s_p2, 1)
                yield
                yield
                eng.wait_ge(s_wo, p + 1)
                step(eng.tensor_tensor(h_b[:, :], h_b[:, :], BB[1][:, 0:C], ALU.add))
                (yield from norm(1, xn_b[:, :], h_b[:, :])).then_inc(s_xb, 1)
                yield
                eng.wait_ge(s_qkvg, p + 1)
                eng.tensor_tensor(g3[:, :], BB[1][:, 0:256], b_g3[:, :], ALU.add).then_inc(s_g3e, 1)
                ins = eng.tensor_tensor(k_exp[:, 0, :, :], bc(BB[1][:, 256:384], [NH], [1]), bc(m16[:, :], [P], [2]),
                                        ALU.mult)
                ins.then_inc(s_k3, 1)
                yield
                for n in range(4):
                    eng.wait_ge(s_s3, 4 * p + n + 1)
                    eng.tensor_reduce(max3[:, 4 * n:4 * n + 4], BB[n % 3][:, :].rearrange("p (h x) -> p h x", h=4),
                                      AX.X, ALU.max, negate=True).then_inc(s_m3, 1)
                yield
                eng.wait_ge(s_e3, 4 * p + 4)
                step(eng.reciprocal(rec3[:, :], sum3[:, :]))
                se, re = (t[:, :].rearrange("p (h e) -> p h e", e=2) for t in (sum3, rec3))
                step(eng.scalar_tensor_tensor(fac3[:, :], se[:, :, 0], neg_lam[:, 0:1], re[:, :, 1], ALU.mult, ALU.mult))
                for h in range(8):
                    ins = eng.scalar_tensor_tensor(a3[:, h, :], s3[:, 2 * h + 1, :], fac3[:, h:h + 1], s3[:, 2 * h, :],
                                                   ALU.mult, ALU.add)
                    if h % 4 == 3:
                        ins.then_inc(s_a3, 1)
                yield
                eng.wait_ge(s_o3, p + 1)
                ov = BB[0][:, 0:256].rearrange("p (h d) -> p h d", d=D3)
                step(eng.tensor_tensor(o3[:, :, :], ov, bc(re[:, :, 0], [D3], [2]), ALU.mult))
                step(eng.tensor_reduce(mean3[:, :], o3[:, :, :], AX.X, ALU.add))
                step(eng.tensor_scalar(mean3[:, :], mean3[:, :], 1.0 / D3, None, ALU.mult))
                step(eng.tensor_tensor(o3[:, :, :], o3[:, :, :], bc(mean3[:, :], [D3], [2]), ALU.subtract))
                step(eng.tensor_tensor(sq3[:, :, :], o3[:, :, :], o3[:, :, :], ALU.mult))
                eng.tensor_reduce(mean3[:, :], sq3[:, :, :], AX.X, ALU.add).then_inc(s_varb, 1)
                yield
                step(eng.tensor_tensor(o3[:, :, :], o3[:, :, :], bc(gam3[:, :], [8], [1]), ALU.mult))
                eng.wait_ge(s_g3x, p + 1)
                step(eng.tensor_scalar(g3[:, :], g3[:, :], 1.0, None, ALU.add))
                step(eng.reciprocal(g3[:, :], g3[:, :]))
                eng.wait_ge(s_stdb, 3 * p + 2)
                step(eng.reciprocal(std_b[:, :], std_b[:, :]))
                step(eng.tensor_tensor(o3[:, :, :], o3[:, :, :], bc(std_b[:, :], [D3], [2]), ALU.mult))
                step(eng.tensor_tensor(o3[:, :, :], o3[:, :, :], bc(bet3[:, :], [8], [1]), ALU.add))
                o3r = o3[:, :, :].rearrange("p h d -> p (h d)")
                eng.scalar_tensor_tensor(o3r, o3r, 1.0 - LAMBDA_INIT, g3[:, :], ALU.mult, ALU.mult).then_inc(s_o3g, 1)
                yield
                eng.wait_ge(s_pr3, p + 1)
                step(eng.tensor_tensor(h_b[:, :], h_b[:, :], BB[2][:, 0:C], ALU.add))
                step(eng.tensor_tensor(h_b[:, :], h_b[:, :], b_out3[:, :], ALU.add))
                (yield from norm(3, xn_b[:, :], h_b[:, :])).then_inc(s_xb, 1)
                yield
                eng.wait_ge(s_ff1, p + 1)
                for m in range(2):
                    ins = eng.tensor_scalar(z1[:, m * P:(m + 1) * P], BB[1][:, m * P:(m + 1) * P], b1c[:, m:m + 1],
                                            None, ALU.add)
                step(ins)
                step(eng.tensor_tensor(z1b[:, :], z1[:, :], z1[:, :], ALU.mult))
                step(eng.tensor_scalar(z1b[:, :], z1b[:, :], 0.044715, 1.0, ALU.mult, ALU.add))
                step(eng.tensor_tensor(z1b[:, :], z1b[:, :], z1[:, :], ALU.mult))
                eng.tensor_scalar(z1b[:, :], z1b[:, :], -54.0, None, ALU.max).then_inc(s_ge, 1)
                yield
                step(eng.tensor_scalar(wrow[:, :], BB[2][:, 0:P], br_c[:, 0:1], None, ALU.add))
                step(eng.tensor_tensor(wcmp[:, :], wrow[:, :], ident[:, :], ALU.mult))
                step(eng.tensor_reduce(wcol[:, :], wcmp[:, :], AX.X, ALU.add))
                eng.wait_ge(s_gx, p + 1)
                step(eng.tensor_scalar(z1b[:, :], z1b[:, :], 1.0, None, ALU.add))
                step(eng.reciprocal(z1b[:, :], z1b[:, :]))
                eng.tensor_tensor(z1[:, :], z1[:, :], z1b[:, :], ALU.mult).then_inc(s_gl, 1)
                yield
                step(eng.scalar_tensor_tensor(wcmp[:, :], wrow[:, :], wcol[:, 0:1], same01[:, :], ALU.is_gt, ALU.mult))
                step(eng.tensor_reduce(rank2[:, 0:1], wcmp[:, :], AX.X, ALU.add))
                step(eng.scalar_tensor_tensor(wcmp[:, :], wrow[:, :], wcol[:, 0:1], before01[:, :], ALU.is_equal, ALU.mult))
                step(eng.tensor_reduce(rank2[:, 1:2], wcmp[:, :], AX.X, ALU.add))
                step(eng.tensor_tensor(factor[:, :], rank2[:, 0:1], rank2[:, 1:2], ALU.add))
                step(eng.scalar_tensor_tensor(factor[:, :], factor[:, :], float(KEEP), wcol[:, :], ALU.is_lt, ALU.mult))
                eng.wait_ge(s_ff2, p + 1)
                step(eng.tensor_tensor(y_o[:, :], BB[0][:, 0:C], b2r[:, :], ALU.add))
                step(eng.scalar_tensor_tensor(y_o[:, :], y_o[:, :], factor[:, 0:1], xn_b[:, :], ALU.mult, ALU.add))
                eng.wait_ge(s_st, 16 * (p + 1))
                eng.tensor_tensor(out_sb[:, :], y_o[:, :], h_b[:, :], ALU.add).then_inc(s_out, 1)
                step.end()

            eng.memset(q_bd[:, :], 0.0)
            eng.memset(w_live[:, :], 0.0)
            eng.memset(ctx_bd[:, :], 0.0).then_inc(s_zero, 1)
            eng.wait_ge(s_zero, 1)
            eng.wait_ge(s_cf, 16)
            step = Steps(eng, n_setup, SETUP_STEPS, 0)

            def second():
                for _ in range(3):
                    yield
                eng.wait_ge(s_cs, 16)
                step(eng.tensor_tensor(rel_bias[:, :], rel_bias[:, :], same_neg[:, :], ALU.add))

            in_turns(front(0), second())
            keep(1)
            shift(1)
            in_turns(search(0))
            pass_weights(1)
            eng.tensor_copy(ident_b[:, :], ident[:, :])
            eng.tensor_copy(same_b[:, :], same_neg[:, :])
            eng.wait_ge(s_cb, 16)
            eng.tensor_copy(causal_b[:, :], causal_neg[:, :])
            step(eng.tensor_tensor(lprod[:, :, :], lqk[:, 0:2, :], lqk[:, 2:4, :], ALU.mult))
            eng.tensor_reduce(lsum[:, :], lprod[:, :, :], AX.X, ALU.add).then_inc(s_lam, 1)
            eng.wait_ge(s_lame, 1)
            step(eng.tensor_tensor(neg_lam[:, :], lexp[:, 1:2], lexp[:, 0:1], ALU.subtract))
            step(eng.tensor_scalar(neg_lam[:, :], neg_lam[:, :], -LAMBDA_INIT, None, ALU.add))
            step.end()
            in_turns(front(1), rows(0, ROWS_AT_0))
            keep(2)
            in_turns(search(1))
            in_turns(front(2))
            pass_weights(2)
            carry(0)
            shift(2)
            keep(3)
            with eng.Fori(1, pairs - 2) as i:
                in_turns(front(i + 2), paced(search(i + 1), PACE), back(i - 1), rows(i))
                pass_weights(i + 2)
                carry(i)
                shift(i + 2)
                keep(i + 3)
            in_turns(search(pairs - 1), back(pairs - 3), rows(pairs - 2))
            pass_weights(pairs)
            carry(pairs - 2)
            shift(pairs)
            in_turns(back(pairs - 2), rows(pairs - 1))
            carry(pairs - 1)
            in_turns(back(pairs - 1))


SETUP_STEPS = 4
FRONT_STEPS = 25
SEARCH_STEPS = 33
BACK_STEPS = 39

_OUT = ((16, 64, 64), "float32")


def packed_columns(v):
    import numpy as np

    def diag(w, n=2):
        o = np.zeros((n * w.shape[0], n * w.shape[1]), np.float32)
        for b in range(n):
            o[b * w.shape[0]:(b + 1) * w.shape[0], b * w.shape[1]:(b + 1) * w.shape[1]] = w
        return o

    def row(w):
        return np.broadcast_to(np.reshape(w, (1, -1)), (P, np.size(w)))

    def split(w, n):
        return np.concatenate(np.split(w, n, axis=0), axis=1)

    part, cols = np.arange(P)[:, None], np.arange(P)[None, :]
    same = part // N == cols // N
    ml = np.zeros((P, 1024), np.float32)
    mr = np.zeros((P, P), np.float32)
    odd = np.arange(1024) // 16 % 2
    ml[1], ml[2] = odd == 0, odd == 1
    mr[0] = 1.0
    mr[1], mr[2] = np.where(np.arange(P) >= N, NEG, 0.0), np.where(np.arange(P) < N, NEG, 0.0)
    rel = np.stack([v["L0_attn_bias_table"][N - 1 - n:2 * N - 1 - n] for n in range(N)])
    keys = v["L0_ffn_pk_keys"]
    bd = np.concatenate([diag4([keys[m // 2, :, 4 * (m % 2) + h, :].T for h in range(4)]) for m in range(4)], axis=1)
    b = v["L0_attn_qkv_b"]
    at = np.cumsum([0] + [nb for _, na, nb in RUNS for _ in range(na)])
    return {
        "ident": np.eye(P), "ident2": np.concatenate([np.eye(C)] * 2), "m8": part // 8 == np.arange(16),
        "m16": part // 16 == np.arange(8), "same_neg": np.where(same, 0.0, NEG),
        "rel_bias": np.tile(rel, (2, 2)), "mask_l": ml, "mask_r": mr, "pos50": row(np.arange(NC)),
        "pos20": row(np.concatenate([at[a] + np.arange(nb) for first, na, nb in RUNS8 for a in range(first, first + na)])),
        "head_off": row(np.repeat(np.arange(NH) * NKV, TOPK)), "eps": np.full((P, 1), EPS),
        "wqT": diag(v["L0_tok_Wq"].T), "wk_bd": diag(v["L0_tok_Wk"]), "wvT": diag(v["L0_tok_Wv"].T),
        "woT2": np.tile(v["L0_tok_Wo"].T, (2, 1)), "bq2": np.tile(v["L0_tok_bq"], 2)[:, None],
        "bk2": np.tile(v["L0_tok_bk"], 2)[:, None], "bv2": np.tile(v["L0_tok_bv"], 2)[:, None],
        "bo_r": row(v["L0_tok_bo"]), "ln1g": row(v["L0_attn_ln1_g"]), "ln1b": row(v["L0_attn_ln1_b"]),
        "ln2g": row(v["L0_attn_ln2_g"]), "ln2b": row(v["L0_attn_ln2_b"]), "w_qkv": v["L0_attn_qkv_w"],
        "b_qk": np.stack([b[0:C], b[C:2 * C]], axis=1), "b_v": row(b[2 * C:]), "scale1": row(v["L0_attn_scale"]),
        "w_proj": v["L0_attn_proj_w"], "b_proj": row(v["L0_attn_proj_b"]), "w_pk": v["L0_ffn_Wq_pk"], "keys_bd": bd,
        "same01": same, "before01": same & (cols < part), "causal_neg": np.where(same & (cols <= part), 0.0, NEG),
        "w_q2": v["L0_ffn_Wq"], "w_o2": split(v["L0_ffn_Wo"], 4), "w_q3": v["L1_attn_Wq"], "w_kv3": v["L1_attn_Wkv"],
        "w_g3": v["L1_attn_Wg"], "w_out3": split(v["L1_attn_Wout"], 2), "b_out3": row(v["L1_attn_bout"]),
        "b_g3": row(v["L1_attn_bg"]), "gam3": row(v["L1_attn_ln_gamma"]), "bet3": row(v["L1_attn_ln_beta"]),
        "lqk": row(np.concatenate([v["L1_attn_" + n] for n in ("lq1", "lq2", "lk1", "lk2")])),
        "wr_bc": np.broadcast_to(v["L1_ffn_wr"], (C, P)), "br_c": row(v["L1_ffn_br"]), "w1": v["L1_ffn_w1"],
        "b1c": v["L1_ffn_b1"].reshape(2, P).T, "w2": split(v["L1_ffn_w2"], 2), "b2r": row(v["L1_ffn_b2"]),
    }


def diag4(blocks):
    import numpy as np

    o = np.zeros((P, 4 * NKEY), np.float32)
    for h, w in enumerate(blocks):
        o[32 * h:32 * h + 32, h * NKEY:(h + 1) * NKEY] = w
    return o


def kernel(**inputs):
    import numpy as _np
    import concourse.bacc as _bacc
    from concourse import mybir as _mybir
    from concourse.bass_utils import run_bass_kernel_spmd as _run

    v = {name: _np.asarray(value) for name, value in inputs.items()}
    at, _ = places()
    packed = _np.zeros((P, sum(n for _, n in at.values())), _np.float32)
    for name, value in packed_columns(v).items():
        lo, n = at[name]
        assert value.shape[1] == n, name
        packed[0:value.shape[0], lo:lo + n] = value
    x = v["x"].reshape(-1, 2, C, GW, GS, GW, GS)
    pairs = x.shape[0]
    arrays = {
        "packed": packed,
        "xw": _np.ascontiguousarray(x.transpose(0, 1, 2, 3, 5, 4, 6)).reshape(pairs * P, 4096),
        "xT": _np.ascontiguousarray(x.reshape(pairs, 2, C, GW, GS, 4, 2, GS).transpose(0, 6, 4, 7, 3, 5, 1, 2))
        .reshape(pairs * P, 4096),
        "table": _np.concatenate([v["L0_ffn_keys_table"], v["L0_ffn_values_table"]], axis=1),
    }
    nc = _bacc.Bacc("TRN2", target_bir_lowering=False, num_devices=1)
    aps = {name: nc.dram_tensor(f"in_{name}", w.shape, _mybir.dt.from_np(w.dtype), kind="ExternalInput").ap()
           for name, w in arrays.items()}
    out = nc.dram_tensor("out_h", _OUT[0], _mybir.dt.from_np(_np.dtype(_OUT[1])), kind="ExternalOutput").ap()
    vit_tower_kernel(nc, aps, out)
    r = _run(nc, [{f"in_{name}": w for name, w in arrays.items()}], core_ids=[0])
    return r.results[0]["out_h"]
```
